# Optimizing a Trainium2 kernel written in Bass

```python
import numpy as np
import jax
import jax.numpy as jnp

def _softmax(x, axis=-1):
    return jax.nn.softmax(x, axis=axis)

def _gelu(x):
    return jax.nn.gelu(x, approximate=True)

def _silu(x):
    return jax.nn.silu(x)

def _sigmoid(x):
    return jax.nn.sigmoid(x)

def _layernorm(x, axis=-1, eps=1e-05):
    m = jnp.mean(x, axis=axis, keepdims=True)
    v = jnp.var(x, axis=axis, keepdims=True)
    return (x - m) / jnp.sqrt(v + eps)

def _scatter_add(tgt, idx, src, axis=0):
    return tgt.at[idx].add(src)

def _segment_sum(src, seg, n):
    return jax.ops.segment_sum(src, seg, n)
kernel_name = 'mk_recurrent_d2_jaxref_r4_1934f0'

def setup_inputs(seed: int=0):
    np.random.seed(seed)
    _w = jnp.asarray

    def _L0_attn_setup():
        import jax, jax.numpy as jnp
        import numpy as np
        B, T, D_IN, D_OUT, NH = (4, 512, 256, 256, 16)
        HD = D_OUT // NH
        SCALE = 1.0 / float(np.sqrt(HD))
        key = jax.random.key(seed)
        k1, k2, k3 = jax.random.split(key, 3)
        x = jax.random.normal(k1, (B, T, D_IN), dtype=jnp.float32)
        w_qkv = jax.random.normal(k2, (3 * D_OUT, D_IN), dtype=jnp.float32) / np.sqrt(D_IN)
        w_out = jax.random.normal(k3, (D_OUT, D_OUT), dtype=jnp.float32) / np.sqrt(D_OUT)
        return {'x': x, 'w_qkv': w_qkv, 'w_out': w_out}
    _L0_attn_in = _L0_attn_setup()

    def _L0_ffn_setup():
        import jax, jax.numpy as jnp
        import numpy as np
        DIM = 256
        HIDDEN = 768
        SCALE = 1.0 / 127.0

        def _dequant(w_int, dtype):
            return w_int.astype(dtype) * jnp.asarray(SCALE, dtype)
        key = jax.random.key(seed)
        k_x, k_g, k_u, k_d = jax.random.split(key, 4)
        x = jax.random.normal(k_x, (4, 512, DIM), dtype=jnp.float32)
        w_gate = jax.random.randint(k_g, (HIDDEN, DIM), -127, 128, dtype=jnp.int32)
        w_up = jax.random.randint(k_u, (HIDDEN, DIM), -127, 128, dtype=jnp.int32)
        w_down = jax.random.randint(k_d, (DIM, HIDDEN), -127, 128, dtype=jnp.int32)
        return {'x': x, 'w_gate': w_gate, 'w_up': w_up, 'w_down': w_down}
    _L0_ffn_in = _L0_ffn_setup()

    def _L1_attn_setup():
        import jax, jax.numpy as jnp
        import numpy as np
        from jax import lax
        D_MODEL = 256
        SEQ_LEN = 2048
        ORDER = 2
        BATCH = 2

        def _hyena_fwd(x, in_proj_w, in_proj_b, short_w, short_b, fw1, fb1, fw2, fb2, fw3, fb3, out_w, out_b):
            B, L, C = x.shape
            proj = (x @ in_proj_w + in_proj_b).reshape(B, L, C, ORDER + 1)
            v = proj[..., 0]
            x_branches = [proj[..., i] for i in range(1, ORDER + 1)]
            vc = v.transpose(0, 2, 1)
            vc = lax.conv_general_dilated(vc, short_w, window_strides=(1,), padding=((1, 1),), feature_group_count=C, dimension_numbers=('NCH', 'OIH', 'NCH'))
            v = (vc + short_b[None, :, None]).transpose(0, 2, 1)
            pos = jnp.linspace(0.0, 1.0, L, dtype=x.dtype)[:, None]
            h = jax.nn.gelu(pos @ fw1 + fb1, approximate=False)
            h = jax.nn.gelu(h @ fw2 + fb2, approximate=False)
            coefs = (h @ fw3 + fb3).reshape(L, C, ORDER)
            n = 2 * L
            v_fft = jnp.fft.rfft(v, n=n, axis=1)
            output = v
            for i in range(ORDER):
                h_fft = jnp.fft.rfft(coefs[:, :, i], n=n, axis=0)
                conv = jnp.fft.irfft(v_fft * h_fft[None], n=n, axis=1)[:, :L, :]
                output = x_branches[i] * conv
            return output @ out_w + out_b
        key = jax.random.key(seed)
        ks = jax.random.split(key, 16)
        s = 0.02
        return {'x': jax.random.normal(ks[0], (BATCH, SEQ_LEN, D_MODEL), jnp.float32), 'in_proj_w': jax.random.normal(ks[1], (D_MODEL, D_MODEL * (ORDER + 1)), jnp.float32) * s, 'in_proj_b': jax.random.normal(ks[2], (D_MODEL * (ORDER + 1),), jnp.float32) * s, 'short_w': jax.random.normal(ks[3], (D_MODEL, 1, 3), jnp.float32) * 0.5, 'short_b': jax.random.normal(ks[4], (D_MODEL,), jnp.float32) * s, 'fw1': jax.random.normal(ks[5], (1, 64), jnp.float32) * 0.5, 'fb1': jax.random.normal(ks[6], (64,), jnp.float32) * s, 'fw2': jax.random.normal(ks[7], (64, 128), jnp.float32) * 0.1, 'fb2': jax.random.normal(ks[8], (128,), jnp.float32) * s, 'fw3': jax.random.normal(ks[9], (128, D_MODEL * ORDER), jnp.float32) * 0.05, 'fb3': jax.random.normal(ks[10], (D_MODEL * ORDER,), jnp.float32) * s, 'out_w': jax.random.normal(ks[11], (D_MODEL, D_MODEL), jnp.float32) * s, 'out_b': jax.random.normal(ks[12], (D_MODEL,), jnp.float32) * s}
    _L1_attn_in = _L1_attn_setup()

    def _L1_ffn_setup():
        import jax, jax.numpy as jnp
        import numpy as np
        B, S, D, DO = (4, 512, 256, 256)
        E, K = (20, 2)
        key = jax.random.key(seed)
        ks = jax.random.split(key, 6)
        sc_d = 1.0 / np.sqrt(D)
        sc_h = 1.0 / np.sqrt(D // 4)
        return {'x': jax.random.normal(ks[0], (B, S, D), jnp.float32), 'wg1': jax.random.normal(ks[1], (D, D // 4), jnp.float32) * sc_d, 'bg1': jnp.zeros((D // 4,), jnp.float32), 'wg2': jax.random.normal(ks[2], (D // 4, 2 * E), jnp.float32) * sc_h, 'bg2': jnp.zeros((2 * E,), jnp.float32), 'We': jax.random.normal(ks[3], (E, D, DO), jnp.float32) * sc_d, 'be': jnp.zeros((E, DO), jnp.float32)}
    _L1_ffn_in = _L1_ffn_setup()
    _d = {'L0_attn_x': _L0_attn_in['x'], 'L0_attn_w_qkv': _L0_attn_in['w_qkv'], 'L0_attn_w_out': _L0_attn_in['w_out'], 'L0_ffn_w_gate': _L0_ffn_in['w_gate'], 'L0_ffn_w_up': _L0_ffn_in['w_up'], 'L0_ffn_w_down': _L0_ffn_in['w_down'], 'L1_attn_in_proj_w': _L1_attn_in['in_proj_w'], 'L1_attn_in_proj_b': _L1_attn_in['in_proj_b'], 'L1_attn_short_w': _L1_attn_in['short_w'], 'L1_attn_short_b': _L1_attn_in['short_b'], 'L1_attn_fw1': _L1_attn_in['fw1'], 'L1_attn_fb1': _L1_attn_in['fb1'], 'L1_attn_fw2': _L1_attn_in['fw2'], 'L1_attn_fb2': _L1_attn_in['fb2'], 'L1_attn_fw3': _L1_attn_in['fw3'], 'L1_attn_fb3': _L1_attn_in['fb3'], 'L1_attn_out_w': _L1_attn_in['out_w'], 'L1_attn_out_b': _L1_attn_in['out_b'], 'L1_ffn_wg1': _L1_ffn_in['wg1'], 'L1_ffn_bg1': _L1_ffn_in['bg1'], 'L1_ffn_wg2': _L1_ffn_in['wg2'], 'L1_ffn_bg2': _L1_ffn_in['bg2'], 'L1_ffn_We': _L1_ffn_in['We'], 'L1_ffn_be': _L1_ffn_in['be']}
    _x0 = _d['L0_attn_x']
    _d['L0_attn_x'] = jax.random.normal(jax.random.fold_in(jax.random.key(seed), 1), (8, 512, 256), dtype=_x0.dtype)
    del _x0
    return _d

def reference(L0_attn_x, L0_attn_w_qkv, L0_attn_w_out, L0_ffn_w_gate, L0_ffn_w_up, L0_ffn_w_down, L1_attn_in_proj_w, L1_attn_in_proj_b, L1_attn_short_w, L1_attn_short_b, L1_attn_fw1, L1_attn_fb1, L1_attn_fw2, L1_attn_fb2, L1_attn_fw3, L1_attn_fb3, L1_attn_out_w, L1_attn_out_b, L1_ffn_wg1, L1_ffn_bg1, L1_ffn_wg2, L1_ffn_bg2, L1_ffn_We, L1_ffn_be):

    def _L0_attn_ref(x, w_qkv, w_out):
        import jax, jax.numpy as jnp
        import numpy as np
        B, T, D_IN, D_OUT, NH = (4, 512, 256, 256, 16)
        HD = D_OUT // NH
        SCALE = 1.0 / float(np.sqrt(HD))
        b, t, _ = x.shape
        qkv = jnp.einsum('btd,ed->bte', x, w_qkv)
        qkv = qkv.reshape(b, t, 3, NH, HD)
        q, k, v = jnp.moveaxis(qkv, 2, 0)
        scores = jnp.einsum('bqhd,bkhd->bhqk', q, k) * SCALE
        causal_bias = (1.0 - jnp.tril(jnp.ones((t, t), dtype=x.dtype))) * -10000.0
        scores = scores + causal_bias
        attn = jax.nn.softmax(scores, axis=-1)
        out = jnp.einsum('bhqk,bkhd->bqhd', attn, v)
        out = out.reshape(b, t, D_OUT)
        return jnp.einsum('btd,ed->bte', out, w_out)

    def _L0_ffn_ref(x, w_gate, w_up, w_down):
        import jax, jax.numpy as jnp
        import numpy as np
        DIM = 256
        HIDDEN = 768
        SCALE = 1.0 / 127.0

        def _dequant(w_int, dtype):
            return w_int.astype(dtype) * jnp.asarray(SCALE, dtype)
        wg = _dequant(w_gate, x.dtype)
        wu = _dequant(w_up, x.dtype)
        wd = _dequant(w_down, x.dtype)
        gate = jnp.einsum('bsd,hd->bsh', x, wg)
        up = jnp.einsum('bsd,hd->bsh', x, wu)
        h = jax.nn.silu(gate) * up
        return jnp.einsum('bsh,dh->bsd', h, wd)

    def _L1_attn_ref(x, in_proj_w, in_proj_b, short_w, short_b, fw1, fb1, fw2, fb2, fw3, fb3, out_w, out_b):
        import jax, jax.numpy as jnp
        import numpy as np
        from jax import lax
        D_MODEL = 256
        SEQ_LEN = 2048
        ORDER = 2
        BATCH = 2

        def _hyena_fwd(x, in_proj_w, in_proj_b, short_w, short_b, fw1, fb1, fw2, fb2, fw3, fb3, out_w, out_b):
            B, L, C = x.shape
            proj = (x @ in_proj_w + in_proj_b).reshape(B, L, C, ORDER + 1)
            v = proj[..., 0]
            x_branches = [proj[..., i] for i in range(1, ORDER + 1)]
            vc = v.transpose(0, 2, 1)
            vc = lax.conv_general_dilated(vc, short_w, window_strides=(1,), padding=((1, 1),), feature_group_count=C, dimension_numbers=('NCH', 'OIH', 'NCH'))
            v = (vc + short_b[None, :, None]).transpose(0, 2, 1)
            pos = jnp.linspace(0.0, 1.0, L, dtype=x.dtype)[:, None]
            h = jax.nn.gelu(pos @ fw1 + fb1, approximate=False)
            h = jax.nn.gelu(h @ fw2 + fb2, approximate=False)
            coefs = (h @ fw3 + fb3).reshape(L, C, ORDER)
            n = 2 * L
            v_fft = jnp.fft.rfft(v, n=n, axis=1)
            output = v
            for i in range(ORDER):
                h_fft = jnp.fft.rfft(coefs[:, :, i], n=n, axis=0)
                conv = jnp.fft.irfft(v_fft * h_fft[None], n=n, axis=1)[:, :L, :]
                output = x_branches[i] * conv
            return output @ out_w + out_b
        return _hyena_fwd(x, in_proj_w, in_proj_b, short_w, short_b, fw1, fb1, fw2, fb2, fw3, fb3, out_w, out_b)

    def _L1_ffn_ref(x, wg1, bg1, wg2, bg2, We, be):
        import jax, jax.numpy as jnp
        import numpy as np
        B, S, D, DO = (4, 512, 256, 256)
        E, K = (20, 2)
        Bv, Sv, Dv = x.shape
        xf = x.reshape(-1, Dv)
        h = jax.nn.gelu(xf @ wg1 + bg1, approximate=False)
        logits = (xf @ 0.0 + (h @ wg2 + bg2))[:, :E] if False else (h @ wg2 + bg2)[:, :E]
        probs = jax.nn.softmax(logits, axis=-1)
        top_vals, top_idx = jax.lax.top_k(probs, K)
        N = xf.shape[0]
        gates = jnp.zeros((N, E), xf.dtype).at[jnp.arange(N)[:, None], top_idx].set(top_vals)

        def body(y, eb):
            We_e, be_e, g_e = eb
            return (y + g_e[:, None] * (xf @ We_e + be_e), None)
        y0 = jnp.zeros((N, be.shape[-1]), xf.dtype)
        y, _ = jax.lax.scan(body, y0, (We, be, gates.T))
        return y.reshape(Bv, Sv, -1)
    x = L0_attn_x
    xn = _layernorm(x, axis=-1)
    s = _L0_attn_ref(xn, L0_attn_w_qkv, L0_attn_w_out)
    g = _silu(_L0_ffn_ref(xn, L0_ffn_w_gate, L0_ffn_w_up, L0_ffn_w_down))
    x = x + s * g
    xn = _layernorm(x, axis=-1)
    s = _L1_attn_ref(xn, L1_attn_in_proj_w, L1_attn_in_proj_b, L1_attn_short_w, L1_attn_short_b, L1_attn_fw1, L1_attn_fb1, L1_attn_fw2, L1_attn_fb2, L1_attn_fw3, L1_attn_fb3, L1_attn_out_w, L1_attn_out_b)
    g = _silu(_L1_ffn_ref(xn, L1_ffn_wg1, L1_ffn_bg1, L1_ffn_wg2, L1_ffn_bg2, L1_ffn_We, L1_ffn_be))
    x = x + s * g
    return x

_drawn_inputs = setup_inputs


def setup_inputs(seed=0):
    import zlib

    import numpy as np

    out = dict(_drawn_inputs(seed))
    spreads = {'L1_ffn_bg1': (0.0, 0.1), 'L1_ffn_bg2': (0.0, 0.1), 'L1_ffn_be': (0.0, 0.1)}
    factors = {}
    for name, (base, spread) in spreads.items():
        noise = np.random.default_rng([zlib.crc32(name.encode()), seed]).standard_normal(out[name].shape)
        drawn = base * np.exp(spread * noise) if base else spread * noise
        out[name] = jnp.asarray(drawn.astype(out[name].dtype))
    for name, factor in factors.items():
        out[name] = (out[name] * factor).astype(out[name].dtype)
    return out
```

```python
import math
import numpy as np
import concourse.bass as bass
from concourse import mybir
from contextlib import ExitStack

F32 = mybir.dt.float32
F32R = mybir.dt.float32r
F16 = mybir.dt.float16
I32 = mybir.dt.int32
U32 = mybir.dt.uint32
ALU = mybir.AluOpType
ACT = mybir.ActivationFunctionType
AX = mybir.AxisListType

P = 128
B, T, C = 8, 512, 256
NT = T // P
CC = C // P
NH, HD = 16, 16
NG, GH = 4, 4
SCALE = 1.0 / math.sqrt(HD)
FF = 768
NF = FF // P
QSCALE = 1.0 / 127.0
EPS = 1e-5
MASK = -10000.0 / SCALE
KS = 96
HG = 64
NE, TOPK = 20, 2
NBLK = B * T * TOPK // P + NE
FQ = 512
NQ = FQ // P
HI, LO = 0, 1
M0 = 64
PAIRS = ((HI, HI), (HI, LO), (LO, HI))
Q_PARTS, K_PARTS = zip(*PAIRS)


def at_least(eng, sem, value):
    if isinstance(value, int) and value <= 0:
        return
    eng.wait_ge(sem, value)


def program(nc, x, wqkvT, woutT, wguT, wdT, wg1, bg1, wg2, bg2, winT, bin_, short, wo2, bo2, fw1, fb1, fw2, fb2,
            fw3, fb3, We, be, ident_c, ramp_c, pos_c, dft_c, idft_c, out):
    x1_rows = nc.dram_tensor("x1_rows", (B, T, C), F32, kind="Internal").ap()
    xn2_rows = nc.dram_tensor("xn2_rows", (B, T, C), F32, kind="Internal").ap()
    xn2T_parts = nc.dram_tensor("xn2T_parts", (B, P, 2, CC, T), F32, kind="Internal").ap()
    qk_parts = nc.dram_tensor("qk_parts", (2, 2, P, 2, T), F32, kind="Internal").ap()
    slots_in = nc.dram_tensor("slots_in", (NBLK * P, C), F32, kind="Internal").ap()
    slots_out = nc.dram_tensor("slots_out", (NBLK * P, C), F32, kind="Internal").ap()
    ctx = ExitStack()
    with ctx:
        sem = lambda name: ctx.enter_context(nc.semaphore(name))
        cursor = [-(-nc.sbuf_base // 32) * 32]

        def size(shape, dt):
            n = 2 if dt == F16 else 4
            for s in shape[1:]:
                n *= s
            return -(-n // 32) * 32

        def keep(name, shape, dt=F32):
            off = cursor[0]
            cursor[0] += size(shape, dt)
            return nc.alloc_sbuf_tensor_at(name, shape, dt, offset=off)

        def share(*tensors):
            made, off = [], cursor[0]
            for name, shape, dt in tensors:
                made.append(nc.alloc_sbuf_tensor_at(name, shape, dt, offset=off))
                off += size(shape, dt)
            return made, off

        ident = keep("ident", [P, P])
        gates = keep("gates", [P, B * NT, TOPK])
        chosen = keep("chosen", [P, B * NT, TOPK], U32)
        first_free = cursor[0]
        ident16 = keep("ident16", [P, P], F16)
        mask16 = keep("mask16", [P, P], F16)
        Wqkv = keep("Wqkv", [P, 2, CC, 3 * C], F32R)
        Wout = keep("Wout", [P, 2, CC, C], F32R)
        Wgu = keep("Wgu", [P, CC, 2 * FF], F32R)
        Wd = keep("Wd", [P, NF, C], F32R)
        Wg1 = keep("Wg1", [P, 2, CC, P], F32R)
        Wg2 = keep("Wg2", [HG, NE])
        bg1c = keep("bg1c", [P, 1])
        bg2b = keep("bg2b", [P, NE])
        neghalf = keep("neghalf", [P, NT])
        zrow = keep("zrow", [2, T])
        xin = keep("xin", [P, NT, C])
        xres = keep("xres", [P, NT, C])
        xn = keep("xn", [P, NT, C])
        xnT = keep("xnT", [P, 2, CC, T], F32R)
        qs = keep("qs", [KS, NH, T], F32R)
        ks = keep("ks", [KS, NH, T], F32R)
        V = keep("V", [P, NT, NH, 2 * HD])
        G = keep("G", [P, NT, C])
        Mneg = keep("Mneg", [P, 2, NT, GH])
        Mhi = keep("Mhi", [P, NT, GH], F32R)
        Mparts = keep("Mparts", [P, NT, 2, GH])
        mrow = keep("mrow", [2 * GH, T])
        stats = keep("stats", [P, NT, 6])
        mv = keep("mv", [P, NT, 2])
        veps = keep("veps", [P, NT])
        rstd = keep("rstd", [P, NT])
        stats2 = keep("stats2", [P, NT, 6])
        mv2 = keep("mv2", [P, NT, 2])
        veps2 = keep("veps2", [P, NT])
        rstd2 = keep("rstd2", [P, NT])
        idle_p = keep("idle_p", [P, NH])
        idle_v = keep("idle_v", [P, 1])
        rinv = keep("rinv", [P, NT, NH])
        lg = keep("lg", [P, NT, NE])
        lge = keep("lge", [P, NT, NE])
        small = keep("small", [P, 4, NT])
        top8 = keep("top8", [P, NT, 8])
        idx8 = keep("idx8", [P, NT, 8], U32)
        (qhl, khl), e1 = share(("qhl", [P, 2, 2, T], F32R), ("khl", [P, 2, 2, T], F32R))
        (OT, On), e2 = share(("OT", [P, NG, T], F32), ("On", [P, NT, C], F32))
        cursor[0] = max(e1, e2)
        (xn2T,), _ = share(("xn2T", [P, 2, CC, T], F32R))
        (OnT,), e1 = share(("OnT", [P, 2, CC, T], F32R))
        cursor[0] = e1
        xn2 = xn
        hgT = keep("hgT", [P, T])
        (PT,), e1 = share(("PT", [P, 2, GH, 1280], F32))
        (h, sil, h32), e2 = share(("h", [P, 2, NF, T], F32R), ("sil", [P, 2, T], F32), ("h32", [P, 2, T], F32))
        (st_qkv, st_out, st_gu, st_d, st_g1), e3 = share(
            ("st_qkv", [P, CC, 3 * C], F32), ("st_out", [P, CC, C], F32), ("st_gu", [P, CC, 2 * FF], I32),
            ("st_d", [P, NF, C], I32), ("st_g1", [P, CC, P], F32))
        cursor[0] = max(e1, e2, e3)
        print("sbuf", cursor[0], nc.sbuf_usable_end)
        PS = ctx.enter_context(nc.psum_tensor("PS", [P, 8, T], F32))

        def f(ap):
            return ap.bitcast(F32)

        w_in = sem("w_in"); w_ms = sem("w_ms"); w_zero = sem("w_zero"); w_hi = sem("w_hi"); w_done = sem("w_done")
        with nc.Block() as block:
            @block.sync
            def _(sp):
                sp.dma_start(st_qkv[:, :, :], wqkvT.rearrange("(c p) n -> p c n", p=P)).then_inc(w_in, 16)
                sp.dma_start(st_out[:, :, :], woutT.rearrange("(c p) n -> p c n", p=P)).then_inc(w_in, 16)
                sp.dma_start(st_g1[:, :, :], wg1.rearrange("(c p) n -> p c n", p=P)).then_inc(w_in, 16)
                sp.dma_start(ident[:, :], ident_c).then_inc(w_in, 16)
                sp.dma_start(st_gu[:, :, :], wguT.rearrange("(c p) n -> p c n", p=P)).then_inc(w_in, 16)
                sp.dma_start(st_d[:, :, :], wdT.rearrange("(c p) n -> p c n", p=P)).then_inc(w_in, 16)
                sp.dma_start(Wg2[:, :], wg2).then_inc(w_in, 16)
                sp.dma_start(bg1c[:, :], bg1).then_inc(w_in, 16)
                sp.dma_start(bg2b[:, :], bg2.partition_broadcast(P)).then_inc(w_in, 16)
                sp.wait_ge(w_in, 16 * 9)

            @block.gpsimd
            def _(pool):
                pool.memset(mask16[:, :], 0.0).then_inc(w_ms, 1)
                pool.memset(neghalf[:, :], -0.5)
                pool.memset(V[:, :, :, :], 1.0)
                pool.wait_ge(w_ms, 1)
                pool.affine_select(out=mask16[:, :], in_=mask16[:, :], compare_op=ALU.is_ge, fill=MASK, base=0,
                                   pattern=[[-1, P]], channel_multiplier=1).then_inc(w_ms, 1)

            @block.scalar
            def _(act):
                act.wait_ge(w_in, 16 * 9)
                for hi, src in ((Wqkv, st_qkv), (Wout, st_out), (Wg1, st_g1)):
                    act.activation(hi[:, HI, :, :], src[:, :, :], ACT.Copy).then_inc(w_hi, 1)
                act.activation(Wd[:, :, :], st_d[:, :, :], ACT.Copy)
                act.activation(ident16[:, :], ident[:, :], ACT.Copy).then_inc(w_done, 1)

            @block.vector
            def _(dve):
                dve.memset(zrow[:, :], 0.0)
                for stacked in (qs, ks):
                    dve.memset(f(stacked[32:64, :, :]), 0.0)
                    last = dve.memset(f(stacked[64:KS, :, :]), 0.0)
                last.then_inc(w_zero, 1)
                dve.wait_ge(w_zero, 1)
                dve.memset(f(ks[M0:M0 + 2, :, :]), 1.0)
                dve.wait_ge(w_in, 16 * 9)
                for n, (w, src) in enumerate(((Wqkv, st_qkv), (Wout, st_out), (Wg1, st_g1))):
                    dve.wait_ge(w_hi, n + 1)
                    dve.tensor_tensor(w[:, LO, :, :], src[:, :, :], f(w[:, HI, :, :]), ALU.subtract)
                dve.tensor_copy(Wgu[:, :, :], st_gu[:, :, :]).then_inc(w_done, 1)

        names = """x_in ln_var ln_std ln_done tx xnT_hi xnT_lo qk_ps qk_hi qk_lo v_ps v_sb
            gu_ps silu_sb h32_sb h_hi h_lo down_ps g_sb ln2_var ln2_std ln2_done t2 xn2T_hi xn2T_lo hg_ps hg_sb
            lg_ps lg_in lge_sb route_sb x1_out xn2_out xn2T_out xres_in unit maxed m_parts mt mrow_sb m_in st_ps
            exped masked pv ot_sb otr rinv_sb on_sb ont ont_hi ont_lo op y_sb x1_sb step"""
        S = {n: sem("s_" + n) for n in names.split()}
        UNITS = ((3, (0, 1), 512), (3, (2, 3), 512), (2, (0, 1), 384), (2, (2, 3), 384),
                 (1, (0, 1, 2, 3), 256), (0, (0, 1, 2, 3), 128))
        NU = len(UNITS)
        BANK = (4, 6, 2)
        PIECES = (((0, 0, 0),), ((1, 0, 512), (3, 384, 896)), ((2, 0, 1024),))
        WIDTH = (512, 512, 256)
        COL = {0: 0, 1: 512, 2: 1024, 3: 896}

        def scores_of_unit(slot, u):
            qt, heads, keys = UNITS[u]
            if keys > 256:
                return [PS[:, slot + n, 0:keys] for n in range(2)], PS[:, slot:slot + 2, 0:keys]
            if keys == 256:
                both = PS[:, slot:slot + 2, :].rearrange("p a (b k) -> p (a b) k", b=2)
                return [PS[:, slot + n // 2, 256 * (n % 2):256 * (n % 2) + 256] for n in range(4)], both
            return ([PS[:, slot, 128 * n:128 * n + 128] for n in range(4)],
                    PS[:, slot, :].rearrange("p (a k) -> p a k", a=4))

        S["mhi"] = sem("s_mhi")
        S["stack_in"] = [sem(f"s_stack_in{g}") for g in range(NG)]
        S["spilt"] = [sem(f"s_spilt{m}") for m in range(2)]
        STACKED = 16 * 7

        def up_to(b):
            return min(b, B) if isinstance(b, int) else b

        with nc.Block() as block:
            @block.sync
            def _(sp):
                def load_x(b):
                    at_least(sp, S["ln_done"], b)
                    sp.dma_start(xin[:, :, :], x[b].rearrange("(t p) d -> p t d", p=P)).then_inc(S["x_in"], 16)

                def spill(b):
                    for g in range(NG):
                        at_least(sp, S["stack_in"][g], STACKED * b)
                    for m, (src, n) in enumerate(((qhl, 0), (khl, 1), (qhl, 0), (khl, 1))):
                        sp.wait_ge(S["qk_lo"], 4 * b + m + 1)
                        sp.dma_start(qk_parts[n, m // 2], f(src[:, m // 2, :, :])).then_inc(S["spilt"][m // 2], 16)

                def stack(b, g):
                    at_least(sp, S["st_ps"], 48 * (b - 1) + 12 * (g + 1))
                    if g % 2 == 0:
                        sp.wait_ge(S["spilt"][g // 2], 32 * (b + 1))
                    sp.dma_start(f(qs[M0:M0 + 2, GH * g:GH * g + GH, :]),
                                 zrow[:, :].unsqueeze(1).to_broadcast([2, GH, T])).then_inc(S["stack_in"][g], 16)
                    for n, (dst, parts) in enumerate(((qs, Q_PARTS), (ks, K_PARTS))):
                        for blk, part in enumerate(parts):
                            sp.dma_start(
                                f(dst[HD * blk:HD * blk + HD, GH * g:GH * g + GH, :]),
                                qk_parts[n, g // 2, 64 * (g % 2):64 * (g % 2) + 64, part, :].rearrange(
                                    "(h d) t -> d h t", d=HD)).then_inc(S["stack_in"][g], 16)

                def store(b):
                    sp.wait_ge(S["x1_sb"], b + 1)
                    sp.dma_start(x1_rows[b].rearrange("(t p) d -> p t d", p=P), xres[:, :, :]
                                 ).then_inc(S["x1_out"], 16)
                    sp.wait_ge(S["ln2_done"], NT * (b + 1))
                    sp.dma_start(xn2_rows[b].rearrange("(t p) d -> p t d", p=P), xn2[:, :, :]
                                 ).then_inc(S["xn2_out"], 16)
                    sp.wait_ge(S["x1_out"], 16 * (b + 1))

                def store_T(b):
                    sp.wait_ge(S["xn2T_lo"], b + 1)
                    sp.dma_start(xn2T_parts[b], f(xn2T[:, :, :, :])).then_inc(S["xn2T_out"], 16)

                def load_res(b):
                    sp.dma_start(xres[:, :, :], x[b].rearrange("(t p) d -> p t d", p=P)).then_inc(S["xres_in"], 16)

                def rows_of_maxima(b, g):
                    sp.wait_ge(S["mrow_sb"], NG * b + g + 1)
                    for r in range(2):
                        sp.dma_start(f(qs[M0 + r:M0 + r + 1, GH * g:GH * g + GH, :]),
                                     mrow[GH * r:GH * r + GH, :]).then_inc(S["m_in"], 16)

                def sequence(b, first=False, last=False):
                    if not last:
                        load_x(b + 1)
                    if not first:
                        store(b - 1)
                    load_res(b)
                    if not first:
                        store_T(b - 1)
                    if not last:
                        spill(b + 1)
                    for g in range(NG + 1):
                        if g < NG:
                            rows_of_maxima(b, g)
                        if g > 0 and not last:
                            stack(b + 1, g - 1)

                load_x(0)
                spill(0)
                for g in range(NG):
                    stack(0, g)
                sequence(0, first=True)
                with sp.Fori(1, B - 1) as b:
                    sequence(b)
                sequence(B - 1, last=True)
                store(B - 1)
                store_T(B - 1)
                for n in ("x1_out", "xn2_out", "xn2T_out"):
                    sp.wait_ge(S[n], 16 * B)

            @block.tensor
            def _(pe):
                def split_products(out, lhs, rhs, chunks=CC, pairs=PAIRS):
                    n, last = len(pairs) * chunks, None
                    for c in range(chunks):
                        for i, j in pairs:
                            n -= 1
                            last = pe.matmul(out, lhs(i, c), rhs(j, c), start=last is None, stop=n == 0)
                    return last

                def transposed_x(b):
                    pe.wait_ge(S["ln_done"], NT * (b + 1))
                    at_least(pe, S["h32_sb"], NF * b)
                    for c in range(CC):
                        for t in range(NT):
                            last = pe.transpose(PS[:, 4 + c, P * t:P * t + P], xn[:, t, P * c:P * c + P], ident[:, :])
                    last.then_inc(S["tx"], 1)

                def project_qk(b):
                    for m in range(4):
                        if m == 0:
                            pe.wait_ge(S["xnT_hi"], b + 1)
                            pe.wait_ge(S["xnT_lo"], b + 1)
                            at_least(pe, S["g_sb"], 2 * b)
                        if m >= 2:
                            pe.wait_ge(S["qk_lo"], 4 * b + m - 1)
                        o = C * (m % 2) + P * (m // 2)
                        split_products(PS[:, m % 2, :],
                                       lambda i, c: Wqkv[:, i, c, o:o + P],
                                       lambda j, c: xnT[:, j, c, :]).then_inc(S["qk_ps"], 1)

                def project_v(b):
                    at_least(pe, S["on_sb"], NT * b)
                    for t in range(NT):
                        last = split_products(PS[:, 2 + t // 2, C * (t % 2):C * (t % 2) + C],
                                              lambda i, c: xnT[:, i, c, P * t:P * t + P],
                                              lambda j, c: Wqkv[:, j, c, 2 * C:3 * C])
                        if t % 2:
                            last.then_inc(S["v_ps"], 1)

                def gate_up(b, first):
                    for i in range(NF):
                        bank = BANK[i % 3]
                        if i == 1:
                            at_least(pe, S["y_sb"], 2 * b)
                        if i == 2:
                            pe.wait_ge(S["v_sb"], 2 * (b + 1))
                            if not first:
                                route_transposes(b - 1)
                        if i >= 3:
                            pe.wait_ge(S["h32_sb"], NF * b + i - 2)
                        for half in range(2):
                            o = FF * half + P * i
                            last = split_products(PS[:, bank + half, :],
                                                  lambda i_, c: Wgu[:, c, o:o + P],
                                                  lambda j, c: xnT[:, j, c, :], pairs=((HI, HI), (HI, LO)))
                            last.then_inc(S["gu_ps"], 1)

                def down(b):
                    for t in range(NT):
                        if t == 0:
                            at_least(pe, S["xn2T_lo"], b)
                            if isinstance(b, int) and b == 0:
                                pe.wait_ge(S["qk_lo"], 4)
                        for i in range(NF):
                            if t == 0:
                                pe.wait_ge(S["h_hi"], NF * b + i + 1)
                                pe.wait_ge(S["h_lo"], NF * b + i + 1)
                            for part in (HI, LO):
                                last = pe.matmul(PS[:, t // 2, C * (t % 2):C * (t % 2) + C],
                                                 h[:, part, i, P * t:P * t + P], Wd[:, i, :],
                                                 start=(i == 0 and part == HI), stop=(i == NF - 1 and part == LO))
                        if t % 2:
                            last.then_inc(S["down_ps"], 1)

                def route_transposes(b):
                    pe.wait_ge(S["ln2_done"], NT * (b + 1))
                    pe.wait_ge(S["on_sb"], NT * (b + 1))
                    for c in range(CC):
                        for t in range(NT):
                            last = pe.transpose(PS[:, c, P * t:P * t + P], xn2[:, t, P * c:P * c + P],
                                                ident[:, :])
                    last.then_inc(S["t2"], 1)

                def route_hidden(b, mlps):
                    pe.wait_ge(S["xn2T_lo"], b + 1)
                    pe.wait_ge(S["h32_sb"], NF * mlps)
                    split_products(PS[:, 6, :], lambda i, c: Wg1[:, i, c, :],
                                   lambda j, c: xn2T[:, j, c, :]).then_inc(S["hg_ps"], 1)

                def route_logits(b):
                    pe.wait_ge(S["hg_sb"], b + 1)
                    for t in range(NT):
                        last = pe.matmul(PS[:, 7, 32 * t:32 * t + NE], hgT[0:HG, P * t:P * t + P], Wg2[:, :],
                                         start=True, stop=True)
                    last.then_inc(S["lg_ps"], 1)

                def unit(b, g, u):
                    slot = 2 * (((NU + 1) * g + u) % 2)
                    if u == 0:
                        pe.wait_ge(S["stack_in"][g], STACKED * (b + 1))
                    if u == 0 and g == 0:
                        pe.wait_ge(S["qk_lo"], 4 * up_to(b + 2))
                        pe.wait_ge(S["g_sb"], 2 * (b + 1))
                    elif u == 1 or (u == 0 and g > 0):
                        if g > 0:
                            if u == 1:
                                pe.wait_ge(S["mrow_sb"], NG * b + g)
                            else:
                                pe.wait_ge(S["maxed"], NU * (NG * b + g))
                    else:
                        pe.wait_ge(S["maxed"], NU * (NG * b + g) + u - 1)
                    qt, heads, keys = UNITS[u]
                    places, _ = scores_of_unit(slot, u)
                    for j, out in zip(heads, places):
                        hd = GH * g + j
                        pe.matmul(out, qs[:, hd, P * qt:P * qt + P], ks[:, hd, 0:keys], start=True, stop=False)
                        last = pe.matmul(out[:, keys - P:keys], ident16[:, :], mask16[:, :], start=False, stop=True)
                    last.then_inc(S["unit"], 1)

                def maxima_as_rows(b, g):
                    slot = 2 * (((NU + 1) * g + NU) % 2)
                    pe.wait_ge(S["m_parts"], NG * b + g + 1)
                    for qt in range(NT):
                        last = pe.matmul(PS[0:2 * GH, slot, P * qt:P * qt + P],
                                         Mparts[:, qt, :, :].rearrange("p r j -> p (r j)"), ident[:, :],
                                         start=True, stop=True)
                    last.then_inc(S["mt"], 1)

                def transposed_scores(b, g, j):
                    hd = GH * g + j
                    if hd == 0:
                        pe.wait_ge(S["xnT_lo"], up_to(b + 2))
                        pe.wait_ge(S["h32_sb"], NF * (b + 1))
                        at_least(pe, S["hg_sb"], b)
                    if j == 0:
                        pe.wait_ge(S["m_in"], 32 * (NG * b + g + 1))
                    for n, piece in enumerate(PIECES):
                        if hd > 0:
                            pe.wait_ge(S["exped"], 48 * b + 3 * (hd - 1) + n + 1)
                        for kt, col, _ in piece:
                            last = pe.matmul(PS[:, 4 + n, col:col + T - P * kt], ks[:, hd, P * kt:P * kt + P],
                                             qs[:, hd, P * kt:T], start=True, stop=True)
                        last.then_inc(S["st_ps"], 1)

                def values(b, g):
                    at_least(pe, S["ot_sb"], NG * b + g)
                    if g == 0:
                        at_least(pe, S["route_sb"], b)
                    pe.wait_ge(S["exped"], 48 * b + 12 * (g + 1))
                    pe.wait_ge(S["masked"], 16 * b + 4 * (g + 1))
                    for kt in range(NT):
                        for j in range(GH):
                            last = pe.matmul(PS[32 * j:32 * j + 32, 7, P * kt:T], V[:, kt, GH * g + j, :],
                                             PT[:, g % 2, j, COL[kt]:COL[kt] + T - P * kt],
                                             start=kt == 0, stop=kt == NT - 1)
                    last.then_inc(S["pv"], 1)

                def attention(b):
                    for s in range(NG + 2):
                        for u in range(NU + 1):
                            if s < NG and u < NU:
                                unit(b, s, u)
                            if u == 1 and 2 <= s:
                                values(b, s - 2)
                            if 1 <= s <= NG and u in (1, 2, 4, 5):
                                transposed_scores(b, s - 1, (1, 2, 4, 5).index(u))
                        if s < NG:
                            maxima_as_rows(b, s)

                def heads_as_rows(b):
                    for qt in range(NT):
                        if qt == 0:
                            pe.wait_ge(S["ot_sb"], NG * (b + 1))
                            pe.wait_ge(S["mrow_sb"], NG * (b + 1))
                        for g in range(NG):
                            last = pe.transpose(PS[:, qt, P * g:P * g + P], OT[:, g, P * qt:P * qt + P], ident[:, :])
                        last.then_inc(S["otr"], 1)

                def output_transposes(b):
                    pe.wait_ge(S["on_sb"], NT * (b + 1))
                    for c in range(CC):
                        for t in range(NT):
                            last = pe.transpose(PS[:, 4 + c, P * t:P * t + P], On[:, t, P * c:P * c + P], ident[:, :])
                    last.then_inc(S["ont"], 1)

                def project_out(b):
                    pe.wait_ge(S["ont_hi"], b + 1)
                    pe.wait_ge(S["ont_lo"], b + 1)
                    for t in range(NT):
                        last = split_products(PS[:, 6 + t // 2, C * (t % 2):C * (t % 2) + C],
                                              lambda i, c: OnT[:, i, c, P * t:P * t + P],
                                              lambda j, c: Wout[:, j, c, :])
                        if t % 2:
                            last.then_inc(S["op"], 1)

                def sequence(b, first=False, last=False):
                    project_v(b)
                    gate_up(b, first)
                    down(b)
                    if not last:
                        transposed_x(b + 1)
                    if not first:
                        route_hidden(b - 1, b + 1)
                    if not last:
                        project_qk(b + 1)
                    if not first:
                        route_logits(b - 1)
                    attention(b)
                    heads_as_rows(b)
                    output_transposes(b)
                    project_out(b)

                transposed_x(0)
                project_qk(0)
                sequence(0, first=True)
                with pe.Fori(1, B - 1) as b:
                    sequence(b)
                sequence(B - 1, last=True)
                route_transposes(B - 1)
                route_hidden(B - 1, B)
                route_logits(B - 1)

            @block.scalar
            def _(act):
                def split_x(b):
                    act.wait_ge(S["tx"], b + 1)
                    at_least(act, S["gu_ps"], 2 * NF * b)
                    act.activation(xnT[:, HI, :, :], PS[:, 4:6, :], ACT.Copy).then_inc(S["xnT_hi"], 1)

                def split_qk(b):
                    for m in range(4):
                        if m == 0:
                            at_least(act, S["on_sb"], NT * (b - 1))
                            at_least(act, S["ont"], b - 1)
                        act.wait_ge(S["qk_ps"], 4 * b + m + 1)
                        dst = khl if m % 2 else qhl
                        act.activation(dst[:, m // 2, HI, :], PS[:, m % 2, :], ACT.Copy).then_inc(S["qk_hi"], 1)

                def keep_v(b):
                    for n in range(2):
                        act.wait_ge(S["v_ps"], 2 * b + n + 1)
                        if n == 0:
                            at_least(act, S["pv"], NG * b)
                        act.activation(V[:, 2 * n:2 * n + 2, :, 0:HD].rearrange("p t h d -> p (t h) d"),
                                       PS[:, 2 + n, :].rearrange("p (x d) -> p x d", d=HD), ACT.Copy
                                       ).then_inc(S["v_sb"], 1)

                def gated(b, first):
                    for i in range(NF):
                        if i == 2 and not first:
                            split_x1(b - 1)
                        bank = BANK[i % 3]
                        act.wait_ge(S["gu_ps"], 2 * NF * b + 2 * i + 1)
                        if i == 0:
                            at_least(act, S["pv"], NG * b)
                        if i >= 2:
                            act.wait_ge(S["h32_sb"], NF * b + i - 1)
                        act.activation(sil[:, i % 2, :], PS[:, bank, :], ACT.Silu, scale=QSCALE
                                       ).then_inc(S["silu_sb"], 1)
                        act.wait_ge(S["h32_sb"], NF * b + i + 1)
                        if i == 0:
                            at_least(act, S["down_ps"], 2 * b)
                        act.activation(h[:, HI, i, :], h32[:, i % 2, :], ACT.Copy).then_inc(S["h_hi"], 1)

                def gate_of_output(b):
                    for n in range(2):
                        act.wait_ge(S["down_ps"], 2 * b + n + 1)
                        if n == 0:
                            at_least(act, S["y_sb"], 2 * b)
                        act.activation(G[:, 2 * n:2 * n + 2, :].rearrange("p t e -> p (t e)"), PS[:, n, :],
                                       ACT.Silu, scale=QSCALE).then_inc(S["g_sb"], 1)

                def split_x1(b):
                    act.wait_ge(S["t2"], b + 1)
                    act.wait_ge(S["op"], 2 * (b + 1))
                    act.activation(xn2T[:, HI, :, :], PS[:, 0:2, :], ACT.Copy).then_inc(S["xn2T_hi"], 1)

                def route_hidden(b):
                    act.wait_ge(S["hg_ps"], b + 1)
                    act.activation(hgT[:, :], PS[:, 6, :], ACT.Gelu, bias=bg1c[:, 0:1]).then_inc(S["hg_sb"], 1)

                def route_exps(b):
                    act.wait_ge(S["lg_in"], b + 1)
                    act.activation(lge[:, :, :], lg[:, :, :], ACT.Exp).then_inc(S["lge_sb"], 1)

                def exps(b, g, j):
                    if j == 0 and g >= 2:
                        act.wait_ge(S["pv"], NG * b + g - 1)
                    if g == 0 and j == 0:
                        at_least(act, S["pv"], NG * b)
                        act.wait_ge(S["down_ps"], 2 * (b + 1))
                    hd = GH * g + j
                    for n, width in enumerate(WIDTH):
                        act.wait_ge(S["st_ps"], 48 * b + 3 * hd + n + 1)
                        act.activation(PT[:, g % 2, j, 512 * n:512 * n + width], PS[:, 4 + n, 0:width], ACT.Exp,
                                       scale=SCALE).then_inc(S["exped"], 1)

                def keep_heads(b, g):
                    act.wait_ge(S["pv"], NG * b + g + 1)
                    if g == 0:
                        for half in S["spilt"]:
                            act.wait_ge(half, 32 * up_to(b + 2))
                    act.activation(OT[:, g, :], PS[:, 7, :], ACT.Copy).then_inc(S["ot_sb"], 1)

                def attention(b, first):
                    for s in range(1, NG + 2):
                        for j in range(GH):
                            if s <= NG:
                                exps(b, s - 1, j)
                            if s == 1 and j == 0 and not first:
                                route_exps(b - 1)
                            if j == 1 and s >= 2:
                                keep_heads(b, s - 2)

                def split_output(b):
                    act.wait_ge(S["ont"], b + 1)
                    at_least(act, S["xn2T_out"], 16 * b)
                    at_least(act, S["hg_ps"], b)
                    act.activation(OnT[:, HI, :, :], PS[:, 4:6, :], ACT.Copy).then_inc(S["ont_hi"], 1)

                def sequence(b, first=False, last=False):
                    keep_v(b)
                    gated(b, first)
                    gate_of_output(b)
                    if not last:
                        split_x(b + 1)
                    if not first:
                        route_hidden(b - 1)
                    if not last:
                        split_qk(b + 1)
                    attention(b, first)
                    split_output(b)

                split_x(0)
                split_qk(0)
                sequence(0, first=True)
                with act.Fori(1, B - 1) as b:
                    sequence(b)
                sequence(B - 1, last=True)
                split_x1(B - 1)
                route_hidden(B - 1)
                route_exps(B - 1)

            @block.vector
            def _(dve):
                steps = {"made": 0}

                def norm(b, src, st, m_, ve, rs, dst, var_sem, std_sem, done_sem):
                    for t in range(NT):
                        last = dve.bn_stats(st[:, t, :], src[:, t, :])
                    last.then_inc(S[var_sem], 1)
                    dve.wait_ge(S[var_sem], 3 * b + 1)
                    dve.memset(idle_v[:, :], 0.0)
                    for t in range(NT):
                        last = dve.bn_aggr(m_[:, t, :], st[:, t, :])
                    last.then_inc(S[var_sem], 1)
                    dve.wait_ge(S[var_sem], 3 * b + 2)
                    dve.tensor_scalar(ve[:, :], m_[:, :, 1], EPS, None, ALU.add).then_inc(S[var_sem], 1)
                    dve.wait_ge(S[std_sem], b + 1)
                    for t in range(NT):
                        dve.tensor_scalar(dst[:, t, :], src[:, t, :], m_[:, t, 0:1], rs[:, t:t + 1],
                                          ALU.subtract, ALU.mult).then_inc(S[done_sem], 1)

                def norm_x(b):
                    dve.wait_ge(S["x_in"], 16 * (b + 1))
                    at_least(dve, S["tx"], b)
                    at_least(dve, S["t2"], b - 1)
                    at_least(dve, S["xn2_out"], 16 * (b - 1))
                    norm(b, xin, stats, mv, veps, rstd, xn, "ln_var", "ln_std", "ln_done")

                def norm_x1(b):
                    dve.wait_ge(S["x1_sb"], b + 1)
                    dve.wait_ge(S["tx"], up_to(b + 2))
                    norm(b, xres, stats2, mv2, veps2, rstd2, xn2, "ln2_var", "ln2_std", "ln2_done")

                def split_x(b):
                    dve.wait_ge(S["xnT_hi"], b + 1)
                    dve.tensor_tensor(xnT[:, LO, :, :], PS[:, 4:6, :], f(xnT[:, HI, :, :]), ALU.subtract
                                      ).then_inc(S["xnT_lo"], 1)

                def split_qk(b):
                    for m in range(4):
                        dve.wait_ge(S["qk_hi"], 4 * b + m + 1)
                        dst = khl if m % 2 else qhl
                        dve.tensor_tensor(dst[:, m // 2, LO, :], PS[:, m % 2, :], f(dst[:, m // 2, HI, :]),
                                          ALU.subtract).then_inc(S["qk_lo"], 1)

                def gated(b, first, last):
                    for i in range(NF):
                        if i == 3 and not first:
                            split_x1(b - 1)
                        if i == 4 and not last:
                            norm_x(b + 1)
                        bank = BANK[i % 3] + 1
                        dve.wait_ge(S["gu_ps"], 2 * NF * b + 2 * i + 2)
                        dve.wait_ge(S["silu_sb"], NF * b + i + 1)
                        if i >= 2:
                            dve.wait_ge(S["h_hi"], NF * b + i - 1)
                            dve.wait_ge(S["h_lo"], NF * b + i - 1)
                        dve.scalar_tensor_tensor(out=h32[:, i % 2, :], in0=PS[:, bank, :], scalar=QSCALE,
                                                 in1=sil[:, i % 2, :], op0=ALU.mult, op1=ALU.mult
                                                 ).then_inc(S["h32_sb"], 1)

                def route(b):
                    N = 9
                    made = 0

                    def step(ins, wait=True):
                        nonlocal made
                        made += 1
                        ins.then_inc(S["step"], 1)
                        if wait:
                            dve.wait_ge(S["step"], N * b + made)

                    dve.wait_ge(S["lg_ps"], b + 1)
                    logits = PS[:, 7, 0:P].rearrange("p (t e) -> p t e", t=NT)[:, :, 0:NE]
                    step(dve.tensor_tensor(lg[:, :, :], logits, bg2b[:, :].unsqueeze(1).to_broadcast([P, NT, NE]),
                                           ALU.add))
                    step(dve.tensor_reduce(out=small[:, 0, :], in_=lg[:, :, :], op=ALU.max, axis=AX.X))
                    dve.tensor_tensor(lg[:, :, :], lg[:, :, :],
                                      small[:, 0, :].unsqueeze(2).to_broadcast([P, NT, NE]),
                                      ALU.subtract).then_inc(S["lg_in"], 1)
                    dve.wait_ge(S["lge_sb"], b + 1)
                    step(dve.tensor_reduce(out=small[:, 1, :], in_=lge[:, :, :], op=ALU.add, axis=AX.X))
                    step(dve.reciprocal(small[:, 2, :], small[:, 1, :]))
                    step(dve.tensor_tensor(lg[:, :, :], lge[:, :, :],
                                           small[:, 2, :].unsqueeze(2).to_broadcast([P, NT, NE]), ALU.mult))
                    dve.memset(idle_v[:, :], 0.0)
                    for t in range(NT):
                        last = dve.max(out=top8[:, t, :], in_=lg[:, t, :])
                    step(last)
                    dve.memset(idle_v[:, :], 0.0)
                    for t in range(NT):
                        last = dve.max_index(out=idx8[:, t, :], in_max=top8[:, t, :], in_values=lg[:, t, :])
                    step(last)
                    step(dve.tensor_copy(gates[:, bass.ds(NT * b, NT), :], top8[:, :, 0:TOPK]), wait=False)
                    step(dve.tensor_copy(chosen[:, bass.ds(NT * b, NT), :], idx8[:, :, 0:TOPK]))
                    dve.tensor_copy(small[:, 3, :], small[:, 2, :]).then_inc(S["route_sb"], 1)
                    assert made == N

                def maxima(b, g, u):
                    slot = 2 * (((NU + 1) * g + u) % 2)
                    qt, heads, keys = UNITS[u]
                    dve.wait_ge(S["unit"], NU * (NG * b + g) + u + 1)
                    if u == 0 and not (isinstance(b, int) and b == 0 and g == 0):
                        dve.wait_ge(S["m_parts"], NG * b + g)
                    _, all_of = scores_of_unit(slot, u)
                    dve.tensor_reduce(out=Mneg[:, 0, qt, heads[0]:heads[-1] + 1], in_=all_of, op=ALU.max, axis=AX.X,
                                      negate=True).then_inc(S["maxed"], 1)

                def parts_of_maxima(b, g):
                    dve.wait_ge(S["maxed"], NU * (NG * b + g + 1))
                    at_least(dve, S["mt"], NG * b + g)
                    dve.tensor_copy(Mhi[:, :, :], Mneg[:, 0, :, :]).then_inc(S["mhi"], 1)
                    dve.wait_ge(S["mhi"], NG * b + g + 1)
                    dve.tensor_copy(Mparts[:, :, HI, :], f(Mhi[:, :, :]))
                    dve.tensor_tensor(Mparts[:, :, LO, :], Mneg[:, 0, :, :], f(Mhi[:, :, :]), ALU.subtract
                                      ).then_inc(S["m_parts"], 1)

                def rows_of_maxima(b, g):
                    slot = 2 * (((NU + 1) * g + NU) % 2)
                    dve.wait_ge(S["mt"], NG * b + g + 1)
                    at_least(dve, S["m_in"], 32 * (NG * b + g))
                    dve.tensor_copy(mrow[:, :], PS[0:2 * GH, slot, :]).then_inc(S["mrow_sb"], 1)

                def attention(b, first):
                    for g in range(NG):
                        for u in range(NU):
                            maxima(b, g, u)
                        parts_of_maxima(b, g)
                        rows_of_maxima(b, g)
                        if g == 0 and not first:
                            route(b - 1)

                def normed_heads(b):
                    for qt in range(NT):
                        dve.wait_ge(S["otr"], NT * b + qt + 1)
                        if qt == 0:
                            for half in S["spilt"]:
                                dve.wait_ge(half, 32 * up_to(b + 2))
                        heads = PS[:, qt, :].rearrange("p (h x) -> p h x", x=2 * HD)
                        dve.reciprocal(rinv[:, qt, :], heads[:, :, HD]).then_inc(S["rinv_sb"], 1)
                        dve.wait_ge(S["rinv_sb"], NT * b + qt + 1)
                        dve.tensor_tensor(On[:, qt, :].rearrange("p (h d) -> p h d", d=HD), heads[:, :, 0:HD],
                                          rinv[:, qt, :].unsqueeze(2).to_broadcast([P, NH, HD]), ALU.mult
                                          ).then_inc(S["on_sb"], 1)

                def split_output(b):
                    dve.wait_ge(S["ont_hi"], b + 1)
                    dve.tensor_tensor(OnT[:, LO, :, :], PS[:, 4:6, :], f(OnT[:, HI, :, :]), ALU.subtract
                                      ).then_inc(S["ont_lo"], 1)

                def residual(b):
                    for n in range(2):
                        dve.wait_ge(S["op"], 2 * b + n + 1)
                        dve.wait_ge(S["g_sb"], 2 * b + n + 1)
                        part = G[:, 2 * n:2 * n + 2, :].rearrange("p t e -> p (t e)")
                        dve.tensor_tensor(part, PS[:, 6 + n, :], part, ALU.mult).then_inc(S["y_sb"], 1)
                    dve.wait_ge(S["y_sb"], 2 * (b + 1))
                    dve.wait_ge(S["xres_in"], 16 * (b + 1))
                    dve.tensor_tensor(xres[:, :, :], xres[:, :, :], G[:, :, :], ALU.add).then_inc(S["x1_sb"], 1)

                def sequence(b, first=False, last=False):
                    if not first:
                        norm_x1(b - 1)
                    gated(b, first, last)
                    if not last:
                        split_x(b + 1)
                        split_qk(b + 1)
                    attention(b, first)
                    normed_heads(b)
                    split_output(b)
                    residual(b)

                def split_x1(b):
                    dve.wait_ge(S["xn2T_hi"], b + 1)
                    dve.tensor_tensor(xn2T[:, LO, :, :], PS[:, 0:2, :], f(xn2T[:, HI, :, :]), ALU.subtract
                                      ).then_inc(S["xn2T_lo"], 1)

                norm_x(0)
                split_x(0)
                split_qk(0)
                sequence(0, first=True)
                with dve.Fori(1, B - 1) as b:
                    sequence(b)
                sequence(B - 1, last=True)
                norm_x1(B - 1)
                split_x1(B - 1)
                route(B - 1)

            @block.gpsimd
            def _(pool):
                def power(b, ve, rs, var_sem, std_sem):
                    pool.wait_ge(S[var_sem], 3 * b + 3)
                    pool.tensor_tensor(rs[:, :], ve[:, :], neghalf[:, :], ALU.pow).then_inc(S[std_sem], 1)

                def gated(b, last):
                    for i in range(NF):
                        if i == 4 and not last:
                            power(b + 1, veps, rstd, "ln_var", "ln_std")
                        pool.wait_ge(S["h_hi"], NF * b + i + 1)
                        pool.tensor_tensor(h[:, LO, i, :], h32[:, i % 2, :], f(h[:, HI, i, :]), ALU.subtract
                                           ).then_inc(S["h_lo"], 1)

                def masks(b):
                    for g in range(NG):
                        for j in range(GH):
                            pool.wait_ge(S["exped"], 48 * b + 3 * (GH * g + j + 1))
                            pool.tensor_tensor(idle_p[:, GH * g + j:GH * g + j + 1], neghalf[:, 0:1], neghalf[:, 0:1], ALU.mult)
                            p = PT[:, g % 2, j, :]
                            first = p[:, 0:1024].rearrange("p (a k) -> p a k", a=2)[:, :, 0:P]
                            second = p[:, 896:896 + 2 * P].rearrange("p (a k) -> p a k", a=2)
                            for blocks in (first, second):
                                last = pool.affine_select(out=blocks, in_=blocks, compare_op=ALU.is_ge, fill=0.0,
                                                          base=0, pattern=[[0, 2], [1, P]], channel_multiplier=-1)
                            last.then_inc(S["masked"], 1)

                def sequence(b, first=False, last=False):
                    if not first:
                        power(b - 1, veps2, rstd2, "ln2_var", "ln2_std")
                    gated(b, last)
                    masks(b)

                power(0, veps, rstd, "ln_var", "ln_std")
                sequence(0, first=True)
                with pool.Fori(1, B - 1) as b:
                    sequence(b)
                sequence(B - 1, last=True)
                power(B - 1, veps2, rstd2, "ln2_var", "ln2_std")

        cursor[0] = first_free
        pos = keep("pos", [P, B, NT, TOPK], U32)
        block_expert = keep("block_expert", [P, NBLK], I32)
        idle_q = keep("idle_q", [P, 4])
        ramp_col = ident[:, 0:1]
        s2_at = cursor[0]
        s2 = keep("s2", [P, B * NT, C])
        after_shared = cursor[0]
        slotcnt = keep("slotcnt", [P, NBLK])
        Fwd = keep("Fwd", [P, 2, 2, FQ], F32R)
        Inv = keep("Inv", [P, 2, NQ, FQ], F32R)
        HA = keep("HA", [P, 2, 2, C])
        HB = keep("HB", [P, 2, 2, C])
        HN = keep("HN", [P, 2, 2, C])
        Win = keep("Win", [P, 2, CC, 2 * C], F32R)
        Wo2 = keep("Wo2", [P, 2, CC, C], F32R)
        bo2b = keep("bo2b", [P, C])
        binc = keep("binc", [P, 4])
        shortc = keep("shortc", [P, CC, 4])
        xT = keep("xT", [P, 2, CC, T], F32R)
        vt = keep("vt", [P, CC, T + 2])
        x2s = keep("x2s", [P, CC, T])
        cv = keep("cv", [P, 2, CC, T])
        v2 = keep("v2", [P, 2, NT, C], F32R)
        Vf = keep("Vf", [P, 2, NQ, C])
        tmp = keep("tmp", [P, 4, 2 * C])
        tmq = keep("tmq", [P, 4, 2 * C])
        Z = keep("Z", [P, 2, NQ, C])
        Zs = keep("Zs", [P, 2, 2, NQ, C], F32R)
        o32 = keep("o32", [P, CC, T])
        oTs = keep("oTs", [P, 2, CC, T], F32R)
        xrows = keep("xrows", [P, NT, C])
        posb = keep("posb", [P, NT, TOPK], U32)
        (st_f, st_i, st_win, st_wo), _ = share(("st_f", [P, 2, FQ], F32), ("st_i", [P, NQ, FQ], F32),
                                               ("st_win", [P, CC, 2 * C], F32), ("st_wo", [P, CC, C], F32))
        cursor[0] += size([P, 2, FQ], F32) + size([P, NQ, FQ], F32) + size([P, CC, 2 * C], F32) + size([P, CC, C], F32)
        fw1s = keep("fw1s", [1, 64]); posr = keep("posr", [1, T]); fb1c = keep("fb1c", [64, 1])
        fw2s = keep("fw2s", [64, P]); fb2c = keep("fb2c", [P, 1]); fw3s = keep("fw3s", [P, C])
        fb3b = keep("fb3b", [P, C]); h1s = keep("h1s", [64, T]); h2s = keep("h2s", [P, T])
        print("sbuf 2", cursor[0], nc.sbuf_usable_end)
        cursor_after = cursor[0]
        cursor[0] = cursor[0] - cursor[0] % 32
        ramp = nc.alloc_sbuf_tensor_at("ramp", [P, P], F32, offset=s2_at)
        q = {}
        off = s2_at + 512

        def over_s2(name, shape, dt=F32):
            nonlocal off
            t = nc.alloc_sbuf_tensor_at(name, shape, dt, offset=off)
            off += size(shape, dt)
            return t

        before = over_s2("before", [P, P])
        ones = over_s2("ones", [P, P])
        chf = over_s2("chf", [P, B * NT, TOPK])
        zeros = over_s2("zeros", [P, 672])
        per = over_s2("per", [P, 12, NE])
        peri = over_s2("peri", [P, 2, NE], I32)
        NTT = B * NT
        onehot = [nc.alloc_sbuf_tensor_at(f"onehot{k}", [P, NTT, NE], F32, offset=off + 2560 * k) for k in range(2)]
        cnt = nc.alloc_sbuf_tensor_at("cnt", [P, NTT, NE], F32, offset=off + 5120)
        tots = [nc.alloc_sbuf_tensor_at(f"tots{k}", [P, NTT, NE], F32, offset=off + 7680 + 2560 * k) for k in range(3)]
        slot = nc.alloc_sbuf_tensor_at("slot", [P, NTT, NE], F32, offset=off + 15360)
        slotf = nc.alloc_sbuf_tensor_at("slotf", [P, NTT, TOPK], F32, offset=off + 17920)
        be_cmp = nc.alloc_sbuf_tensor_at("be_cmp", [P, NBLK, NE], F32, offset=off + 18432)
        assert off + 18432 + NBLK * NE * 4 <= after_shared, (off, after_shared)

        r_in = sem("r_in"); r_pool = sem("r_pool"); r_dve = sem("r_dve"); r_ps = sem("r_ps"); r_hi = sem("r_hi")
        t_hi = sem("t_hi"); t_lo = sem("t_lo"); t_in = sem("t_in"); f_ps = sem("f_ps"); f_sb = sem("f_sb")
        z_in = sem("z_in"); f_hi = sem("f_hi"); f_lo = sem("f_lo"); h_sb = sem("h_sb"); f_cf = sem("f_cf")
        slots_z = sem("slots_z")

        def transform(pe, src, bank, piece_ready, done):
            for half in range(2):
                for q_ in range(NQ):
                    n = 0
                    for kc in range(2):
                        for i, j in PAIRS:
                            last = pe.matmul(PS[:, bank + 2 * half + q_ // 2, C * (q_ % 2):C * (q_ % 2) + C],
                                             Fwd[:, i, kc, P * q_:P * q_ + P], src[:, j, 2 * half + kc, :],
                                             start=n == 0, stop=n == 5)
                            n += 1
                    if q_ % 2:
                        last.then_inc(done, 1)

        with nc.Block() as block:
            @block.sync
            def _(sp):
                sp.dma_start(ramp[:, :], ramp_c.partition_broadcast(P)).then_inc(r_in, 16)
                for dst, src in ((st_f[:, :, :], dft_c.rearrange("(c p) n -> p c n", p=P)),
                                 (st_i[:, :, :], idft_c.rearrange("(c p) n -> p c n", p=P)),
                                 (st_win[:, :, :], winT.rearrange("(c p) n -> p c n", p=P)),
                                 (st_wo[:, :, :], wo2.rearrange("(c p) n -> p c n", p=P)),
                                 (bo2b[:, :], bo2.partition_broadcast(P)), (binc[:, :], bin_),
                                 (shortc[:, :, :], short), (fw1s[:, :], fw1), (posr[:, :], pos_c),
                                 (fb1c[:, :], fb1), (fw2s[:, :], fw2), (fb2c[:, :], fb2), (fw3s[:, :], fw3),
                                 (fb3b[:, :], fb3.partition_broadcast(P))):
                    sp.dma_start(dst, src).then_inc(t_in, 16)
                sp.wait_ge(z_in, 1)
                for n in range(4):
                    sp.dma_start(slots_in.rearrange("(a p m) d -> a p (m d)", a=4, p=P)[n].rearrange(
                        "p (r e) -> p r e", e=672), zeros[:, :].unsqueeze(1).to_broadcast([P, 8, 672])
                        ).then_inc(slots_z, 16)
                sp.wait_ge(slots_z, 64)

            @block.gpsimd
            def _(pool):
                pool.memset(zeros[:, :], 0.0).then_inc(z_in, 1)
                pool.memset(ones[:, :], 1.0).then_inc(r_pool, 1)
                pool.wait_ge(r_pool, 1)
                pool.affine_select(out=before[:, :], in_=ones[:, :], compare_op=ALU.is_gt, fill=0.0, base=0,
                                   pattern=[[1, P]], channel_multiplier=-1).then_inc(r_pool, 1)
                pool.memset(vt[:, :, 0:1], 0.0)
                pool.memset(vt[:, :, T + 1:T + 2], 0.0)

            @block.scalar
            def _(act):
                act.wait_ge(t_in, 16 * 14)
                for hi, src in ((Fwd, st_f), (Inv, st_i), (Win, st_win), (Wo2, st_wo)):
                    act.activation(hi[:, HI, :, :], src[:, :, :], ACT.Copy).then_inc(t_hi, 1)
                act.wait_ge(f_ps, 1)
                act.activation(h1s[:, :], PS[0:64, 4, :], ACT.Gelu, bias=fb1c[:, 0:1]).then_inc(f_sb, 1)
                act.wait_ge(f_ps, 2)
                act.activation(h2s[:, :], PS[:, 5, :], ACT.Gelu, bias=fb2c[:, 0:1]).then_inc(f_sb, 1)
                act.wait_ge(f_cf, 1)
                act.activation(v2[:, HI, :, :], Z[:, 0, :, :], ACT.Copy).then_inc(f_hi, 1)
                for half in range(2):
                    act.wait_ge(f_ps, 4 + 2 * half)
                    act.activation(HA[:, half, :, :].rearrange("p a c -> p (a c)"), PS[:, 4 + 2 * half, :], ACT.Copy
                                   ).then_inc(h_sb, 1)
                    act.activation(HN[:, half, :, :].rearrange("p a c -> p (a c)"), PS[:, 4 + 2 * half, :], ACT.Copy
                                   ).then_inc(h_sb, 1)
                    act.wait_ge(f_ps, 5 + 2 * half)
                    act.activation(HB[:, half, :, :].rearrange("p a c -> p (a c)"), PS[:, 5 + 2 * half, :], ACT.Copy
                                   ).then_inc(h_sb, 1)

            @block.tensor
            def _(pe):
                pe.wait_ge(t_in, 16 * 14)
                pe.matmul(PS[0:64, 4, :], fw1s[:, :], posr[:, :], start=True, stop=True).then_inc(f_ps, 1)
                pe.wait_ge(f_sb, 1)
                pe.matmul(PS[:, 5, :], fw2s[:, :], h1s[:, :], start=True, stop=True).then_inc(f_ps, 1)
                pe.wait_ge(f_sb, 2)
                for t in range(NT):
                    last = pe.matmul(PS[:, 6 + t // 2, C * (t % 2):C * (t % 2) + C], h2s[:, P * t:P * t + P], fw3s[:, :],
                                     start=True, stop=True)
                last.then_inc(f_ps, 1)
                pe.wait_ge(r_pool, 2)
                pe.wait_ge(r_dve, 4)
                for n, lhs in enumerate((before, ones)):
                    for half in range(2):
                        last = pe.matmul(PS[:, 2 * n + half, 0:16 * NE], lhs[:, :],
                                         cnt[:, 16 * half:16 * half + 16, :].rearrange("p t e -> p (t e)"),
                                         start=True, stop=True)
                last.then_inc(r_ps, 1)
                pe.wait_ge(f_lo, 1)
                transform(pe, v2, 4, None, f_ps)

            @block.vector
            def _(dve):
                made = [0]

                def step(ins):
                    made[0] += 1
                    ins.then_inc(r_dve, 1)
                    dve.wait_ge(r_dve, made[0])

                def bc_e(ap, n):
                    return ap.unsqueeze(1).to_broadcast([P, n, NE])

                dve.wait_ge(r_in, 16)
                step(dve.tensor_copy(chf[:, :, :], chosen[:, :, :]))
                for k in range(TOPK):
                    step(dve.tensor_tensor(onehot[k][:, :, :], bc_e(ramp[:, 0:NE], NTT),
                                           chf[:, :, k].unsqueeze(2).to_broadcast([P, NTT, NE]), ALU.is_equal))
                step(dve.tensor_tensor(cnt[:, :, :], onehot[0][:, :, :], onehot[1][:, :, :], ALU.add))
                dve.wait_ge(f_ps, 3)
                for n in range(2):
                    last = dve.tensor_tensor(Z[:, 0, 2 * n:2 * n + 2, :], PS[:, 6 + n, :].rearrange("p (t c) -> p t c", t=2),
                                             fb3b[:, :].unsqueeze(1).to_broadcast([P, 2, C]), ALU.add)
                last.then_inc(f_cf, 1)
                for n, (w, src) in enumerate(((Fwd, st_f), (Inv, st_i), (Win, st_win), (Wo2, st_wo))):
                    dve.wait_ge(t_hi, n + 1)
                    dve.tensor_tensor(w[:, LO, :, :], src[:, :, :], f(w[:, HI, :, :]), ALU.subtract)
                dve.wait_ge(f_hi, 1)
                dve.tensor_tensor(v2[:, LO, :, :], Z[:, 0, :, :], f(v2[:, HI, :, :]), ALU.subtract).then_inc(f_lo, 1)
                dve.wait_ge(r_ps, 1)
                tiles = lambda n: PS[:, n:n + 2, 0:16 * NE].rearrange("p a (t e) -> p a t e", e=NE)
                halves = lambda t: t[:, :, :].rearrange("p (a t) e -> p a t e", a=2)
                step(dve.tensor_copy(halves(tots[0]), tiles(2)))
                step(dve.tensor_copy(tots[1][:, :, :], tots[0][:, :, :]))
                src, dst = 1, 2
                for d in (1, 2, 4, 8, 16):
                    dve.tensor_copy(tots[dst][:, 0:d, :], tots[src][:, 0:d, :])
                    step(dve.tensor_tensor(tots[dst][:, d:, :], tots[src][:, d:, :], tots[src][:, 0:NTT - d, :], ALU.add))
                    src, dst = dst, src
                run = tots[src]
                step(dve.tensor_scalar(peri[:, 0, :], run[:, NTT - 1, :], float(P - 1), None, ALU.add))
                step(dve.tensor_scalar(peri[:, 1, :], peri[:, 0, :], 7, None, ALU.arith_shift_right))
                step(dve.tensor_copy(per[:, 0, :], peri[:, 1, :]))
                step(dve.tensor_copy(per[:, 1, :], per[:, 0, :]))
                a, z = 1, 2
                for d in (1, 2, 4, 8, 16):
                    dve.tensor_copy(per[:, z, 0:d], per[:, a, 0:d])
                    step(dve.tensor_tensor(per[:, z, d:NE], per[:, a, d:NE], per[:, a, 0:NE - d], ALU.add))
                    a, z = z, a
                end = per[:, a, :]
                step(dve.tensor_tensor(per[:, 4, :], end, per[:, 0, :], ALU.subtract))
                step(dve.tensor_scalar(per[:, 5, :], per[:, 4, :], float(P), None, ALU.mult))
                step(dve.tensor_tensor(slot[:, :, :], run[:, :, :], tots[0][:, :, :], ALU.subtract))
                step(dve.tensor_tensor(slot[:, :, :], slot[:, :, :], bc_e(per[:, 5, :], NTT), ALU.add))
                step(dve.tensor_tensor(halves(slot), halves(slot), tiles(0), ALU.add))
                for k in range(TOPK):
                    step(dve.tensor_tensor(onehot[k][:, :, :], onehot[k][:, :, :], slot[:, :, :], ALU.mult))
                    step(dve.tensor_reduce(out=slotf[:, :, k], in_=onehot[k][:, :, :], op=ALU.add, axis=AX.X))
                step(dve.tensor_copy(pos[:, :, :, :].rearrange("p b t k -> p (b t) k"), slotf[:, :, :]))
                step(dve.tensor_tensor(be_cmp[:, :, :], bc_e(end, NBLK),
                                       ramp[:, 0:NBLK].unsqueeze(2).to_broadcast([P, NBLK, NE]), ALU.is_le))
                step(dve.tensor_reduce(out=slotcnt[:, :],
                                       in_=be_cmp[:, :, :], op=ALU.add, axis=AX.X))
                step(dve.tensor_scalar(block_expert[:, :], slotcnt[:, :], float(NE - 1), None, ALU.min))
                dve.wait_ge(h_sb, 6)
                step(dve.tensor_copy(HN[0:1, :, 0, :], HB[0:1, :, 0, :]))
                dve.memset(HB[0:1, :, 0, :], 0.0)

        U = {n: sem("u_" + n) for n in """xT_in xr_in posb_sb sent vx_ps vx_sb conv0 conv tr v2_hi v2_lo vf_ps vf_sb
            dstep pstep z_hi z_lo y_ps o_sb o_hi o_lo s_ps s_sb""".split()}
        ND, NPQ = 13, 7
        with nc.Block() as block:
            @block.sync
            def _(sp):
                with sp.Fori(0, B) as b:
                    sp.wait_ge(U["vx_ps"], 4 * b)
                    sp.dma_start(f(xT[:, :, :, :]), xn2T_parts[b]).then_inc(U["xT_in"], 16)
                    sp.wait_ge(U["sent"], 128 * b)
                    sp.dma_start(xrows[:, :, :], xn2_rows[b].rearrange("(t p) d -> p t d", p=P)
                                 ).then_inc(U["xr_in"], 16)

            @block.tensor
            def _(pe):
                def products(out, lhs, rhs, chunks):
                    n, last = len(PAIRS) * chunks, None
                    for c in range(chunks):
                        for i, j in PAIRS:
                            n -= 1
                            last = pe.matmul(out, lhs(i, c), rhs(j, c), start=last is None, stop=n == 0)
                    return last

                with pe.Fori(0, B) as b:
                    pe.wait_ge(U["xT_in"], 16 * (b + 1))
                    pe.wait_ge(U["vf_sb"], 4 * b)
                    for m in range(4):
                        products(PS[:, m, :], lambda i, c: Win[:, i, c, P * m:P * m + P],
                                 lambda j, c: xT[:, j, c, :], CC).then_inc(U["vx_ps"], 1)
                    pe.wait_ge(U["conv"], 4 * (b + 1))
                    pe.wait_ge(U["s_sb"], 2 * b)
                    for t in range(NT):
                        for m in range(CC):
                            o = C * (t % 2) + P * m
                            last = pe.transpose(PS[:, 4 + t // 2, o:o + P], cv[:, 0, m, P * t:P * t + P], ident[:, :])
                    last.then_inc(U["tr"], 1)
                    pe.wait_ge(U["v2_lo"], b + 1)
                    pe.wait_ge(U["vx_sb"], 4 * (b + 1))
                    transform(pe, v2, 0, None, U["vf_ps"])
                    pe.wait_ge(U["z_lo"], 2 * (b + 1))
                    pe.wait_ge(U["o_sb"], 2 * b)
                    for m in range(CC):
                        products(PS[:, 6 + m, :], lambda i, c: Zs[:, i, 0, c, P * m:P * m + P],
                                 lambda j, c: Inv[:, j, c, :], NQ)
                        n = 0
                        for c in range(NQ):
                            for i, j in PAIRS:
                                n += 1
                                last = pe.matmul(PS[:, 6 + m, T // 2:T], Zs[:, i, 1, c, P * m:P * m + P],
                                                 Inv[:, j, c, 0:T // 2], start=False, stop=n == 3 * NQ,
                                                 skip_group_check=True)
                        last.then_inc(U["y_ps"], 1)
                    pe.wait_ge(U["o_lo"], b + 1)
                    for t in range(NT):
                        last = products(PS[:, 4 + t // 2, C * (t % 2):C * (t % 2) + C],
                                        lambda i, c: oTs[:, i, c, P * t:P * t + P], lambda j, c: Wo2[:, j, c, :], CC)
                        if t % 2:
                            last.then_inc(U["s_ps"], 1)

            @block.scalar
            def _(act):
                with act.Fori(0, B) as b:
                    for m in range(4):
                        act.wait_ge(U["vx_ps"], 4 * b + m + 1)
                        if m == 0:
                            act.wait_ge(U["conv"], 4 * b)
                        if m == 2:
                            act.wait_ge(U["o_sb"], 2 * b)
                        dst = vt[:, m, 1:T + 1] if m < 2 else x2s[:, m - 2, :]
                        act.activation(dst, PS[:, m, :], ACT.Identity, bias=binc[:, m:m + 1]).then_inc(U["vx_sb"], 1)
                    act.wait_ge(U["tr"], b + 1)
                    act.wait_ge(U["vf_ps"], 4 * b)
                    act.activation(v2[:, HI, :, :].rearrange("p (a t) c -> p a (t c)", a=2), PS[:, 4:6, :], ACT.Copy
                                   ).then_inc(U["v2_hi"], 1)
                    for n in range(4):
                        act.wait_ge(U["vf_ps"], 4 * b + n + 1)
                        if n == 0:
                            act.wait_ge(U["dstep"], ND * b)
                            act.wait_ge(U["pstep"], NPQ * b)
                        act.activation(Vf[:, n // 2, 2 * (n % 2):2 * (n % 2) + 2, :].rearrange("p q c -> p (q c)"),
                                       PS[:, n, :], ACT.Copy).then_inc(U["vf_sb"], 1)
                    for z in range(2):
                        act.wait_ge(U["dstep"], ND * b + (6 if z == 0 else ND))
                        if z == 0:
                            act.wait_ge(U["y_ps"], 2 * b)
                        else:
                            act.wait_ge(U["pstep"], NPQ * (b + 1))
                        act.activation(Zs[:, HI, z, :, :], Z[:, z, :, :], ACT.Copy).then_inc(U["z_hi"], 1)
                    act.wait_ge(U["o_sb"], 2 * (b + 1))
                    act.wait_ge(U["s_ps"], 2 * b)
                    act.activation(oTs[:, HI, :, :], o32[:, :, :], ACT.Copy).then_inc(U["o_hi"], 1)

            @block.vector
            def _(dve):
                with dve.Fori(0, B) as b:
                    dve.wait_ge(U["sent"], 128 * b)
                    dve.tensor_copy(posb[:, :, :], pos[:, bass.ds(b, 1), :, :].rearrange("p o t k -> p (o t) k")
                                    ).then_inc(U["posb_sb"], 1)
                    for k in (1, 2):
                        for m in range(CC):
                            if k == 1:
                                dve.wait_ge(U["conv0"], 2 * b + m + 1)
                                dve.wait_ge(U["tr"], b)
                            else:
                                dve.wait_ge(U["conv"], 4 * b + m + 1)
                            dve.scalar_tensor_tensor(out=cv[:, 2 - k, m, :], in0=vt[:, m, k:k + T],
                                                     scalar=shortc[:, m, k:k + 1],
                                                     in1=cv[:, k - 1, m, :], op0=ALU.mult, op1=ALU.add
                                                     ).then_inc(U["conv"], 1)
                    dve.wait_ge(U["v2_hi"], b + 1)
                    dve.tensor_tensor(v2[:, LO, :, :].rearrange("p (a t) c -> p a (t c)", a=2), PS[:, 4:6, :],
                                      f(v2[:, HI, :, :]).rearrange("p (a t) c -> p a (t c)", a=2), ALU.subtract
                                      ).then_inc(U["v2_lo"], 1)
                    made = 0

                    def step(ins):
                        nonlocal made
                        made += 1
                        ins.then_inc(U["dstep"], 1)

                    def done(n):
                        dve.wait_ge(U["dstep"], ND * b + n)

                    flat = lambda ap: ap.rearrange("p q c -> p (q c)")
                    re = lambda h_: flat(Vf[:, h_, 0:2, :])
                    im = lambda h_: flat(Vf[:, h_, 2:4, :])
                    tb = lambda t_, h_: flat(t_[:, h_, :, :])
                    mul = lambda n, a_, b_: step(dve.tensor_tensor(tmp[:, n, :], a_, b_, ALU.mult))
                    dve.wait_ge(U["vf_sb"], 4 * b + 2)
                    dve.wait_ge(U["z_lo"], 2 * b)
                    mul(0, re(0), tb(HA, 0))
                    mul(1, im(0), tb(HB, 0))
                    mul(2, re(0), tb(HB, 0))
                    mul(3, im(0), tb(HN, 0))
                    done(2)
                    step(dve.tensor_tensor(flat(Z[:, 0, 0:2, :]), tmp[:, 0, :], tmp[:, 1, :], ALU.subtract))
                    done(4)
                    step(dve.tensor_tensor(flat(Z[:, 0, 2:4, :]), tmp[:, 2, :], tmp[:, 3, :], ALU.add))
                    done(5)
                    mul(0, re(0), tb(HA, 1))
                    mul(1, im(0), tb(HB, 1))
                    dve.wait_ge(U["vf_sb"], 4 * b + 4)
                    done(6)
                    mul(2, re(1), tb(HA, 0))
                    mul(3, im(1), tb(HB, 0))
                    done(8)
                    step(dve.tensor_tensor(tmp[:, 0, :], tmp[:, 0, :], tmp[:, 1, :], ALU.subtract))
                    done(10)
                    step(dve.tensor_tensor(tmp[:, 2, :], tmp[:, 2, :], tmp[:, 3, :], ALU.subtract))
                    done(12)
                    step(dve.tensor_tensor(flat(Z[:, 1, 0:2, :]), tmp[:, 0, :], tmp[:, 2, :], ALU.add))
                    assert made == ND
                    for z in range(2):
                        dve.wait_ge(U["z_hi"], 2 * b + z + 1)
                        dve.tensor_tensor(Zs[:, LO, z, :, :], Z[:, z, :, :], f(Zs[:, HI, z, :, :]), ALU.subtract
                                          ).then_inc(U["z_lo"], 1)
                    for m in range(CC):
                        dve.wait_ge(U["y_ps"], 2 * b + m + 1)
                        if m == 0:
                            dve.wait_ge(U["o_lo"], b)
                        dve.tensor_tensor(o32[:, m, :], PS[:, 6 + m, :], x2s[:, m, :], ALU.mult).then_inc(U["o_sb"], 1)
                    dve.wait_ge(U["o_hi"], b + 1)
                    dve.tensor_tensor(oTs[:, LO, :, :], o32[:, :, :], f(oTs[:, HI, :, :]), ALU.subtract
                                      ).then_inc(U["o_lo"], 1)
                    for n in range(2):
                        dve.wait_ge(U["s_ps"], 2 * b + n + 1)
                        dve.tensor_tensor(s2[:, bass.ds(NT * b + 2 * n, 2), :],
                                          PS[:, 4 + n, :].rearrange("p (t c) -> p t c", t=2),
                                          bo2b[:, :].unsqueeze(1).to_broadcast([P, 2, C]), ALU.add
                                          ).then_inc(U["s_sb"], 1)

            @block.gpsimd
            def _(pool):
                flat = lambda ap: ap.rearrange("p q c -> p (q c)")
                with pool.Fori(0, B) as b:
                    for m in range(CC):
                        pool.wait_ge(U["vx_sb"], 4 * b + m + 1)
                        pool.wait_ge(U["tr"], b)
                        pool.wait_ge(U["conv"], 4 * b)
                        pool.tensor_tensor(idle_q[:, m:m + 1], ramp_col[:, :], ramp_col[:, :], ALU.mult)
                        pool.tensor_scalar(cv[:, 0, m, :], vt[:, m, 0:T], shortc[:, m, 0:1], shortc[:, m, 3:4],
                                           ALU.mult, ALU.add).then_inc(U["conv0"], 1)
                    pool.wait_ge(U["xr_in"], 16 * (b + 1))
                    pool.wait_ge(U["posb_sb"], b + 1)
                    pool.tensor_tensor(idle_q[:, 2:3], ramp_col[:, :], ramp_col[:, :], ALU.mult)
                    for t in range(NT):
                        for k in range(TOPK):
                            pool.indirect_dma_start(slots_in, bass.IndirectOffsetOnAxis(posb[:, t, k:k + 1], axis=0),
                                                    xrows[:, t, :], None).then_inc(U["sent"], 16)
                    made = 0

                    def step(ins):
                        nonlocal made
                        made += 1
                        ins.then_inc(U["pstep"], 1)

                    pool.wait_ge(U["vf_sb"], 4 * b + 4)
                    pool.wait_ge(U["z_lo"], 2 * b)
                    mul = lambda n, a_, b_: step(pool.tensor_tensor(tmq[:, n, :], flat(a_), flat(b_), ALU.mult))
                    mul(0, Vf[:, 0, 0:2, :], HB[:, 1, :, :])
                    mul(1, Vf[:, 0, 2:4, :], HN[:, 1, :, :])
                    mul(2, Vf[:, 1, 0:2, :], HB[:, 0, :, :])
                    mul(3, Vf[:, 1, 2:4, :], HN[:, 0, :, :])
                    pool.wait_ge(U["pstep"], NPQ * b + 2)
                    step(pool.tensor_tensor(tmq[:, 0, :], tmq[:, 0, :], tmq[:, 1, :], ALU.add))
                    pool.wait_ge(U["pstep"], NPQ * b + 4)
                    step(pool.tensor_tensor(tmq[:, 2, :], tmq[:, 2, :], tmq[:, 3, :], ALU.add))
                    pool.wait_ge(U["pstep"], NPQ * b + 6)
                    step(pool.tensor_tensor(flat(Z[:, 1, 2:4, :]), tmq[:, 0, :], tmq[:, 2, :], ALU.add))
                pool.wait_ge(U["sent"], 128 * B)

        cursor[0] = after_shared
        Wes = keep("Wes", [P, 2, CC, NE * C], F32R)
        bes = keep("bes", [P, NE * C])
        st_we, st_off = share(("st_we", [P, CC, NE * C // 2], F32))
        (xb, xbT, yb), e1 = share(("xb", [P, 4, C], F32), ("xbT", [P, 4, 2, CC, P], F32R), ("yb", [P, 4, C], F32))
        st_we = st_we[0]
        e_in = sem("e_in"); e_hi = sem("e_hi"); e_lo = sem("e_lo")
        with nc.Block() as block:
            @block.sync
            def _(sp):
                sp.dma_start(bes[:, :], be.partition_broadcast(P)).then_inc(e_in, 16)
                for n in range(2):
                    if n:
                        sp.wait_ge(e_lo, CC)
                    for c in range(CC):
                        sp.dma_start(st_we[:, c, :], We[10 * n:10 * n + 10, P * c:P * c + P, :].rearrange(
                            "e p n -> p e n")).then_inc(e_in, 16)
                    sp.wait_ge(e_in, 16 * (1 + CC * (n + 1)))

            @block.scalar
            def _(act):
                for n in range(2):
                    act.wait_ge(e_in, 16 * (1 + CC * (n + 1)))
                    for c in range(CC):
                        act.activation(Wes[:, HI, c, 2560 * n:2560 * n + 2560], st_we[:, c, :], ACT.Copy).then_inc(e_hi, 1)

            @block.vector
            def _(dve):
                for n in range(2):
                    for c in range(CC):
                        dve.wait_ge(e_hi, CC * n + c + 1)
                        o = slice(2560 * n, 2560 * n + 2560)
                        dve.tensor_tensor(Wes[:, LO, c, o], st_we[:, c, :], f(Wes[:, HI, c, o]), ALU.subtract
                                          ).then_inc(e_lo, 1)

        W = {n: sem("e_" + n + "_of") for n in "tr hi lo out kept".split()}
        xb_in = [sem(f"xb_in{u}") for u in range(4)]
        yb_out = [sem(f"yb_out{u}") for u in range(4)]
        NI = NBLK // 4
        with nc.Block() as block:
            @block.sync
            def _(sp):
                rows = lambda ap, j: ap.rearrange("(j p) d -> j p d", p=P)[j]
                with sp.Fori(0, NI) as i:
                    for u in range(4):
                        sp.wait_ge(W["tr"], 4 * i)
                        sp.dma_start(xb[:, u, :], rows(slots_in, 4 * i + u)).then_inc(xb_in[u], 16)
                    for u in range(4):
                        sp.wait_ge(W["kept"], 4 * i + u + 1)
                        sp.dma_start(rows(slots_out, 4 * i + u), yb[:, u, :]).then_inc(yb_out[u], 16)
                for u in range(4):
                    sp.wait_ge(yb_out[u], 16 * NI)

            @block.tensor
            def _(pe):
                with pe.Fori(0, NI) as i:
                    experts = [pe.value_load(block_expert[0:1, bass.ds(4 * i + u, 1)], min_val=0, max_val=NE - 1)
                               for u in range(4)]

                    def turn(u):
                        pe.wait_ge(xb_in[u], 16 * (i + 1))
                        pe.wait_ge(W["lo"], 4 * i)
                        for c in range(CC):
                            last = pe.transpose(PS[:, u, P * c:P * c + P], xb[:, u, P * c:P * c + P], ident[:, :])
                        last.then_inc(W["tr"], 1)

                    def expert(u):
                        pe.wait_ge(W["lo"], 4 * i + u + 1)
                        pe.wait_ge(W["kept"], 4 * i)
                        n = 0
                        for c in range(CC):
                            for a, z in PAIRS:
                                last = pe.matmul(PS[:, 4 + u, 0:C], xbT[:, u, a, c, :],
                                                 Wes[:, z, c, bass.ds(experts[u] * C, C)], start=n == 0, stop=n == 5)
                                n += 1
                        last.then_inc(W["out"], 1)

                    for u in range(6):
                        if u < 4:
                            turn(u)
                        if u >= 2:
                            expert(u - 2)

            @block.scalar
            def _(act):
                with act.Fori(0, NI) as i:
                    for u in range(4):
                        act.wait_ge(W["tr"], 4 * i + u + 1)
                        act.wait_ge(W["out"], 4 * i)
                        act.activation(xbT[:, u, HI, :, :].rearrange("p c k -> p (c k)"), PS[:, u, 0:C], ACT.Copy
                                       ).then_inc(W["hi"], 1)

            @block.vector
            def _(dve):
                with dve.Fori(0, NI) as i:
                    experts = [dve.value_load(block_expert[0:1, bass.ds(4 * i + u, 1)], min_val=0, max_val=NE - 1)
                               for u in range(4)]

                    def keep_out(u):
                        dve.wait_ge(W["out"], 4 * i + u + 1)
                        dve.wait_ge(yb_out[u], 16 * i)
                        dve.tensor_tensor(yb[:, u, :], PS[:, 4 + u, 0:C], bes[:, bass.ds(experts[u] * C, C)], ALU.add
                                          ).then_inc(W["kept"], 1)

                    for u in range(4):
                        dve.wait_ge(W["hi"], 4 * i + u + 1)
                        dve.tensor_tensor(xbT[:, u, LO, :, :].rearrange("p c k -> p (c k)"), PS[:, u, 0:C],
                                          f(xbT[:, u, HI, :, :]).rearrange("p c k -> p (c k)"), ALU.subtract
                                          ).then_inc(W["lo"], 1)
                        if u >= 2:
                            keep_out(u - 2)
                    keep_out(2)
                    keep_out(3)

        cursor[0] = after_shared
        yg = keep("yg", [P, TOPK, NT, C])
        acc = keep("acc", [P, NT, C])
        acc2 = keep("acc2", [P, NT, C])
        sg = keep("sg", [P, NT, C])
        x1b = keep("x1b", [P, NT, C])
        posc = keep("posc", [P, NT, TOPK], U32)
        gb = keep("gb", [P, NT, TOPK])
        X = {n: sem("x_" + n) for n in "idle x1_in posc_sb gb_sb got acc_sb acc2_sb sg_sb prod out_sb stored".split()}
        with nc.Block() as block:
            @block.sync
            def _(sp):
                with sp.Fori(0, B) as b:
                    sp.wait_ge(X["out_sb"], b)
                    sp.dma_start(x1b[:, :, :], x1_rows[b].rearrange("(t p) d -> p t d", p=P)).then_inc(X["x1_in"], 16)
                    sp.wait_ge(X["out_sb"], b + 1)
                    sp.dma_start(out[b].rearrange("(t p) d -> p t d", p=P), sg[:, :, :]).then_inc(X["stored"], 16)
                sp.wait_ge(X["stored"], 16 * B)

            @block.gpsimd
            def _(pool):
                with pool.Fori(0, B) as b:
                    pool.wait_ge(X["posc_sb"], b + 1)
                    pool.wait_ge(X["acc2_sb"], b)
                    pool.wait_ge(X["idle"], b)
                    pool.tensor_tensor(idle_q[:, 3:4], ramp_col[:, :], ramp_col[:, :], ALU.mult
                                       ).then_inc(X["idle"], 1)
                    for k in range(TOPK):
                        for t in range(NT):
                            pool.indirect_dma_start(yg[:, k, t, :], None, slots_out,
                                                    bass.IndirectOffsetOnAxis(posc[:, t, k:k + 1], axis=0)
                                                    ).then_inc(X["got"], 16)
                pool.wait_ge(X["got"], 128 * B)

            @block.vector
            def _(dve):
                with dve.Fori(0, B) as b:
                    dve.wait_ge(X["got"], 128 * b)
                    dve.tensor_copy(posc[:, :, :], pos[:, bass.ds(b, 1), :, :].rearrange("p o t k -> p (o t) k")
                                    ).then_inc(X["posc_sb"], 1)
                    dve.wait_ge(X["acc2_sb"], b)
                    dve.tensor_copy(gb[:, :, :], gates[:, bass.ds(NT * b, NT), :]).then_inc(X["gb_sb"], 1)
                    dve.wait_ge(X["gb_sb"], b + 1)
                    dve.wait_ge(X["got"], 128 * (b + 1))
                    for t in range(NT):
                        last = dve.tensor_scalar(acc[:, t, :], yg[:, 0, t, :], gb[:, t, 0:1], None, ALU.mult)
                    last.then_inc(X["acc_sb"], 1)
                    dve.wait_ge(X["acc_sb"], b + 1)
                    dve.wait_ge(X["sg_sb"], b)
                    for t in range(NT):
                        last = dve.scalar_tensor_tensor(out=acc2[:, t, :], in0=yg[:, 1, t, :], scalar=gb[:, t, 1:2],
                                                        in1=acc[:, t, :], op0=ALU.mult, op1=ALU.add)
                    last.then_inc(X["acc2_sb"], 1)
                    dve.wait_ge(X["sg_sb"], b + 1)
                    dve.tensor_tensor(acc[:, :, :], sg[:, :, :], s2[:, bass.ds(NT * b, NT), :], ALU.mult
                                      ).then_inc(X["prod"], 1)
                    dve.wait_ge(X["prod"], b + 1)
                    dve.wait_ge(X["x1_in"], 16 * (b + 1))
                    dve.tensor_tensor(sg[:, :, :], acc[:, :, :], x1b[:, :, :], ALU.add).then_inc(X["out_sb"], 1)

            @block.scalar
            def _(act):
                with act.Fori(0, B) as b:
                    act.wait_ge(X["acc2_sb"], b + 1)
                    act.wait_ge(X["stored"], 16 * b)
                    act.activation(sg[:, :, :], acc2[:, :, :], ACT.Silu).then_inc(X["sg_sb"], 1)


def constants():
    half = T // 2
    t = np.arange(FQ, dtype=np.float64)
    k = np.arange(half, dtype=np.float64)
    angle = 2 * np.pi * np.outer(t, k) / FQ
    top = np.where(t % 2 == 0, 1.0, -1.0)
    fwd = np.concatenate([np.cos(angle), -np.sin(angle)], axis=1)
    fwd[:, half] = top
    weight = np.full(half, 2.0 / FQ)
    weight[0] = 1.0 / FQ
    inv = np.concatenate([(np.cos(angle) * weight).T, (-np.sin(angle) * weight).T], axis=0)
    inv[half] = top / FQ
    return {"ident_c": np.eye(P, dtype=np.float32), "ramp_c": np.arange(P, dtype=np.float32)[None],
            "pos_c": np.linspace(0.0, 1.0, T, dtype=np.float32)[None],
            "dft_c": np.ascontiguousarray(fwd[:half], dtype=np.float32), "idft_c": inv.astype(np.float32)}


def kernel(**inputs):
    import concourse.bacc as bacc
    from concourse.bass_utils import run_bass_kernel_spmd

    a = {name: np.asarray(v) for name, v in inputs.items()}

    def padded(w, shape):
        out = np.zeros(shape, w.dtype)
        out[tuple(slice(0, n) for n in w.shape)] = w
        return out

    columns = lambda v: v.reshape(-1, P).T
    w_in, b_in = a["L1_attn_in_proj_w"], a["L1_attn_in_proj_b"]
    short = np.concatenate([a["L1_attn_short_w"][:, 0, :], a["L1_attn_short_b"][:, None]], axis=1)
    arrays = {
        "x": a["L0_attn_x"], "wqkvT": a["L0_attn_w_qkv"].T, "woutT": a["L0_attn_w_out"].T,
        "wguT": np.concatenate([a["L0_ffn_w_gate"], a["L0_ffn_w_up"]]).T, "wdT": a["L0_ffn_w_down"].T,
        "wg1": padded(a["L1_ffn_wg1"], (C, P)), "bg1": padded(a["L1_ffn_bg1"][:, None], (P, 1)),
        "wg2": a["L1_ffn_wg2"][:, :NE], "bg2": a["L1_ffn_bg2"][None, :NE],
        "winT": np.concatenate([w_in[:, 0::3], w_in[:, 2::3]], axis=1),
        "bin_": columns(np.concatenate([b_in[0::3], b_in[2::3]])),
        "short": short.reshape(CC, P, 4).transpose(1, 0, 2),
        "wo2": a["L1_attn_out_w"], "bo2": a["L1_attn_out_b"][None],
        "fw1": a["L1_attn_fw1"], "fb1": a["L1_attn_fb1"][:, None], "fw2": a["L1_attn_fw2"],
        "fb2": a["L1_attn_fb2"][:, None], "fw3": a["L1_attn_fw3"][:, 1::2], "fb3": a["L1_attn_fb3"][None, 1::2],
        "We": a["L1_ffn_We"], "be": a["L1_ffn_be"].reshape(1, -1),
    }
    arrays.update(constants())
    arrays = {name: np.ascontiguousarray(v) for name, v in arrays.items()}
    nc = bacc.Bacc("TRN2", target_bir_lowering=False, num_devices=1)
    args = {name: nc.dram_tensor(name, v.shape, mybir.dt.from_np(v.dtype), kind="ExternalInput").ap()
            for name, v in arrays.items()}
    args["out"] = nc.dram_tensor("out", (B, T, C), F32, kind="ExternalOutput").ap()
    program(nc, **args)
    return run_bass_kernel_spmd(nc, [arrays], core_ids=[0]).results[0]["out"]
```

```python
import math
import numpy as np
import concourse.bass as bass
from concourse import mybir
from contextlib import ExitStack

F32 = mybir.dt.float32
F32R = mybir.dt.float32r
F16 = mybir.dt.float16
I32 = mybir.dt.int32
U32 = mybir.dt.uint32
ALU = mybir.AluOpType
ACT = mybir.ActivationFunctionType
AX = mybir.AxisListType

P = 128
B, T, C = 8, 512, 256
NT = T // P
CC = C // P
NH, HD = 16, 16
NG, GH = 4, 4
SCALE = 1.0 / math.sqrt(HD)
FF = 768
NF = FF // P
QSCALE = 1.0 / 127.0
EPS = 1e-5
MASK = -10000.0 / SCALE
KS = 96
HG = 64
NE, TOPK = 20, 2
NBLK = B * T * TOPK // P + NE
FQ = 512
NQ = FQ // P
HI, LO = 0, 1
EARLY = 2
FIRST_HALF = 3
ZW = 448
M0 = 64
PAIRS = ((HI, HI), (HI, LO), (LO, HI))
Q_PARTS, K_PARTS = zip(*PAIRS)


def at_least(eng, sem, value):
    if isinstance(value, int) and value <= 0:
        return
    eng.wait_ge(sem, value)


def program(nc, x, wqkvT, woutT, wguT, wdT, wg1, bg1, wg2, bg2, winT, bin_, short, wo2, bo2, fw1, fb1, fw2, fb2,
            fw3, fb3, We, be, ident_c, ramp_c, pos_c, dft_c, idft_c, out):
    x1_rows = nc.dram_tensor("x1_rows", (B, T, C), F32, kind="Internal").ap()
    xn2_rows = nc.dram_tensor("xn2_rows", (B, T, C), F32, kind="Internal").ap()
    xn2T_parts = nc.dram_tensor("xn2T_parts", (B, P, 2, CC, T), F32, kind="Internal").ap()
    qk_parts = nc.dram_tensor("qk_parts", (2, 2, P, 2, T), F32, kind="Internal").ap()
    slots_in = nc.dram_tensor("slots_in", (NBLK * P, C), F32, kind="Internal").ap()
    slots_out = nc.dram_tensor("slots_out", (NBLK * P, C), F32, kind="Internal").ap()
    ctx = ExitStack()
    with ctx:
        sem = lambda name: ctx.enter_context(nc.semaphore(name))
        cursor = [-(-nc.sbuf_base // 32) * 32]

        def size(shape, dt):
            n = 2 if dt == F16 else 4
            for s in shape[1:]:
                n *= s
            return -(-n // 32) * 32

        def keep(name, shape, dt=F32):
            off = cursor[0]
            cursor[0] += size(shape, dt)
            return nc.alloc_sbuf_tensor_at(name, shape, dt, offset=off)

        def share(*tensors):
            made, off = [], cursor[0]
            for name, shape, dt in tensors:
                made.append(nc.alloc_sbuf_tensor_at(name, shape, dt, offset=off))
                off += size(shape, dt)
            return made, off

        ident = keep("ident", [P, P])
        gates = keep("gates", [P, B * NT, TOPK])
        chosen = keep("chosen", [P, B * NT, TOPK], U32)
        first_free = cursor[0]
        ident16 = keep("ident16", [P, P], F16)
        mask16 = keep("mask16", [P, P], F16)
        Wqkv = keep("Wqkv", [P, 2, CC, 3 * C], F32R)
        Wout = keep("Wout", [P, 2, CC, C], F32R)
        Wgu = keep("Wgu", [P, CC, 2 * FF], F32R)
        Wd = keep("Wd", [P, NF, C], F32R)
        Wg1 = keep("Wg1", [P, 2, CC, P], F32R)
        Wg2 = keep("Wg2", [HG, NE])
        bg1c = keep("bg1c", [P, 1])
        bg2b = keep("bg2b", [P, NE])
        neghalf = keep("neghalf", [P, NT])
        zeros = keep("zeros", [P, T])
        xin = keep("xin", [P, NT, C])
        xres = keep("xres", [P, NT, C])
        xn = keep("xn", [P, NT, C])
        xnT = keep("xnT", [P, 2, CC, T], F32R)
        qs = keep("qs", [KS, NH, T], F32R)
        ks = keep("ks", [KS, NH, T], F32R)
        V = keep("V", [P, NT, NH, 2 * HD])
        G = keep("G", [P, NT, C])
        Mneg = keep("Mneg", [P, 2, NT, GH])
        Mhi = keep("Mhi", [P, NT, GH], F32R)
        Mparts = keep("Mparts", [P, NT, 2, GH])
        mrow = keep("mrow", [2 * GH, T])
        stats = keep("stats", [P, NT, 6])
        mv = keep("mv", [P, NT, 2])
        veps = keep("veps", [P, NT])
        rstd = keep("rstd", [P, NT])
        stats2 = keep("stats2", [P, NT, 6])
        mv2 = keep("mv2", [P, NT, 2])
        veps2 = keep("veps2", [P, NT])
        rstd2 = keep("rstd2", [P, NT])
        idle_p = keep("idle_p", [P, NH])
        idle_v = keep("idle_v", [P, 1])
        rinv = keep("rinv", [P, NT, NH])
        lg = keep("lg", [P, NT, NE])
        lge = keep("lge", [P, NT, NE])
        small = keep("small", [P, 4, NT])
        top8 = keep("top8", [P, NT, 8])
        idx8 = keep("idx8", [P, NT, 8], U32)
        (qhl, khl), e1 = share(("qhl", [P, 2, 2, T], F32R), ("khl", [P, 2, 2, T], F32R))
        (OT, On), e2 = share(("OT", [P, NG, T], F32), ("On", [P, NT, C], F32))
        cursor[0] = max(e1, e2)
        (xn2T,), _ = share(("xn2T", [P, 2, CC, T], F32R))
        (OnT,), e1 = share(("OnT", [P, 2, CC, T], F32R))
        cursor[0] = e1
        xn2 = xn
        hgT = keep("hgT", [P, T])
        (PT,), e1 = share(("PT", [P, 2, GH, 1280], F32))
        (sil, h32, h), e2 = share(("sil", [P, 2, T], F32), ("h32", [P, 2, T], F32), ("h", [P, NF, 2, T], F32R))
        assert 4 * T * (4 + 2 * FIRST_HALF) <= 4 * GH * 1280
        (st_qkv, st_out, st_gu, st_d, st_g1), e3 = share(
            ("st_qkv", [P, CC, 3 * C], F32), ("st_out", [P, CC, C], F32), ("st_gu", [P, CC, 2 * FF], I32),
            ("st_d", [P, NF, C], I32), ("st_g1", [P, CC, P], F32))
        cursor[0] = max(e1, e2, e3)
        print("sbuf", cursor[0], nc.sbuf_usable_end)
        PS = ctx.enter_context(nc.psum_tensor("PS", [P, 8, T], F32))

        def f(ap):
            return ap.bitcast(F32)

        w_in = sem("w_in"); w_ms = sem("w_ms"); w_zero = sem("w_zero"); w_hi = sem("w_hi"); w_done = sem("w_done")
        with nc.Block() as block:
            @block.sync
            def _(sp):
                sp.dma_start(st_qkv[:, :, :], wqkvT.rearrange("(c p) n -> p c n", p=P)).then_inc(w_in, 16)
                sp.dma_start(st_out[:, :, :], woutT.rearrange("(c p) n -> p c n", p=P)).then_inc(w_in, 16)
                sp.dma_start(st_g1[:, :, :], wg1.rearrange("(c p) n -> p c n", p=P)).then_inc(w_in, 16)
                sp.dma_start(ident[:, :], ident_c).then_inc(w_in, 16)
                sp.dma_start(st_gu[:, :, :], wguT.rearrange("(c p) n -> p c n", p=P)).then_inc(w_in, 16)
                sp.dma_start(st_d[:, :, :], wdT.rearrange("(c p) n -> p c n", p=P)).then_inc(w_in, 16)
                sp.dma_start(Wg2[:, :], wg2).then_inc(w_in, 16)
                sp.dma_start(bg1c[:, :], bg1).then_inc(w_in, 16)
                sp.dma_start(bg2b[:, :], bg2.partition_broadcast(P)).then_inc(w_in, 16)
                sp.wait_ge(w_in, 16 * 9)

            @block.gpsimd
            def _(pool):
                pool.memset(mask16[:, :], 0.0).then_inc(w_ms, 1)
                pool.memset(neghalf[:, :], -0.5)
                pool.memset(V[:, :, :, :], 1.0)
                pool.wait_ge(w_ms, 1)
                pool.affine_select(out=mask16[:, :], in_=mask16[:, :], compare_op=ALU.is_ge, fill=MASK, base=0,
                                   pattern=[[-1, P]], channel_multiplier=1).then_inc(w_ms, 1)

            @block.scalar
            def _(act):
                act.wait_ge(w_in, 16 * 9)
                for hi, src in ((Wqkv, st_qkv), (Wout, st_out), (Wg1, st_g1)):
                    act.activation(hi[:, HI, :, :], src[:, :, :], ACT.Copy).then_inc(w_hi, 1)
                act.activation(Wd[:, :, :], st_d[:, :, :], ACT.Copy)
                act.activation(ident16[:, :], ident[:, :], ACT.Copy).then_inc(w_done, 1)

            @block.vector
            def _(dve):
                dve.memset(zeros[:, :], 0.0)
                for stacked in (qs, ks):
                    dve.memset(f(stacked[32:64, :, :]), 0.0)
                    last = dve.memset(f(stacked[64:KS, :, :]), 0.0)
                last.then_inc(w_zero, 1)
                dve.wait_ge(w_zero, 1)
                dve.memset(f(ks[M0:M0 + 2, :, :]), 1.0)
                dve.wait_ge(w_in, 16 * 9)
                for n, (w, src) in enumerate(((Wqkv, st_qkv), (Wout, st_out), (Wg1, st_g1))):
                    dve.wait_ge(w_hi, n + 1)
                    dve.tensor_tensor(w[:, LO, :, :], src[:, :, :], f(w[:, HI, :, :]), ALU.subtract)
                dve.tensor_copy(Wgu[:, :, :], st_gu[:, :, :]).then_inc(w_done, 1)

        names = """x_in ln_var ln_std ln_done tx xnT_hi xnT_lo qk_ps qk_hi qk_lo v_ps v_sb
            gu_ps silu_sb h32_sb h_hi h_lo down_ps g_sb ln2_var ln2_std ln2_done t2 xn2T_hi xn2T_lo hg_ps hg_sb
            lg_ps lg_in lge_sb route_sb x1_out xn2_out xn2T_out xres_in unit maxed m_parts mt mrow_sb m_in st_ps
            exped masked pv ot_sb otr rinv_sb on_sb ont ont_hi ont_lo op y_sb x1_sb step slots_clear"""
        S = {n: sem("s_" + n) for n in names.split()}
        UNITS = ((3, (0, 1), 512), (3, (2, 3), 512), (2, (0, 1), 384), (2, (2, 3), 384),
                 (1, (0, 1, 2, 3), 256), (0, (0, 1, 2, 3), 128))
        NU = len(UNITS)
        BANK = (4, 6)
        PIECES = (((0, 0, 0),), ((1, 0, 512), (3, 384, 896)), ((2, 0, 1024),))
        WIDTH = (512, 512, 256)
        COL = {0: 0, 1: 512, 2: 1024, 3: 896}

        def scores_of_unit(slot, u):
            qt, heads, keys = UNITS[u]
            if keys > 256:
                return [PS[:, slot + n, 0:keys] for n in range(2)], PS[:, slot:slot + 2, 0:keys]
            if keys == 256:
                both = PS[:, slot:slot + 2, :].rearrange("p a (b k) -> p (a b) k", b=2)
                return [PS[:, slot + n // 2, 256 * (n % 2):256 * (n % 2) + 256] for n in range(4)], both
            return ([PS[:, slot, 128 * n:128 * n + 128] for n in range(4)],
                    PS[:, slot, :].rearrange("p (a k) -> p a k", a=4))

        S["mhi"] = sem("s_mhi")
        S["stack_in"] = [sem(f"s_stack_in{g}") for g in range(NG)]
        S["spilt"] = [sem(f"s_spilt{m}") for m in range(2)]
        STACKED = 16 * 7

        def up_to(b):
            return min(b, B) if isinstance(b, int) else b

        with nc.Block() as block:
            @block.sync
            def _(sp):
                def load_x(b):
                    at_least(sp, S["ln_done"], b)
                    sp.dma_start(xin[:, :, :], x[b].rearrange("(t p) d -> p t d", p=P)).then_inc(S["x_in"], 16)

                def spill(b):
                    for g in range(NG):
                        at_least(sp, S["stack_in"][g], STACKED * b)
                    for m, (src, n) in enumerate(((qhl, 0), (khl, 1), (qhl, 0), (khl, 1))):
                        sp.wait_ge(S["qk_lo"], 4 * b + m + 1)
                        sp.dma_start(qk_parts[n, m // 2], f(src[:, m // 2, :, :])).then_inc(S["spilt"][m // 2], 16)

                def stack(b, g):
                    at_least(sp, S["st_ps"], 48 * (b - 1) + 12 * (g + 1))
                    if g % 2 == 0:
                        sp.wait_ge(S["spilt"][g // 2], 32 * (b + 1))
                    sp.dma_start(f(qs[M0:M0 + 2, GH * g:GH * g + GH, :]),
                                 zeros[0:2, :].unsqueeze(1).to_broadcast([2, GH, T])).then_inc(S["stack_in"][g], 16)
                    for n, (dst, parts) in enumerate(((qs, Q_PARTS), (ks, K_PARTS))):
                        for blk, part in enumerate(parts):
                            sp.dma_start(
                                f(dst[HD * blk:HD * blk + HD, GH * g:GH * g + GH, :]),
                                qk_parts[n, g // 2, 64 * (g % 2):64 * (g % 2) + 64, part, :].rearrange(
                                    "(h d) t -> d h t", d=HD)).then_inc(S["stack_in"][g], 16)

                def store(b):
                    sp.wait_ge(S["x1_sb"], b + 1)
                    sp.dma_start(x1_rows[b].rearrange("(t p) d -> p t d", p=P), xres[:, :, :]
                                 ).then_inc(S["x1_out"], 16)
                    sp.wait_ge(S["ln2_done"], NT * (b + 1))
                    sp.dma_start(xn2_rows[b].rearrange("(t p) d -> p t d", p=P), xn2[:, :, :]
                                 ).then_inc(S["xn2_out"], 16)
                    sp.wait_ge(S["x1_out"], 16 * (b + 1))

                def store_T(b):
                    sp.wait_ge(S["xn2T_lo"], b + 1)
                    sp.dma_start(xn2T_parts[b], f(xn2T[:, :, :, :])).then_inc(S["xn2T_out"], 16)

                def load_res(b):
                    sp.dma_start(xres[:, :, :], x[b].rearrange("(t p) d -> p t d", p=P)).then_inc(S["xres_in"], 16)

                def rows_of_maxima(b, g):
                    sp.wait_ge(S["mrow_sb"], NG * b + g + 1)
                    for r in range(2):
                        sp.dma_start(f(qs[M0 + r:M0 + r + 1, GH * g:GH * g + GH, :]),
                                     mrow[GH * r:GH * r + GH, :]).then_inc(S["m_in"], 16)

                def clear_slots(b):
                    sp.dma_start(slots_in.rearrange("s d -> (s d)").rearrange(
                        "(b p r e) -> b p r e", b=B, p=P, e=ZW)[b], zeros[:, 0:ZW].unsqueeze(1).to_broadcast([P, NBLK * C // (B * ZW), ZW])
                        ).then_inc(S["slots_clear"], 16)

                def sequence(b, first=False, last=False):
                    if not last:
                        load_x(b + 1)
                    if not first:
                        store(b - 1)
                    load_res(b)
                    if not first:
                        store_T(b - 1)
                    if not last:
                        spill(b + 1)
                    clear_slots(b)
                    for g in range(NG + 1):
                        if g < NG:
                            rows_of_maxima(b, g)
                        if g > 0 and not last:
                            stack(b + 1, g - 1)

                load_x(0)
                spill(0)
                for g in range(NG):
                    stack(0, g)
                sequence(0, first=True)
                with sp.Fori(1, B - 1) as b:
                    sequence(b)
                sequence(B - 1, last=True)
                store(B - 1)
                store_T(B - 1)
                for n in ("x1_out", "xn2_out", "xn2T_out", "slots_clear"):
                    sp.wait_ge(S[n], 16 * B)

            @block.tensor
            def _(pe):
                def split_products(out, lhs, rhs, chunks=CC, pairs=PAIRS):
                    n, last = len(pairs) * chunks, None
                    for c in range(chunks):
                        for i, j in pairs:
                            n -= 1
                            last = pe.matmul(out, lhs(i, c), rhs(j, c), start=last is None, stop=n == 0)
                    return last

                def transposed_x(b):
                    pe.wait_ge(S["ln_done"], NT * (b + 1))
                    at_least(pe, S["h32_sb"], NF * b)
                    for c in range(CC):
                        for t in range(NT):
                            last = pe.transpose(PS[:, 4 + c, P * t:P * t + P], xn[:, t, P * c:P * c + P], ident[:, :])
                    last.then_inc(S["tx"], 1)

                def project_qk(b):
                    for m in range(4):
                        if m == 0:
                            pe.wait_ge(S["xnT_hi"], b + 1)
                            pe.wait_ge(S["xnT_lo"], b + 1)
                            at_least(pe, S["g_sb"], 2 * b)
                        if m >= 2:
                            pe.wait_ge(S["qk_lo"], 4 * b + m - 1)
                        o = C * (m % 2) + P * (m // 2)
                        split_products(PS[:, m % 2, :],
                                       lambda i, c: Wqkv[:, i, c, o:o + P],
                                       lambda j, c: xnT[:, j, c, :]).then_inc(S["qk_ps"], 1)

                def project_v(b):
                    at_least(pe, S["ot_sb"], NG * b)
                    for t in range(NT):
                        last = split_products(PS[:, 6 + t // 2, C * (t % 2):C * (t % 2) + C],
                                              lambda i, c: xnT[:, i, c, P * t:P * t + P],
                                              lambda j, c: Wqkv[:, j, c, 2 * C:3 * C])
                        if t % 2:
                            last.then_inc(S["v_ps"], 1)

                def gate_up(b, tiles):
                    for i in tiles:
                        bank = BANK[i % 2]
                        if i == 0:
                            at_least(pe, S["exped"], 48 * b)
                            pe.wait_ge(S["xnT_hi"], b + 1)
                            pe.wait_ge(S["xnT_lo"], b + 1)
                        elif i == 1:
                            pe.wait_ge(S["v_sb"], 2 * (b + 1))
                        else:
                            pe.wait_ge(S["h32_sb"], NF * b + i - 1)
                        for half in range(2):
                            o = FF * half + P * i
                            last = split_products(PS[:, bank + half, :],
                                                  lambda i_, c: Wgu[:, c, o:o + P],
                                                  lambda j, c: xnT[:, j, c, :], pairs=((HI, HI), (HI, LO)))
                            last.then_inc(S["gu_ps"], 1)

                def down(b, last):
                    for t in range(NT):
                        if t == 2 and not last:
                            transposed_x(b + 1)
                        if t == 0:
                            at_least(pe, S["ont_lo"], b)
                            if isinstance(b, int) and b == 0:
                                pe.wait_ge(S["qk_lo"], 4)
                        for i in range(NF):
                            if t == 0:
                                pe.wait_ge(S["h_hi"], NF * b + i + 1)
                                pe.wait_ge(S["h_lo"], NF * b + i + 1)
                            for part in (HI, LO):
                                ins = pe.matmul(PS[:, t // 2, C * (t % 2):C * (t % 2) + C],
                                                 h[:, i, part, P * t:P * t + P], Wd[:, i, :],
                                                 start=(i == 0 and part == HI), stop=(i == NF - 1 and part == LO))
                        if t % 2:
                            ins.then_inc(S["down_ps"], 1)

                def route_transposes(b):
                    pe.wait_ge(S["ln2_done"], NT * (b + 1))
                    pe.wait_ge(S["y_sb"], 2 * (b + 1))
                    for c in range(CC):
                        for t in range(NT):
                            last = pe.transpose(PS[:, 2 + c, P * t:P * t + P], xn2[:, t, P * c:P * c + P],
                                                ident[:, :])
                    last.then_inc(S["t2"], 1)

                def route_hidden(b, mlps):
                    pe.wait_ge(S["xn2T_lo"], b + 1)
                    pe.wait_ge(S["h32_sb"], NF * mlps)
                    split_products(PS[:, 6, :], lambda i, c: Wg1[:, i, c, :],
                                   lambda j, c: xn2T[:, j, c, :]).then_inc(S["hg_ps"], 1)

                def route_logits(b):
                    pe.wait_ge(S["hg_sb"], b + 1)
                    for t in range(NT):
                        last = pe.matmul(PS[:, 7, 32 * t:32 * t + NE], hgT[0:HG, P * t:P * t + P], Wg2[:, :],
                                         start=True, stop=True)
                    last.then_inc(S["lg_ps"], 1)

                def unit(b, g, u):
                    slot = 2 * (((NU + 1) * g + u) % 2)
                    if u == 0:
                        pe.wait_ge(S["stack_in"][g], STACKED * (b + 1))
                    if u == 0 and g == 0:
                        pe.wait_ge(S["qk_lo"], 4 * up_to(b + 2))
                        pe.wait_ge(S["g_sb"], 2 * (b + 1))
                    elif u == 1 or (u == 0 and g > 0):
                        if g > 0:
                            if u == 1:
                                pe.wait_ge(S["mrow_sb"], NG * b + g)
                            else:
                                pe.wait_ge(S["maxed"], NU * (NG * b + g))
                    else:
                        pe.wait_ge(S["maxed"], NU * (NG * b + g) + u - 1)
                    qt, heads, keys = UNITS[u]
                    places, _ = scores_of_unit(slot, u)
                    for j, out in zip(heads, places):
                        hd = GH * g + j
                        pe.matmul(out, qs[:, hd, P * qt:P * qt + P], ks[:, hd, 0:keys], start=True, stop=False)
                        last = pe.matmul(out[:, keys - P:keys], ident16[:, :], mask16[:, :], start=False, stop=True)
                    last.then_inc(S["unit"], 1)

                def maxima_as_rows(b, g):
                    slot = 2 * (((NU + 1) * g + NU) % 2)
                    pe.wait_ge(S["m_parts"], NG * b + g + 1)
                    for qt in range(NT):
                        last = pe.matmul(PS[0:2 * GH, slot, P * qt:P * qt + P],
                                         Mparts[:, qt, :, :].rearrange("p r j -> p (r j)"), ident[:, :],
                                         start=True, stop=True)
                    last.then_inc(S["mt"], 1)

                def transposed_scores(b, g, j):
                    hd = GH * g + j
                    if hd == 0:
                        pe.wait_ge(S["xnT_lo"], up_to(b + 2))
                        pe.wait_ge(S["h32_sb"], NF * (b + 1))
                        at_least(pe, S["hg_sb"], b)
                    if j == 0:
                        pe.wait_ge(S["m_in"], 32 * (NG * b + g + 1))
                    for n, piece in enumerate(PIECES):
                        if hd > 0:
                            pe.wait_ge(S["exped"], 48 * b + 3 * (hd - 1) + n + 1)
                        for kt, col, _ in piece:
                            last = pe.matmul(PS[:, 4 + n, col:col + T - P * kt], ks[:, hd, P * kt:P * kt + P],
                                             qs[:, hd, P * kt:T], start=True, stop=True)
                        last.then_inc(S["st_ps"], 1)

                def values(b, g):
                    at_least(pe, S["ot_sb"], NG * b + g)
                    if g == 0:
                        at_least(pe, S["route_sb"], b)
                    pe.wait_ge(S["exped"], 48 * b + 12 * (g + 1))
                    pe.wait_ge(S["masked"], 16 * b + 4 * (g + 1))
                    for kt in range(NT):
                        for j in range(GH):
                            last = pe.matmul(PS[32 * j:32 * j + 32, 7, P * kt:T], V[:, kt, GH * g + j, :],
                                             PT[:, g % 2, j, COL[kt]:COL[kt] + T - P * kt],
                                             start=kt == 0, stop=kt == NT - 1)
                    last.then_inc(S["pv"], 1)

                def attention(b, last):
                    for s in range(NG + 2):
                        if s == NG + 1 and not last:
                            gate_up(b + 1, (0,))
                        for u in range(NU + 1):
                            if s < NG and u < NU:
                                unit(b, s, u)
                            if u == 1 and 2 <= s:
                                values(b, s - 2)
                            if 1 <= s <= NG and u in (1, 2, 4, 5):
                                transposed_scores(b, s - 1, (1, 2, 4, 5).index(u))
                        if s < NG:
                            maxima_as_rows(b, s)

                def heads_as_rows(b):
                    for qt in range(NT):
                        if qt == 0:
                            pe.wait_ge(S["ot_sb"], NG * (b + 1))
                            pe.wait_ge(S["mrow_sb"], NG * (b + 1))
                        for g in range(NG):
                            last = pe.transpose(PS[:, qt, P * g:P * g + P], OT[:, g, P * qt:P * qt + P], ident[:, :])
                        last.then_inc(S["otr"], 1)

                def output_transposes(b):
                    pe.wait_ge(S["on_sb"], NT * (b + 1))
                    for c in range(CC):
                        for t in range(NT):
                            last = pe.transpose(PS[:, c, P * t:P * t + P], On[:, t, P * c:P * c + P], ident[:, :])
                    last.then_inc(S["ont"], 1)

                def project_out(b):
                    pe.wait_ge(S["ont_hi"], b + 1)
                    pe.wait_ge(S["ont_lo"], b + 1)
                    for t in range(NT):
                        last = split_products(PS[:, 2 + t // 2, C * (t % 2):C * (t % 2) + C],
                                              lambda i, c: OnT[:, i, c, P * t:P * t + P],
                                              lambda j, c: Wout[:, j, c, :])
                        if t % 2:
                            last.then_inc(S["op"], 1)

                def sequence(b, first=False, last=False):
                    gate_up(b, range(EARLY, NF))
                    if not first:
                        route_transposes(b - 1)
                    down(b, last)
                    if not first:
                        route_hidden(b - 1, b + 1)
                    if not last:
                        project_qk(b + 1)
                    if not first:
                        route_logits(b - 1)
                    attention(b, last)
                    heads_as_rows(b)
                    if not last:
                        project_v(b + 1)
                    output_transposes(b)
                    if not last:
                        gate_up(b + 1, (1,))
                    project_out(b)

                transposed_x(0)
                project_qk(0)
                gate_up(0, (0,))
                project_v(0)
                gate_up(0, (1,))
                sequence(0, first=True)
                with pe.Fori(1, B - 1) as b:
                    sequence(b)
                sequence(B - 1, last=True)
                route_transposes(B - 1)
                route_hidden(B - 1, B)
                route_logits(B - 1)

            @block.scalar
            def _(act):
                def split_x(b):
                    act.wait_ge(S["tx"], b + 1)
                    at_least(act, S["gu_ps"], 2 * NF * b)
                    act.activation(xnT[:, HI, :, :], PS[:, 4:6, :], ACT.Copy).then_inc(S["xnT_hi"], 1)

                def split_qk(b):
                    for m in range(4):
                        if m == 0:
                            at_least(act, S["on_sb"], NT * (b - 1))
                            at_least(act, S["ont"], b - 1)
                        act.wait_ge(S["qk_ps"], 4 * b + m + 1)
                        dst = khl if m % 2 else qhl
                        act.activation(dst[:, m // 2, HI, :], PS[:, m % 2, :], ACT.Copy).then_inc(S["qk_hi"], 1)

                def keep_v(b):
                    for n in range(2):
                        act.wait_ge(S["v_ps"], 2 * b + n + 1)
                        if n == 0:
                            at_least(act, S["pv"], NG * b)
                        act.activation(V[:, 2 * n:2 * n + 2, :, 0:HD].rearrange("p t h d -> p (t h) d"),
                                       PS[:, 6 + n, :].rearrange("p (x d) -> p x d", d=HD), ACT.Copy
                                       ).then_inc(S["v_sb"], 1)

                def silu_of_gate(b, i):
                    act.wait_ge(S["gu_ps"], 2 * NF * b + 2 * i + 1)
                    if i == 0:
                        at_least(act, S["pv"], NG * b - 1)
                    if i == FIRST_HALF:
                        at_least(act, S["pv"], NG * b)
                    if i >= 2:
                        act.wait_ge(S["h32_sb"], NF * b + i - 1)
                    act.activation(sil[:, i % 2, :], PS[:, BANK[i % 2], :], ACT.Silu, scale=QSCALE
                                   ).then_inc(S["silu_sb"], 1)

                def hidden(b, i):
                    act.wait_ge(S["h32_sb"], NF * b + i + 1)
                    if i == 0:
                        at_least(act, S["down_ps"], 2 * b)
                    act.activation(h[:, i, HI, :], h32[:, i % 2, :], ACT.Copy).then_inc(S["h_hi"], 1)

                def gate_of_output(b, last):
                    for n in range(2):
                        if n == 1 and not last:
                            split_x(b + 1)
                        act.wait_ge(S["down_ps"], 2 * b + n + 1)
                        if n == 0:
                            at_least(act, S["y_sb"], 2 * b)
                        act.activation(G[:, 2 * n:2 * n + 2, :].rearrange("p t e -> p (t e)"), PS[:, n, :],
                                       ACT.Silu, scale=QSCALE).then_inc(S["g_sb"], 1)

                def split_x1(b):
                    act.wait_ge(S["t2"], b + 1)
                    act.wait_ge(S["op"], 2 * (b + 1))
                    act.activation(xn2T[:, HI, :, :], PS[:, 2:4, :], ACT.Copy).then_inc(S["xn2T_hi"], 1)

                def route_hidden(b):
                    act.wait_ge(S["hg_ps"], b + 1)
                    act.activation(hgT[:, :], PS[:, 6, :], ACT.Gelu, bias=bg1c[:, 0:1]).then_inc(S["hg_sb"], 1)

                def route_exps(b):
                    act.wait_ge(S["lg_in"], b + 1)
                    act.activation(lge[:, :, :], lg[:, :, :], ACT.Exp).then_inc(S["lge_sb"], 1)

                def exps(b, g, j):
                    if j == 0 and g >= 2:
                        act.wait_ge(S["pv"], NG * b + g - 1)
                    if g == 0 and j == 0:
                        at_least(act, S["pv"], NG * b)
                        act.wait_ge(S["down_ps"], 2 * (b + 1))
                    hd = GH * g + j
                    for n, width in enumerate(WIDTH):
                        act.wait_ge(S["st_ps"], 48 * b + 3 * hd + n + 1)
                        act.activation(PT[:, g % 2, j, 512 * n:512 * n + width], PS[:, 4 + n, 0:width], ACT.Exp,
                                       scale=SCALE).then_inc(S["exped"], 1)

                def keep_heads(b, g):
                    act.wait_ge(S["pv"], NG * b + g + 1)
                    if g == 0:
                        for half in S["spilt"]:
                            act.wait_ge(half, 32 * up_to(b + 2))
                    act.activation(OT[:, g, :], PS[:, 7, :], ACT.Copy).then_inc(S["ot_sb"], 1)

                def attention(b, first, last):
                    if not first:
                        route_exps(b - 1)
                    for s in range(1, NG + 2):
                        if s == NG + 1 and not last:
                            silu_of_gate(b + 1, 0)
                        for j in range(GH):
                            if s <= NG:
                                exps(b, s - 1, j)
                            if j == 1 and s >= 2:
                                keep_heads(b, s - 2)

                def split_output(b):
                    act.wait_ge(S["ont"], b + 1)
                    at_least(act, S["xn2T_out"], 16 * b)
                    at_least(act, S["hg_ps"], b)
                    act.activation(OnT[:, HI, :, :], PS[:, 0:2, :], ACT.Copy).then_inc(S["ont_hi"], 1)

                def sequence(b, first=False, last=False):
                    for i in range(EARLY, NF):
                        silu_of_gate(b, i)
                        hidden(b, i)
                    if not first:
                        split_x1(b - 1)
                    gate_of_output(b, last)
                    if not first:
                        route_hidden(b - 1)
                    if not last:
                        split_qk(b + 1)
                    attention(b, first, last)
                    if not last:
                        hidden(b + 1, 0)
                        keep_v(b + 1)
                    split_output(b)
                    if not last:
                        silu_of_gate(b + 1, 1)
                        hidden(b + 1, 1)

                split_x(0)
                split_qk(0)
                silu_of_gate(0, 0)
                hidden(0, 0)
                keep_v(0)
                silu_of_gate(0, 1)
                hidden(0, 1)
                sequence(0, first=True)
                with act.Fori(1, B - 1) as b:
                    sequence(b)
                sequence(B - 1, last=True)
                split_x1(B - 1)
                route_hidden(B - 1)
                route_exps(B - 1)

            @block.vector
            def _(dve):
                steps = {"made": 0}

                NORM_X = (xin, stats, mv, veps, rstd, xn, "ln_var", "ln_std", "ln_done")
                NORM_X1 = (xres, stats2, mv2, veps2, rstd2, xn2, "ln2_var", "ln2_std", "ln2_done")

                def norm_stats(b, norm):
                    src, st, _, _, _, _, var_sem, _, _ = norm
                    if norm is NORM_X:
                        dve.wait_ge(S["x_in"], 16 * (b + 1))
                    else:
                        dve.wait_ge(S["x1_sb"], b + 1)
                    for t in range(NT):
                        last = dve.bn_stats(st[:, t, :], src[:, t, :])
                    last.then_inc(S[var_sem], 1)

                def norm_variance(b, norm):
                    _, st, m_, ve, _, _, var_sem, _, _ = norm
                    dve.wait_ge(S[var_sem], 3 * b + 1)
                    dve.memset(idle_v[:, :], 0.0)
                    for t in range(NT):
                        last = dve.bn_aggr(m_[:, t, :], st[:, t, :])
                    last.then_inc(S[var_sem], 1)
                    dve.wait_ge(S[var_sem], 3 * b + 2)
                    dve.tensor_scalar(ve[:, :], m_[:, :, 1], EPS, None, ALU.add).then_inc(S[var_sem], 1)

                def norm_rows(b, norm):
                    src, _, m_, _, rs, dst, _, std_sem, done_sem = norm
                    if norm is NORM_X:
                        at_least(dve, S["tx"], b)
                        at_least(dve, S["t2"], b - 1)
                        at_least(dve, S["xn2_out"], 16 * (b - 1))
                    else:
                        dve.wait_ge(S["tx"], b + 2 if not isinstance(b, int) else min(b + 2, B))
                    dve.wait_ge(S[std_sem], b + 1)
                    for t in range(NT):
                        dve.tensor_scalar(dst[:, t, :], src[:, t, :], m_[:, t, 0:1], rs[:, t:t + 1],
                                          ALU.subtract, ALU.mult).then_inc(S[done_sem], 1)

                def norm(b, which):
                    norm_stats(b, which)
                    norm_variance(b, which)
                    norm_rows(b, which)

                def split_x(b):
                    dve.wait_ge(S["xnT_hi"], b + 1)
                    dve.tensor_tensor(xnT[:, LO, :, :], PS[:, 4:6, :], f(xnT[:, HI, :, :]), ALU.subtract
                                      ).then_inc(S["xnT_lo"], 1)

                def split_qk(b):
                    for m in range(4):
                        dve.wait_ge(S["qk_hi"], 4 * b + m + 1)
                        dst = khl if m % 2 else qhl
                        dve.tensor_tensor(dst[:, m // 2, LO, :], PS[:, m % 2, :], f(dst[:, m // 2, HI, :]),
                                          ALU.subtract).then_inc(S["qk_lo"], 1)

                def gated(b, i):
                    dve.wait_ge(S["gu_ps"], 2 * NF * b + 2 * i + 2)
                    dve.wait_ge(S["silu_sb"], NF * b + i + 1)
                    if i >= 2:
                        dve.wait_ge(S["h_hi"], NF * b + i - 1)
                        dve.wait_ge(S["h_lo"], NF * b + i - 1)
                    dve.scalar_tensor_tensor(out=h32[:, i % 2, :], in0=PS[:, BANK[i % 2] + 1, :], scalar=QSCALE,
                                             in1=sil[:, i % 2, :], op0=ALU.mult, op1=ALU.mult
                                             ).then_inc(S["h32_sb"], 1)

                ROUTE_STEPS = 9

                def route_step(b, n, ins, wait=True):
                    ins.then_inc(S["step"], 1)
                    if wait:
                        dve.wait_ge(S["step"], ROUTE_STEPS * b + n)

                def route_logits(b):
                    dve.wait_ge(S["lg_ps"], b + 1)
                    logits = PS[:, 7, 0:P].rearrange("p (t e) -> p t e", t=NT)[:, :, 0:NE]
                    route_step(b, 1, dve.tensor_tensor(
                        lg[:, :, :], logits, bg2b[:, :].unsqueeze(1).to_broadcast([P, NT, NE]), ALU.add))
                    route_step(b, 2, dve.tensor_reduce(out=small[:, 0, :], in_=lg[:, :, :], op=ALU.max, axis=AX.X))
                    dve.tensor_tensor(lg[:, :, :], lg[:, :, :],
                                      small[:, 0, :].unsqueeze(2).to_broadcast([P, NT, NE]),
                                      ALU.subtract).then_inc(S["lg_in"], 1)

                def route_choice(b):
                    dve.wait_ge(S["lge_sb"], b + 1)
                    route_step(b, 3, dve.tensor_reduce(out=small[:, 1, :], in_=lge[:, :, :], op=ALU.add, axis=AX.X))
                    route_step(b, 4, dve.reciprocal(small[:, 2, :], small[:, 1, :]))
                    route_step(b, 5, dve.tensor_tensor(lg[:, :, :], lge[:, :, :],
                                                       small[:, 2, :].unsqueeze(2).to_broadcast([P, NT, NE]), ALU.mult))
                    dve.memset(idle_v[:, :], 0.0)
                    for t in range(NT):
                        last = dve.max(out=top8[:, t, :], in_=lg[:, t, :])
                    route_step(b, 6, last)
                    dve.memset(idle_v[:, :], 0.0)
                    for t in range(NT):
                        last = dve.max_index(out=idx8[:, t, :], in_max=top8[:, t, :], in_values=lg[:, t, :])
                    route_step(b, 7, last)
                    route_step(b, 8, dve.tensor_copy(gates[:, bass.ds(NT * b, NT), :], top8[:, :, 0:TOPK]), wait=False)
                    route_step(b, 9, dve.tensor_copy(chosen[:, bass.ds(NT * b, NT), :], idx8[:, :, 0:TOPK]))
                    dve.tensor_copy(small[:, 3, :], small[:, 2, :]).then_inc(S["route_sb"], 1)

                def maxima(b, g, u):
                    slot = 2 * (((NU + 1) * g + u) % 2)
                    qt, heads, keys = UNITS[u]
                    dve.wait_ge(S["unit"], NU * (NG * b + g) + u + 1)
                    if u == 0 and not (isinstance(b, int) and b == 0 and g == 0):
                        dve.wait_ge(S["m_parts"], NG * b + g)
                    _, all_of = scores_of_unit(slot, u)
                    dve.tensor_reduce(out=Mneg[:, 0, qt, heads[0]:heads[-1] + 1], in_=all_of, op=ALU.max, axis=AX.X,
                                      negate=True).then_inc(S["maxed"], 1)

                def parts_of_maxima(b, g):
                    dve.wait_ge(S["maxed"], NU * (NG * b + g + 1))
                    at_least(dve, S["mt"], NG * b + g)
                    dve.tensor_copy(Mhi[:, :, :], Mneg[:, 0, :, :]).then_inc(S["mhi"], 1)
                    dve.wait_ge(S["mhi"], NG * b + g + 1)
                    dve.tensor_copy(Mparts[:, :, HI, :], f(Mhi[:, :, :]))
                    dve.tensor_tensor(Mparts[:, :, LO, :], Mneg[:, 0, :, :], f(Mhi[:, :, :]), ALU.subtract
                                      ).then_inc(S["m_parts"], 1)

                def rows_of_maxima(b, g):
                    slot = 2 * (((NU + 1) * g + NU) % 2)
                    dve.wait_ge(S["mt"], NG * b + g + 1)
                    at_least(dve, S["m_in"], 32 * (NG * b + g))
                    dve.tensor_copy(mrow[:, :], PS[0:2 * GH, slot, :]).then_inc(S["mrow_sb"], 1)

                def attention(b, first):
                    for g in range(NG):
                        for u in range(NU):
                            maxima(b, g, u)
                            if g == 0 and u == 1 and not first:
                                route_logits(b - 1)
                        parts_of_maxima(b, g)
                        rows_of_maxima(b, g)
                        if g == 1 and not first:
                            route_choice(b - 1)

                def normed_heads(b):
                    for qt in range(NT):
                        dve.wait_ge(S["otr"], NT * b + qt + 1)
                        if qt == 0:
                            for half in S["spilt"]:
                                dve.wait_ge(half, 32 * up_to(b + 2))
                        heads = PS[:, qt, :].rearrange("p (h x) -> p h x", x=2 * HD)
                        dve.reciprocal(rinv[:, qt, :], heads[:, :, HD]).then_inc(S["rinv_sb"], 1)
                        dve.wait_ge(S["rinv_sb"], NT * b + qt + 1)
                        dve.tensor_tensor(On[:, qt, :].rearrange("p (h d) -> p h d", d=HD), heads[:, :, 0:HD],
                                          rinv[:, qt, :].unsqueeze(2).to_broadcast([P, NH, HD]), ALU.mult
                                          ).then_inc(S["on_sb"], 1)

                def split_output(b):
                    dve.wait_ge(S["ont_hi"], b + 1)
                    dve.tensor_tensor(OnT[:, LO, :, :], PS[:, 0:2, :], f(OnT[:, HI, :, :]), ALU.subtract
                                      ).then_inc(S["ont_lo"], 1)

                def residual(b):
                    for n in range(2):
                        dve.wait_ge(S["op"], 2 * b + n + 1)
                        dve.wait_ge(S["g_sb"], 2 * b + n + 1)
                        part = G[:, 2 * n:2 * n + 2, :].rearrange("p t e -> p (t e)")
                        dve.tensor_tensor(part, PS[:, 2 + n, :], part, ALU.mult).then_inc(S["y_sb"], 1)
                    dve.wait_ge(S["y_sb"], 2 * (b + 1))
                    dve.wait_ge(S["xres_in"], 16 * (b + 1))
                    dve.tensor_tensor(xres[:, :, :], xres[:, :, :], G[:, :, :], ALU.add).then_inc(S["x1_sb"], 1)

                def sequence(b, first=False, last=False):
                    gated(b, 2)
                    if not first:
                        norm_stats(b - 1, NORM_X1)
                    gated(b, 3)
                    if not first:
                        norm_variance(b - 1, NORM_X1)
                    if not last:
                        norm_stats(b + 1, NORM_X)
                    gated(b, 4)
                    if not first:
                        norm_rows(b - 1, NORM_X1)
                    if not last:
                        norm_variance(b + 1, NORM_X)
                    gated(b, 5)
                    if not last:
                        norm_rows(b + 1, NORM_X)
                    if not first:
                        split_x1(b - 1)
                    if not last:
                        split_x(b + 1)
                        split_qk(b + 1)
                    attention(b, first)
                    if not last:
                        gated(b + 1, 0)
                    normed_heads(b)
                    split_output(b)
                    if not last:
                        gated(b + 1, 1)
                    residual(b)

                def split_x1(b):
                    dve.wait_ge(S["xn2T_hi"], b + 1)
                    dve.tensor_tensor(xn2T[:, LO, :, :], PS[:, 2:4, :], f(xn2T[:, HI, :, :]), ALU.subtract
                                      ).then_inc(S["xn2T_lo"], 1)

                norm(0, NORM_X)
                split_x(0)
                split_qk(0)
                gated(0, 0)
                gated(0, 1)
                sequence(0, first=True)
                with dve.Fori(1, B - 1) as b:
                    sequence(b)
                sequence(B - 1, last=True)
                norm(B - 1, NORM_X1)
                split_x1(B - 1)
                route_logits(B - 1)
                route_choice(B - 1)

            @block.gpsimd
            def _(pool):
                def power(b, ve, rs, var_sem, std_sem):
                    pool.wait_ge(S[var_sem], 3 * b + 3)
                    pool.tensor_tensor(rs[:, :], ve[:, :], neghalf[:, :], ALU.pow).then_inc(S[std_sem], 1)

                def hidden_low(b, i):
                    pool.wait_ge(S["h_hi"], NF * b + i + 1)
                    pool.tensor_tensor(h[:, i, LO, :], h32[:, i % 2, :], f(h[:, i, HI, :]), ALU.subtract
                                       ).then_inc(S["h_lo"], 1)

                def masks(b):
                    for g in range(NG):
                        for j in range(GH):
                            pool.wait_ge(S["exped"], 48 * b + 3 * (GH * g + j + 1))
                            pool.tensor_tensor(idle_p[:, GH * g + j:GH * g + j + 1], neghalf[:, 0:1], neghalf[:, 0:1], ALU.mult)
                            p = PT[:, g % 2, j, :]
                            first = p[:, 0:1024].rearrange("p (a k) -> p a k", a=2)[:, :, 0:P]
                            second = p[:, 896:896 + 2 * P].rearrange("p (a k) -> p a k", a=2)
                            for blocks in (first, second):
                                last = pool.affine_select(out=blocks, in_=blocks, compare_op=ALU.is_ge, fill=0.0,
                                                          base=0, pattern=[[0, 2], [1, P]], channel_multiplier=-1)
                            last.then_inc(S["masked"], 1)

                def sequence(b, first=False, last=False):
                    hidden_low(b, 2)
                    hidden_low(b, 3)
                    if not first:
                        power(b - 1, veps2, rstd2, "ln2_var", "ln2_std")
                    hidden_low(b, 4)
                    if not last:
                        power(b + 1, veps, rstd, "ln_var", "ln_std")
                    hidden_low(b, 5)
                    masks(b)
                    if not last:
                        hidden_low(b + 1, 0)
                        hidden_low(b + 1, 1)

                power(0, veps, rstd, "ln_var", "ln_std")
                hidden_low(0, 0)
                hidden_low(0, 1)
                sequence(0, first=True)
                with pool.Fori(1, B - 1) as b:
                    sequence(b)
                sequence(B - 1, last=True)
                power(B - 1, veps2, rstd2, "ln2_var", "ln2_std")

        cursor[0] = first_free
        pos = keep("pos", [P, B, NT, TOPK], U32)
        block_expert = keep("block_expert", [P, NBLK], I32)
        idle_q = keep("idle_q", [P, 4])
        ramp_col = ident[:, 0:1]
        s2_at = cursor[0]
        s2 = keep("s2", [P, B * NT, C])
        after_shared = cursor[0]
        slotcnt = keep("slotcnt", [P, NBLK])
        Fwd = keep("Fwd", [P, 2, 2, FQ], F32R)
        Inv = keep("Inv", [P, 2, NQ, FQ], F32R)
        HA = keep("HA", [P, 2, 2, C])
        HB = keep("HB", [P, 2, 2, C])
        HN = keep("HN", [P, 2, 2, C])
        Win = keep("Win", [P, 2, CC, 2 * C], F32R)
        Wo2 = keep("Wo2", [P, 2, CC, C], F32R)
        bo2b = keep("bo2b", [P, C])
        binc = keep("binc", [P, 4])
        shortc = keep("shortc", [P, CC, 4])
        xT = keep("xT", [P, 2, CC, T], F32R)
        vt = keep("vt", [P, CC, T + 2])
        cv = keep("cv", [P, 2, CC, T])
        v2 = keep("v2", [P, 2, NT, C], F32R)
        Vf = keep("Vf", [P, 2, NQ, C])
        tmp = keep("tmp", [P, 4, 2 * C])
        tmq = keep("tmq", [P, 4, 2 * C])
        Z = keep("Z", [P, 2, NQ, C])
        Zs = keep("Zs", [P, 2, 2, NQ, C], F32R)
        o32 = keep("o32", [P, CC, T])
        oTs = keep("oTs", [P, 2, CC, T], F32R)
        xrows = keep("xrows", [P, NT, C])
        posb = keep("posb", [P, NT, TOPK], U32)
        (st_f, st_i, st_win, st_wo), _ = share(("st_f", [P, 2, FQ], F32), ("st_i", [P, NQ, FQ], F32),
                                               ("st_win", [P, CC, 2 * C], F32), ("st_wo", [P, CC, C], F32))
        cursor[0] += size([P, 2, FQ], F32) + size([P, NQ, FQ], F32) + size([P, CC, 2 * C], F32) + size([P, CC, C], F32)
        fw1s = keep("fw1s", [1, 64]); posr = keep("posr", [1, T]); fb1c = keep("fb1c", [64, 1])
        fw2s = keep("fw2s", [64, P]); fb2c = keep("fb2c", [P, 1]); fw3s = keep("fw3s", [P, C])
        fb3b = keep("fb3b", [P, C]); h1s = keep("h1s", [64, T]); h2s = keep("h2s", [P, T])
        print("sbuf 2", cursor[0], nc.sbuf_usable_end)
        cursor_after = cursor[0]
        cursor[0] = cursor[0] - cursor[0] % 32
        ramp = nc.alloc_sbuf_tensor_at("ramp", [P, P], F32, offset=s2_at)
        q = {}
        off = s2_at + 512

        def over_s2(name, shape, dt=F32):
            nonlocal off
            t = nc.alloc_sbuf_tensor_at(name, shape, dt, offset=off)
            off += size(shape, dt)
            return t

        before = over_s2("before", [P, P])
        ones = over_s2("ones", [P, P])
        chf = over_s2("chf", [P, B * NT, TOPK])
        per = over_s2("per", [P, 12, NE])
        peri = over_s2("peri", [P, 2, NE], I32)
        NTT = B * NT
        onehot = [nc.alloc_sbuf_tensor_at(f"onehot{k}", [P, NTT, NE], F32, offset=off + 2560 * k) for k in range(2)]
        cnt = nc.alloc_sbuf_tensor_at("cnt", [P, NTT, NE], F32, offset=off + 5120)
        tots = [nc.alloc_sbuf_tensor_at(f"tots{k}", [P, NTT, NE], F32, offset=off + 7680 + 2560 * k) for k in range(3)]
        slot = nc.alloc_sbuf_tensor_at("slot", [P, NTT, NE], F32, offset=off + 15360)
        slotf = nc.alloc_sbuf_tensor_at("slotf", [P, NTT, TOPK], F32, offset=off + 17920)
        be_cmp = nc.alloc_sbuf_tensor_at("be_cmp", [P, NBLK, NE], F32, offset=off + 18432)
        assert off + 18432 + NBLK * NE * 4 <= after_shared, (off, after_shared)

        r_in = sem("r_in"); r_pool = sem("r_pool"); r_dve = sem("r_dve"); r_ps = sem("r_ps"); r_hi = sem("r_hi")
        t_hi = sem("t_hi"); t_lo = sem("t_lo"); t_in = sem("t_in"); f_ps = sem("f_ps"); f_sb = sem("f_sb")
        f_hi = sem("f_hi"); f_lo = sem("f_lo"); h_sb = sem("h_sb"); f_cf = sem("f_cf")

        def transform(pe, src, bank, done):
            for half in range(2):
                for q_ in range(NQ):
                    n = 0
                    for kc in range(2):
                        for i, j in PAIRS:
                            last = pe.matmul(PS[:, bank + 2 * half + q_ // 2, C * (q_ % 2):C * (q_ % 2) + C],
                                             Fwd[:, i, kc, P * q_:P * q_ + P], src[:, j, 2 * half + kc, :],
                                             start=n == 0, stop=n == 5)
                            n += 1
                    if q_ % 2:
                        last.then_inc(done, 1)

        with nc.Block() as block:
            @block.sync
            def _(sp):
                sp.dma_start(ramp[:, :], ramp_c.partition_broadcast(P)).then_inc(r_in, 16)
                for dst, src in ((st_f[:, :, :], dft_c.rearrange("(c p) n -> p c n", p=P)),
                                 (st_i[:, :, :], idft_c.rearrange("(c p) n -> p c n", p=P)),
                                 (st_win[:, :, :], winT.rearrange("(c p) n -> p c n", p=P)),
                                 (st_wo[:, :, :], wo2.rearrange("(c p) n -> p c n", p=P)),
                                 (bo2b[:, :], bo2.partition_broadcast(P)), (binc[:, :], bin_),
                                 (shortc[:, :, :], short), (fw1s[:, :], fw1), (posr[:, :], pos_c),
                                 (fb1c[:, :], fb1), (fw2s[:, :], fw2), (fb2c[:, :], fb2), (fw3s[:, :], fw3),
                                 (fb3b[:, :], fb3.partition_broadcast(P))):
                    sp.dma_start(dst, src).then_inc(t_in, 16)

            @block.gpsimd
            def _(pool):
                pool.memset(ones[:, :], 1.0).then_inc(r_pool, 1)
                pool.wait_ge(r_pool, 1)
                pool.affine_select(out=before[:, :], in_=ones[:, :], compare_op=ALU.is_gt, fill=0.0, base=0,
                                   pattern=[[1, P]], channel_multiplier=-1).then_inc(r_pool, 1)
                pool.memset(vt[:, :, 0:1], 0.0)
                pool.memset(vt[:, :, T + 1:T + 2], 0.0)

            @block.scalar
            def _(act):
                act.wait_ge(t_in, 16 * 14)
                for hi, src in ((Fwd, st_f), (Inv, st_i), (Win, st_win), (Wo2, st_wo)):
                    act.activation(hi[:, HI, :, :], src[:, :, :], ACT.Copy).then_inc(t_hi, 1)
                act.wait_ge(f_ps, 1)
                act.activation(h1s[:, :], PS[0:64, 4, :], ACT.Gelu, bias=fb1c[:, 0:1]).then_inc(f_sb, 1)
                act.wait_ge(f_ps, 2)
                act.activation(h2s[:, :], PS[:, 5, :], ACT.Gelu, bias=fb2c[:, 0:1]).then_inc(f_sb, 1)
                act.wait_ge(f_cf, 1)
                act.activation(v2[:, HI, :, :], Z[:, 0, :, :], ACT.Copy).then_inc(f_hi, 1)
                for half in range(2):
                    act.wait_ge(f_ps, 4 + 2 * half)
                    act.activation(HA[:, half, :, :].rearrange("p a c -> p (a c)"), PS[:, 4 + 2 * half, :], ACT.Copy
                                   ).then_inc(h_sb, 1)
                    act.activation(HN[:, half, :, :].rearrange("p a c -> p (a c)"), PS[:, 4 + 2 * half, :], ACT.Copy
                                   ).then_inc(h_sb, 1)
                    act.wait_ge(f_ps, 5 + 2 * half)
                    act.activation(HB[:, half, :, :].rearrange("p a c -> p (a c)"), PS[:, 5 + 2 * half, :], ACT.Copy
                                   ).then_inc(h_sb, 1)

            @block.tensor
            def _(pe):
                pe.wait_ge(t_in, 16 * 14)
                pe.matmul(PS[0:64, 4, :], fw1s[:, :], posr[:, :], start=True, stop=True).then_inc(f_ps, 1)
                pe.wait_ge(f_sb, 1)
                pe.matmul(PS[:, 5, :], fw2s[:, :], h1s[:, :], start=True, stop=True).then_inc(f_ps, 1)
                pe.wait_ge(f_sb, 2)
                for t in range(NT):
                    last = pe.matmul(PS[:, 6 + t // 2, C * (t % 2):C * (t % 2) + C], h2s[:, P * t:P * t + P], fw3s[:, :],
                                     start=True, stop=True)
                last.then_inc(f_ps, 1)
                pe.wait_ge(r_pool, 2)
                pe.wait_ge(r_dve, 4)
                for n, lhs in enumerate((before, ones)):
                    for half in range(2):
                        last = pe.matmul(PS[:, 2 * n + half, 0:16 * NE], lhs[:, :],
                                         cnt[:, 16 * half:16 * half + 16, :].rearrange("p t e -> p (t e)"),
                                         start=True, stop=True)
                last.then_inc(r_ps, 1)
                pe.wait_ge(f_lo, 1)
                transform(pe, v2, 4, f_ps)

            @block.vector
            def _(dve):
                made = [0]

                def step(ins):
                    made[0] += 1
                    ins.then_inc(r_dve, 1)
                    dve.wait_ge(r_dve, made[0])

                def bc_e(ap, n):
                    return ap.unsqueeze(1).to_broadcast([P, n, NE])

                dve.wait_ge(r_in, 16)
                step(dve.tensor_copy(chf[:, :, :], chosen[:, :, :]))
                for k in range(TOPK):
                    step(dve.tensor_tensor(onehot[k][:, :, :], bc_e(ramp[:, 0:NE], NTT),
                                           chf[:, :, k].unsqueeze(2).to_broadcast([P, NTT, NE]), ALU.is_equal))
                step(dve.tensor_tensor(cnt[:, :, :], onehot[0][:, :, :], onehot[1][:, :, :], ALU.add))
                dve.wait_ge(f_ps, 3)
                for n in range(2):
                    last = dve.tensor_tensor(Z[:, 0, 2 * n:2 * n + 2, :], PS[:, 6 + n, :].rearrange("p (t c) -> p t c", t=2),
                                             fb3b[:, :].unsqueeze(1).to_broadcast([P, 2, C]), ALU.add)
                last.then_inc(f_cf, 1)
                for n, (w, src) in enumerate(((Fwd, st_f), (Inv, st_i), (Win, st_win), (Wo2, st_wo))):
                    dve.wait_ge(t_hi, n + 1)
                    dve.tensor_tensor(w[:, LO, :, :], src[:, :, :], f(w[:, HI, :, :]), ALU.subtract)
                dve.wait_ge(f_hi, 1)
                dve.tensor_tensor(v2[:, LO, :, :], Z[:, 0, :, :], f(v2[:, HI, :, :]), ALU.subtract).then_inc(f_lo, 1)
                dve.wait_ge(r_ps, 1)
                tiles = lambda n: PS[:, n:n + 2, 0:16 * NE].rearrange("p a (t e) -> p a t e", e=NE)
                halves = lambda t: t[:, :, :].rearrange("p (a t) e -> p a t e", a=2)
                step(dve.tensor_copy(halves(tots[0]), tiles(2)))
                step(dve.tensor_copy(tots[1][:, :, :], tots[0][:, :, :]))
                src, dst = 1, 2
                for d in (1, 2, 4, 8, 16):
                    dve.tensor_copy(tots[dst][:, 0:d, :], tots[src][:, 0:d, :])
                    step(dve.tensor_tensor(tots[dst][:, d:, :], tots[src][:, d:, :], tots[src][:, 0:NTT - d, :], ALU.add))
                    src, dst = dst, src
                run = tots[src]
                step(dve.tensor_scalar(peri[:, 0, :], run[:, NTT - 1, :], float(P - 1), None, ALU.add))
                step(dve.tensor_scalar(peri[:, 1, :], peri[:, 0, :], 7, None, ALU.arith_shift_right))
                step(dve.tensor_copy(per[:, 0, :], peri[:, 1, :]))
                step(dve.tensor_copy(per[:, 1, :], per[:, 0, :]))
                a, z = 1, 2
                for d in (1, 2, 4, 8, 16):
                    dve.tensor_copy(per[:, z, 0:d], per[:, a, 0:d])
                    step(dve.tensor_tensor(per[:, z, d:NE], per[:, a, d:NE], per[:, a, 0:NE - d], ALU.add))
                    a, z = z, a
                end = per[:, a, :]
                step(dve.tensor_tensor(per[:, 4, :], end, per[:, 0, :], ALU.subtract))
                step(dve.tensor_scalar(per[:, 5, :], per[:, 4, :], float(P), None, ALU.mult))
                step(dve.tensor_tensor(slot[:, :, :], run[:, :, :], tots[0][:, :, :], ALU.subtract))
                step(dve.tensor_tensor(slot[:, :, :], slot[:, :, :], bc_e(per[:, 5, :], NTT), ALU.add))
                step(dve.tensor_tensor(halves(slot), halves(slot), tiles(0), ALU.add))
                for k in range(TOPK):
                    step(dve.tensor_tensor(onehot[k][:, :, :], onehot[k][:, :, :], slot[:, :, :], ALU.mult))
                    step(dve.tensor_reduce(out=slotf[:, :, k], in_=onehot[k][:, :, :], op=ALU.add, axis=AX.X))
                step(dve.tensor_copy(pos[:, :, :, :].rearrange("p b t k -> p (b t) k"), slotf[:, :, :]))
                step(dve.tensor_tensor(be_cmp[:, :, :], bc_e(end, NBLK),
                                       ramp[:, 0:NBLK].unsqueeze(2).to_broadcast([P, NBLK, NE]), ALU.is_le))
                step(dve.tensor_reduce(out=slotcnt[:, :],
                                       in_=be_cmp[:, :, :], op=ALU.add, axis=AX.X))
                step(dve.tensor_scalar(block_expert[:, :], slotcnt[:, :], float(NE - 1), None, ALU.min))
                dve.wait_ge(h_sb, 6)
                step(dve.tensor_copy(HN[0:1, :, 0, :], HB[0:1, :, 0, :]))
                dve.memset(HB[0:1, :, 0, :], 0.0)

        U = {n: sem("u_" + n) for n in """xT_in xr_in posb_sb sent vx_ps vx_sb conv0 conv tr v2_hi v2_lo vf_ps vf_sb
            dstep pstep z_hi z_lo y_ps o_sb o_hi o_lo s_ps s_sb""".split()}
        ND, NPQ = 13, 7

        def x2_of(b, m):
            return s2[:, bass.ds(NT * b + 2 * m, 2), :].rearrange("p t c -> p (t c)")

        def turns(eng, before, turn):
            before()
            turn(0)
            with eng.Fori(1, B - 1) as b:
                turn(b)
            turn(B - 1, last=True)

        with nc.Block() as block:
            @block.sync
            def _(sp):
                def load_T(b):
                    at_least(sp, U["vx_ps"], 4 * b)
                    sp.dma_start(f(xT[:, :, :, :]), xn2T_parts[b]).then_inc(U["xT_in"], 16)

                def turn(b, last=False):
                    at_least(sp, U["sent"], 128 * b)
                    sp.dma_start(xrows[:, :, :], xn2_rows[b].rearrange("(t p) d -> p t d", p=P)
                                 ).then_inc(U["xr_in"], 16)
                    if not last:
                        load_T(b + 1)

                turns(sp, lambda: load_T(0), turn)

            @block.tensor
            def _(pe):
                def products(out, lhs, rhs, chunks, stop=True):
                    n, last = len(PAIRS) * chunks, None
                    for c in range(chunks):
                        for i, j in PAIRS:
                            n -= 1
                            last = pe.matmul(out, lhs(i, c), rhs(j, c), start=last is None, stop=stop and n == 0,
                                             skip_group_check=not stop)
                    return last

                def project(b):
                    pe.wait_ge(U["xT_in"], 16 * (b + 1))
                    at_least(pe, U["vf_sb"], 4 * b)
                    for m in range(4):
                        products(PS[:, m, :], lambda i, c: Win[:, i, c, P * m:P * m + P],
                                 lambda j, c: xT[:, j, c, :], CC).then_inc(U["vx_ps"], 1)

                def transposes(b):
                    pe.wait_ge(U["conv"], 4 * (b + 1))
                    if not (isinstance(b, int) and b == 0):
                        at_least(pe, U["s_sb"], 2 * (b - 1))
                    for t in range(NT):
                        for m in range(CC):
                            o = C * (t % 2) + P * m
                            last = pe.transpose(PS[:, 4 + t // 2, o:o + P], cv[:, 0, m, P * t:P * t + P], ident[:, :])
                    last.then_inc(U["tr"], 1)

                def forward(b):
                    pe.wait_ge(U["v2_lo"], b + 1)
                    pe.wait_ge(U["vx_sb"], 4 * (b + 1))
                    transform(pe, v2, 0, U["vf_ps"])

                def back_whole(b):
                    pe.wait_ge(U["z_lo"], 2 * b + 1)
                    at_least(pe, U["o_sb"], 2 * b)
                    for m in range(CC):
                        products(PS[:, 6 + m, :], lambda i, c: Zs[:, i, 0, c, P * m:P * m + P],
                                 lambda j, c: Inv[:, j, c, :], NQ, stop=False)

                def back_mixed(b):
                    pe.wait_ge(U["z_lo"], 2 * (b + 1))
                    for m in range(CC):
                        n = 0
                        for c in range(NQ):
                            for i, j in PAIRS:
                                n += 1
                                last = pe.matmul(PS[:, 6 + m, T // 2:T], Zs[:, i, 1, c, P * m:P * m + P],
                                                 Inv[:, j, c, 0:T // 2], start=False, stop=n == 3 * NQ,
                                                 skip_group_check=True)
                        last.then_inc(U["y_ps"], 1)

                def project_out(b, last):
                    pe.wait_ge(U["o_lo"], b + 1)
                    pe.wait_ge(U["v2_lo"], B if last else b + 2)
                    if last:
                        pe.wait_ge(U["s_sb"], 2 * b)
                    for t in range(NT):
                        ins = products(PS[:, 4 + t // 2, C * (t % 2):C * (t % 2) + C],
                                       lambda i, c: oTs[:, i, c, P * t:P * t + P], lambda j, c: Wo2[:, j, c, :], CC)
                        if t % 2:
                            ins.then_inc(U["s_ps"], 1)

                def before():
                    project(0)
                    transposes(0)
                    forward(0)

                def turn(b, last=False):
                    if not last:
                        project(b + 1)
                    back_whole(b)
                    if not last:
                        transposes(b + 1)
                    back_mixed(b)
                    if not last:
                        forward(b + 1)
                    project_out(b, last)

                turns(pe, before, turn)

            @block.scalar
            def _(act):
                def projected(b, tiles):
                    for m in tiles:
                        act.wait_ge(U["vx_ps"], 4 * b + m + 1)
                        if m < 2:
                            at_least(act, U["conv"], 4 * b)
                        dst = vt[:, m, 1:T + 1] if m < 2 else x2_of(b, m - 2)
                        act.activation(dst, PS[:, m, :], ACT.Identity, bias=binc[:, m:m + 1]).then_inc(U["vx_sb"], 1)

                def first_tap(b):
                    for m in range(CC):
                        act.wait_ge(U["vx_sb"], 4 * b + m + 1)
                        if m == 0:
                            at_least(act, U["tr"], b)
                        act.activation(cv[:, 0, m, :], vt[:, m, 0:T], ACT.Identity, scale=shortc[:, m, 0:1],
                                       bias=shortc[:, m, 3:4]).then_inc(U["conv0"], 1)

                def split_v(b):
                    act.wait_ge(U["tr"], b + 1)
                    at_least(act, U["vf_ps"], 4 * b)
                    act.activation(v2[:, HI, :, :].rearrange("p (a t) c -> p a (t c)", a=2), PS[:, 4:6, :], ACT.Copy
                                   ).then_inc(U["v2_hi"], 1)

                def transformed(b):
                    for n in range(4):
                        act.wait_ge(U["vf_ps"], 4 * b + n + 1)
                        if n == 0:
                            at_least(act, U["dstep"], ND * b)
                            at_least(act, U["pstep"], NPQ * b)
                        act.activation(Vf[:, n // 2, 2 * (n % 2):2 * (n % 2) + 2, :].rearrange("p q c -> p (q c)"),
                                       PS[:, n, :], ACT.Copy).then_inc(U["vf_sb"], 1)

                def split_z(b, z):
                    if z == 0:
                        act.wait_ge(U["dstep"], ND * b + 6)
                        at_least(act, U["y_ps"], 2 * b)
                    else:
                        act.wait_ge(U["dstep"], ND * b + ND)
                        act.wait_ge(U["pstep"], NPQ * (b + 1))
                    act.activation(Zs[:, HI, z, :, :], Z[:, z, :, :], ACT.Copy).then_inc(U["z_hi"], 1)

                def split_o(b):
                    act.wait_ge(U["o_sb"], 2 * (b + 1))
                    at_least(act, U["s_ps"], 2 * b)
                    act.activation(oTs[:, HI, :, :], o32[:, :, :], ACT.Copy).then_inc(U["o_hi"], 1)

                def before():
                    projected(0, (0, 1))
                    first_tap(0)
                    projected(0, (2, 3))
                    split_v(0)
                    transformed(0)

                def turn(b, last=False):
                    split_z(b, 0)
                    if not last:
                        projected(b + 1, (0, 1))
                        first_tap(b + 1)
                        projected(b + 1, (2,))
                    split_z(b, 1)
                    if not last:
                        projected(b + 1, (3,))
                        split_v(b + 1)
                    split_o(b)
                    if not last:
                        transformed(b + 1)

                turns(act, before, turn)

            @block.vector
            def _(dve):
                def short_filter(b):
                    for k in (1, 2):
                        for m in range(CC):
                            if k == 1:
                                dve.wait_ge(U["conv0"], 2 * b + m + 1)
                                at_least(dve, U["tr"], b)
                            else:
                                dve.wait_ge(U["conv"], 4 * b + m + 1)
                            if k == 2:
                                dve.wait_ge(U["vx_sb"], 4 * b + 2)
                            dve.scalar_tensor_tensor(out=cv[:, 2 - k, m, :], in0=vt[:, m, k:k + T],
                                                     scalar=shortc[:, m, k:k + 1],
                                                     in1=cv[:, k - 1, m, :], op0=ALU.mult, op1=ALU.add
                                                     ).then_inc(U["conv"], 1)

                def split_v(b):
                    dve.wait_ge(U["v2_hi"], b + 1)
                    dve.tensor_tensor(v2[:, LO, :, :].rearrange("p (a t) c -> p a (t c)", a=2), PS[:, 4:6, :],
                                      f(v2[:, HI, :, :]).rearrange("p (a t) c -> p a (t c)", a=2), ALU.subtract
                                      ).then_inc(U["v2_lo"], 1)

                def split_z(b, z):
                    dve.wait_ge(U["z_hi"], 2 * b + z + 1)
                    dve.tensor_tensor(Zs[:, LO, z, :, :], Z[:, z, :, :], f(Zs[:, HI, z, :, :]), ALU.subtract
                                      ).then_inc(U["z_lo"], 1)

                def with_filter(b):
                    made = 0

                    def step(ins):
                        nonlocal made
                        made += 1
                        ins.then_inc(U["dstep"], 1)

                    def done(n):
                        dve.wait_ge(U["dstep"], ND * b + n)

                    flat = lambda ap: ap.rearrange("p q c -> p (q c)")
                    re = lambda h_: flat(Vf[:, h_, 0:2, :])
                    im = lambda h_: flat(Vf[:, h_, 2:4, :])
                    tb = lambda t_, h_: flat(t_[:, h_, :, :])
                    mul = lambda n, a_, b_: step(dve.tensor_tensor(tmp[:, n, :], a_, b_, ALU.mult))
                    dve.wait_ge(U["vf_sb"], 4 * b + 2)
                    at_least(dve, U["z_lo"], 2 * b)
                    mul(0, re(0), tb(HA, 0))
                    mul(1, im(0), tb(HB, 0))
                    mul(2, re(0), tb(HB, 0))
                    mul(3, im(0), tb(HN, 0))
                    done(2)
                    step(dve.tensor_tensor(flat(Z[:, 0, 0:2, :]), tmp[:, 0, :], tmp[:, 1, :], ALU.subtract))
                    done(4)
                    step(dve.tensor_tensor(flat(Z[:, 0, 2:4, :]), tmp[:, 2, :], tmp[:, 3, :], ALU.add))
                    done(5)
                    mul(0, re(0), tb(HA, 1))
                    mul(1, im(0), tb(HB, 1))
                    dve.wait_ge(U["vf_sb"], 4 * b + 4)
                    done(6)
                    mul(2, re(1), tb(HA, 0))
                    mul(3, im(1), tb(HB, 0))
                    split_z(b, 0)
                    done(8)
                    step(dve.tensor_tensor(tmp[:, 0, :], tmp[:, 0, :], tmp[:, 1, :], ALU.subtract))
                    done(10)
                    step(dve.tensor_tensor(tmp[:, 2, :], tmp[:, 2, :], tmp[:, 3, :], ALU.subtract))
                    done(12)
                    step(dve.tensor_tensor(flat(Z[:, 1, 0:2, :]), tmp[:, 0, :], tmp[:, 2, :], ALU.add))
                    assert made == ND

                def slots_of(b):
                    at_least(dve, U["sent"], 128 * b)
                    dve.tensor_copy(posb[:, :, :], pos[:, bass.ds(b, 1), :, :].rearrange("p o t k -> p (o t) k")
                                    ).then_inc(U["posb_sb"], 1)

                def gated(b):
                    for m in range(CC):
                        dve.wait_ge(U["y_ps"], 2 * b + m + 1)
                        if m == 0:
                            at_least(dve, U["o_lo"], b)
                            dve.wait_ge(U["vx_sb"], 4 * (b + 1))
                        dve.tensor_tensor(o32[:, m, :], PS[:, 6 + m, :], x2_of(b, m), ALU.mult).then_inc(U["o_sb"], 1)

                def split_o(b):
                    dve.wait_ge(U["o_hi"], b + 1)
                    dve.tensor_tensor(oTs[:, LO, :, :], o32[:, :, :], f(oTs[:, HI, :, :]), ALU.subtract
                                      ).then_inc(U["o_lo"], 1)

                def branch_out(b):
                    for n in range(2):
                        dve.wait_ge(U["s_ps"], 2 * b + n + 1)
                        if n == 0:
                            dve.wait_ge(U["o_sb"], 2 * (b + 1))
                        dve.tensor_tensor(s2[:, bass.ds(NT * b + 2 * n, 2), :],
                                          PS[:, 4 + n, :].rearrange("p (t c) -> p t c", t=2),
                                          bo2b[:, :].unsqueeze(1).to_broadcast([P, 2, C]), ALU.add
                                          ).then_inc(U["s_sb"], 1)

                def before():
                    short_filter(0)
                    split_v(0)

                def turn(b, last=False):
                    with_filter(b)
                    slots_of(b)
                    if not (isinstance(b, int) and b == 0):
                        branch_out(b - 1)
                    if not last:
                        short_filter(b + 1)
                    split_z(b, 1)
                    if not last:
                        split_v(b + 1)
                    gated(b)
                    split_o(b)

                turns(dve, before, turn)
                branch_out(B - 1)

            @block.gpsimd
            def _(pool):
                flat = lambda ap: ap.rearrange("p q c -> p (q c)")

                def with_filter(b):
                    made = 0

                    def step(ins):
                        nonlocal made
                        made += 1
                        ins.then_inc(U["pstep"], 1)

                    pool.wait_ge(U["vf_sb"], 4 * b + 2)
                    at_least(pool, U["z_lo"], 2 * b)
                    mul = lambda n, a_, b_: step(pool.tensor_tensor(tmq[:, n, :], flat(a_), flat(b_), ALU.mult))
                    mul(0, Vf[:, 0, 0:2, :], HB[:, 1, :, :])
                    mul(1, Vf[:, 0, 2:4, :], HN[:, 1, :, :])
                    pool.wait_ge(U["vf_sb"], 4 * b + 4)
                    mul(2, Vf[:, 1, 0:2, :], HB[:, 0, :, :])
                    mul(3, Vf[:, 1, 2:4, :], HN[:, 0, :, :])
                    pool.wait_ge(U["pstep"], NPQ * b + 2)
                    step(pool.tensor_tensor(tmq[:, 0, :], tmq[:, 0, :], tmq[:, 1, :], ALU.add))
                    pool.wait_ge(U["pstep"], NPQ * b + 4)
                    step(pool.tensor_tensor(tmq[:, 2, :], tmq[:, 2, :], tmq[:, 3, :], ALU.add))
                    pool.wait_ge(U["pstep"], NPQ * b + 6)
                    step(pool.tensor_tensor(flat(Z[:, 1, 2:4, :]), tmq[:, 0, :], tmq[:, 2, :], ALU.add))

                def send(b):
                    pool.wait_ge(U["xr_in"], 16 * (b + 1))
                    pool.wait_ge(U["posb_sb"], b + 1)
                    pool.wait_ge(U["pstep"], NPQ * (b + 1))
                    pool.tensor_tensor(idle_q[:, 2:3], ramp_col[:, :], ramp_col[:, :], ALU.mult)
                    for t in range(NT):
                        for k in range(TOPK):
                            pool.indirect_dma_start(slots_in, bass.IndirectOffsetOnAxis(posb[:, t, k:k + 1], axis=0),
                                                    xrows[:, t, :], None).then_inc(U["sent"], 16)

                def turn(b, last=False):
                    with_filter(b)
                    send(b)

                turns(pool, lambda: None, turn)
                pool.wait_ge(U["sent"], 128 * B)

        NW = 10
        EW = NE // NW * C
        cursor[0] = after_shared
        Wes = keep("Wes", [P, 2, CC, NE * C], F32R)
        bes = keep("bes", [P, NE * C])
        st_we = keep("st_we", [P, 2, CC, EW])
        xb = keep("xb", [P, 4, C])
        xbT = keep("xbT", [P, 4, 2, CC, P], F32R)
        yb = keep("yb", [P, 4, C])
        b_in = sem("b_in"); e_hi = sem("e_hi"); e_lo = sem("e_lo")
        e_in = [sem(f"e_in{n}") for n in range(2)]
        with nc.Block() as block:
            @block.sync
            def _(sp):
                for n in range(NW):
                    if n >= 2:
                        sp.wait_ge(e_lo, n - 1)
                    for c in range(CC):
                        sp.dma_start(st_we[:, n % 2, c, :], We[NE // NW * n:NE // NW * (n + 1), P * c:P * c + P, :
                                                               ].rearrange("e p n -> p e n")).then_inc(e_in[n % 2], 16)
                sp.dma_start(bes[:, :], be.partition_broadcast(P)).then_inc(b_in, 16)
                sp.wait_ge(b_in, 16)

            @block.scalar
            def _(act):
                for n in range(NW):
                    act.wait_ge(e_in[n % 2], 16 * CC * (n // 2 + 1))
                    act.activation(Wes[:, HI, :, EW * n:EW * n + EW], st_we[:, n % 2, :, :], ACT.Copy).then_inc(e_hi, 1)

            @block.vector
            def _(dve):
                for n in range(NW):
                    dve.wait_ge(e_hi, n + 1)
                    o = slice(EW * n, EW * n + EW)
                    dve.tensor_tensor(Wes[:, LO, :, o], st_we[:, n % 2, :, :], f(Wes[:, HI, :, o]), ALU.subtract
                                      ).then_inc(e_lo, 1)

        W = {n: sem("e_" + n + "_of") for n in "tr hi lo out kept".split()}
        xb_in = [sem(f"xb_in{u}") for u in range(4)]
        yb_out = [sem(f"yb_out{u}") for u in range(4)]
        NI = NBLK // 4

        def in_fours(eng, before, four):
            before()
            four(0)
            with eng.Fori(1, NI - 1) as i:
                four(i)
            four(NI - 1, last=True)

        rows = lambda ap, j: ap.rearrange("(j p) d -> j p d", p=P)[j]
        with nc.Block() as block:
            @block.sync
            def _(sp):
                def before():
                    for u in range(4):
                        sp.dma_start(xb[:, u, :], rows(slots_in, u)).then_inc(xb_in[u], 16)

                def four(i, last=False):
                    if last:
                        return
                    for u in range(4):
                        sp.wait_ge(W["tr"], 4 * i + u + 1)
                        sp.dma_start(xb[:, u, :], rows(slots_in, 4 * (i + 1) + u)).then_inc(xb_in[u], 16)

                in_fours(sp, before, four)

            @block.gpsimd
            def _(pool):
                def four(i, last=False):
                    for u in range(4):
                        pool.wait_ge(W["kept"], 4 * i + u + 1)
                        pool.dma_start(rows(slots_out, 4 * i + u), yb[:, u, :]).then_inc(yb_out[u], 16)

                in_fours(pool, lambda: None, four)
                for u in range(4):
                    pool.wait_ge(yb_out[u], 16 * NI)

            @block.tensor
            def _(pe):
                def turn(i, u):
                    i, u = i + u // 4, u % 4
                    pe.wait_ge(xb_in[u], 16 * (i + 1))
                    at_least(pe, W["lo"], 4 * (i - 1) + u + 1)
                    for c in range(CC):
                        last = pe.transpose(PS[:, u, P * c:P * c + P], xb[:, u, P * c:P * c + P], ident[:, :])
                    last.then_inc(W["tr"], 1)

                def four(i, last=False):
                    experts = [pe.value_load(block_expert[0:1, bass.ds(4 * i + u, 1)], min_val=0, max_val=NE - 1)
                               for u in range(4)]
                    for u in range(4):
                        if not last or u < 2:
                            turn(i, u + 2)
                        pe.wait_ge(W["lo"], 4 * i + u + 1)
                        at_least(pe, W["kept"], 4 * (i - 1) + u + 1)
                        n = 0
                        for c in range(CC):
                            for a, z in PAIRS:
                                ins = pe.matmul(PS[:, 4 + u, 0:C], xbT[:, u, a, c, :],
                                                Wes[:, z, c, bass.ds(experts[u] * C, C)], start=n == 0, stop=n == 5)
                                n += 1
                        ins.then_inc(W["out"], 1)

                def before():
                    turn(0, 0)
                    turn(0, 1)

                in_fours(pe, before, four)

            @block.scalar
            def _(act):
                def four(i, last=False):
                    for u in range(4):
                        act.wait_ge(W["tr"], 4 * i + u + 1)
                        at_least(act, W["out"], 4 * (i - 1) + u + 1)
                        act.activation(xbT[:, u, HI, :, :].rearrange("p c k -> p (c k)"), PS[:, u, 0:C], ACT.Copy
                                       ).then_inc(W["hi"], 1)

                in_fours(act, lambda: None, four)

            @block.vector
            def _(dve):
                def split(i, u):
                    i, u = i + u // 4, u % 4
                    dve.wait_ge(W["hi"], 4 * i + u + 1)
                    dve.tensor_tensor(xbT[:, u, LO, :, :].rearrange("p c k -> p (c k)"), PS[:, u, 0:C],
                                      f(xbT[:, u, HI, :, :]).rearrange("p c k -> p (c k)"), ALU.subtract
                                      ).then_inc(W["lo"], 1)

                def four(i, last=False):
                    experts = [dve.value_load(block_expert[0:1, bass.ds(4 * i + u, 1)], min_val=0, max_val=NE - 1)
                               for u in range(4)]
                    for u in range(4):
                        if not last or u < 2:
                            split(i, u + 2)
                        dve.wait_ge(W["out"], 4 * i + u + 1)
                        at_least(dve, yb_out[u], 16 * i)
                        dve.tensor_tensor(yb[:, u, :], PS[:, 4 + u, 0:C], bes[:, bass.ds(experts[u] * C, C)], ALU.add
                                          ).then_inc(W["kept"], 1)

                def before():
                    split(0, 0)
                    split(0, 1)

                in_fours(dve, before, four)

        cursor[0] = after_shared
        yg = keep("yg", [P, 2, TOPK, NT, C])
        acc = keep("acc", [P, 2, NT, C])
        acc2 = keep("acc2", [P, 2, NT, C])
        sg = keep("sg", [P, 2, NT, C])
        x1b = keep("x1b", [P, 2, NT, C])
        posc = keep("posc", [P, 2, NT, TOPK], U32)
        X = {n: sem("x_" + n) for n in "idle posc_sb acc_sb acc2_sb sg_sb prod out_sb".split()}
        for n in ("x1_in", "got", "stored"):
            X[n] = [sem(f"x_{n}{e}") for e in range(2)]

        def pairs(eng, pair):
            pair(0)
            with eng.Fori(1, B // 2) as i:
                pair(i)

        with nc.Block() as block:
            @block.sync
            def _(sp):
                def pair(i):
                    for e in range(2):
                        b = 2 * i + e
                        at_least(sp, X["out_sb"], b - 1)
                        sp.dma_start(x1b[:, e, :, :], x1_rows[b].rearrange("(t p) d -> p t d", p=P)
                                     ).then_inc(X["x1_in"][e], 16)

                pairs(sp, pair)

            @block.gpsimd
            def _(pool):
                def pair(i):
                    for e in range(2):
                        b = 2 * i + e
                        pool.wait_ge(X["posc_sb"], b + 1)
                        at_least(pool, X["acc2_sb"], b - 1)
                        at_least(pool, X["idle"], b)
                        pool.tensor_tensor(idle_q[:, 3:4], ramp_col[:, :], ramp_col[:, :], ALU.mult
                                           ).then_inc(X["idle"], 1)
                        for k in range(TOPK):
                            for t in range(NT):
                                pool.indirect_dma_start(yg[:, e, k, t, :], None, slots_out,
                                                        bass.IndirectOffsetOnAxis(posc[:, e, t, k:k + 1], axis=0)
                                                        ).then_inc(X["got"][e], 16)

                pairs(pool, pair)

            @block.vector
            def _(dve):
                def slots_of(b, e, gathered):
                    at_least(dve, X["got"][e], 128 * gathered)
                    dve.tensor_copy(posc[:, e, :, :], pos[:, bass.ds(b, 1), :, :].rearrange("p o t k -> p (o t) k")
                                    ).then_inc(X["posc_sb"], 1)

                def pair(i, last_pair=False):
                    for e in range(2):
                        b = 2 * i + e
                        dve.wait_ge(X["got"][e], 128 * (i + 1))
                        gate = lambda t, k: gates[:, bass.ds(NT * b + t, 1), k]
                        for t in range(NT):
                            last = dve.tensor_scalar(acc[:, e, t, :], yg[:, e, 0, t, :], gate(t, 0), None, ALU.mult)
                        last.then_inc(X["acc_sb"], 1)
                        dve.wait_ge(X["acc_sb"], b + 1)
                        at_least(dve, X["sg_sb"], b - 1)
                        for t in range(NT):
                            last = dve.scalar_tensor_tensor(out=acc2[:, e, t, :], in0=yg[:, e, 1, t, :],
                                                            scalar=gate(t, 1), in1=acc[:, e, t, :],
                                                            op0=ALU.mult, op1=ALU.add)
                        last.then_inc(X["acc2_sb"], 1)
                        if not last_pair:
                            slots_of(b + 2, e, i + 1)
                        dve.wait_ge(X["sg_sb"], b + 1)
                        dve.tensor_tensor(acc[:, e, :, :], sg[:, e, :, :], s2[:, bass.ds(NT * b, NT), :], ALU.mult
                                          ).then_inc(X["prod"], 1)
                        dve.wait_ge(X["prod"], b + 1)
                        dve.wait_ge(X["x1_in"][e], 16 * (i + 1))
                        dve.tensor_tensor(sg[:, e, :, :], acc[:, e, :, :], x1b[:, e, :, :], ALU.add
                                          ).then_inc(X["out_sb"], 1)

                slots_of(0, 0, 0)
                slots_of(1, 1, 0)
                pair(0)
                with dve.Fori(1, B // 2 - 1) as i:
                    pair(i)
                pair(B // 2 - 1, last_pair=True)

            @block.scalar
            def _(act):
                def pair(i):
                    for e in range(2):
                        b = 2 * i + e
                        act.wait_ge(X["acc2_sb"], b + 1)
                        at_least(act, X["stored"][e], 16 * i)
                        act.activation(sg[:, e, :, :], acc2[:, e, :, :], ACT.Silu).then_inc(X["sg_sb"], 1)
                        act.wait_ge(X["out_sb"], b + 1)
                        act.dma_start(out[b].rearrange("(t p) d -> p t d", p=P), sg[:, e, :, :]
                                      ).then_inc(X["stored"][e], 16)

                pairs(act, pair)
                for e in range(2):
                    act.wait_ge(X["stored"][e], 16 * B // 2)


def constants():
    half = T // 2
    t = np.arange(FQ, dtype=np.float64)
    k = np.arange(half, dtype=np.float64)
    angle = 2 * np.pi * np.outer(t, k) / FQ
    top = np.where(t % 2 == 0, 1.0, -1.0)
    fwd = np.concatenate([np.cos(angle), -np.sin(angle)], axis=1)
    fwd[:, half] = top
    weight = np.full(half, 2.0 / FQ)
    weight[0] = 1.0 / FQ
    inv = np.concatenate([(np.cos(angle) * weight).T, (-np.sin(angle) * weight).T], axis=0)
    inv[half] = top / FQ
    return {"ident_c": np.eye(P, dtype=np.float32), "ramp_c": np.arange(P, dtype=np.float32)[None],
            "pos_c": np.linspace(0.0, 1.0, T, dtype=np.float32)[None],
            "dft_c": np.ascontiguousarray(fwd[:half], dtype=np.float32), "idft_c": inv.astype(np.float32)}


def kernel(**inputs):
    import concourse.bacc as bacc
    from concourse.bass_utils import run_bass_kernel_spmd

    a = {name: np.asarray(v) for name, v in inputs.items()}

    def padded(w, shape):
        out = np.zeros(shape, w.dtype)
        out[tuple(slice(0, n) for n in w.shape)] = w
        return out

    columns = lambda v: v.reshape(-1, P).T
    w_in, b_in = a["L1_attn_in_proj_w"], a["L1_attn_in_proj_b"]
    short = np.concatenate([a["L1_attn_short_w"][:, 0, :], a["L1_attn_short_b"][:, None]], axis=1)
    arrays = {
        "x": a["L0_attn_x"], "wqkvT": a["L0_attn_w_qkv"].T, "woutT": a["L0_attn_w_out"].T,
        "wguT": np.concatenate([a["L0_ffn_w_gate"], a["L0_ffn_w_up"]]).T, "wdT": a["L0_ffn_w_down"].T,
        "wg1": padded(a["L1_ffn_wg1"], (C, P)), "bg1": padded(a["L1_ffn_bg1"][:, None], (P, 1)),
        "wg2": a["L1_ffn_wg2"][:, :NE], "bg2": a["L1_ffn_bg2"][None, :NE],
        "winT": np.concatenate([w_in[:, 0::3], w_in[:, 2::3]], axis=1),
        "bin_": columns(np.concatenate([b_in[0::3], b_in[2::3]])),
        "short": short.reshape(CC, P, 4).transpose(1, 0, 2),
        "wo2": a["L1_attn_out_w"], "bo2": a["L1_attn_out_b"][None],
        "fw1": a["L1_attn_fw1"], "fb1": a["L1_attn_fb1"][:, None], "fw2": a["L1_attn_fw2"],
        "fb2": a["L1_attn_fb2"][:, None], "fw3": a["L1_attn_fw3"][:, 1::2], "fb3": a["L1_attn_fb3"][None, 1::2],
        "We": a["L1_ffn_We"], "be": a["L1_ffn_be"].reshape(1, -1),
    }
    arrays.update(constants())
    arrays = {name: np.ascontiguousarray(v) for name, v in arrays.items()}
    nc = bacc.Bacc("TRN2", target_bir_lowering=False, num_devices=1)
    args = {name: nc.dram_tensor(name, v.shape, mybir.dt.from_np(v.dtype), kind="ExternalInput").ap()
            for name, v in arrays.items()}
    args["out"] = nc.dram_tensor("out", (B, T, C), F32, kind="ExternalOutput").ap()
    program(nc, **args)
    return run_bass_kernel_spmd(nc, [arrays], core_ids=[0]).results[0]["out"]
```

```python
import math
import numpy as np
import concourse.bass as bass
from concourse import mybir
from contextlib import ExitStack

F32 = mybir.dt.float32
F32R = mybir.dt.float32r
F16 = mybir.dt.float16
I32 = mybir.dt.int32
U32 = mybir.dt.uint32
ALU = mybir.AluOpType
ACT = mybir.ActivationFunctionType
AX = mybir.AxisListType

P = 128
B, T, C = 8, 512, 256
NT = T // P
CC = C // P
NH, HD = 16, 16
NG, GH = 4, 4
SCALE = 1.0 / math.sqrt(HD)
FF = 768
NF = FF // P
QSCALE = 1.0 / 127.0
EPS = 1e-5
MASK = -10000.0 / SCALE
KS = 96
HG = 64
NE, TOPK = 20, 2
NBLK = B * T * TOPK // P + NE
FQ = 512
NQ = FQ // P
HI, LO = 0, 1
EARLY = 3
FIRST_HALF = 3
ZW = 448
M0 = 64
PAIRS = ((HI, HI), (HI, LO), (LO, HI))
Q_PARTS, K_PARTS = zip(*PAIRS)


def at_least(eng, sem, value):
    if isinstance(value, int) and value <= 0:
        return
    eng.wait_ge(sem, value)


def program(nc, x, wqkvT, woutT, wguT, wdT, wg1, bg1, wg2, bg2, winT, bin_, short, wo2, bo2, fw1, fb1, fw2, fb2,
            fw3, fb3, We, be, ident_c, ramp_c, pos_c, dft_c, idft_c, out):
    x1_rows = nc.dram_tensor("x1_rows", (B, T, C), F32, kind="Internal").ap()
    xn2_rows = nc.dram_tensor("xn2_rows", (B, T, C), F32, kind="Internal").ap()
    xn2T_parts = nc.dram_tensor("xn2T_parts", (B, P, 2, CC, T), F32, kind="Internal").ap()
    qk_parts = nc.dram_tensor("qk_parts", (2, 2, P, 2, T), F32, kind="Internal").ap()
    slots_in = nc.dram_tensor("slots_in", (NBLK * P, C), F32, kind="Internal").ap()
    slots_out = nc.dram_tensor("slots_out", (NBLK * P, C), F32, kind="Internal").ap()
    ctx = ExitStack()
    with ctx:
        sem = lambda name: ctx.enter_context(nc.semaphore(name))
        cursor = [-(-nc.sbuf_base // 32) * 32]

        def size(shape, dt):
            n = 2 if dt == F16 else 4
            for s in shape[1:]:
                n *= s
            return -(-n // 32) * 32

        def keep(name, shape, dt=F32):
            off = cursor[0]
            cursor[0] += size(shape, dt)
            return nc.alloc_sbuf_tensor_at(name, shape, dt, offset=off)

        def share(*tensors):
            made, off = [], cursor[0]
            for name, shape, dt in tensors:
                made.append(nc.alloc_sbuf_tensor_at(name, shape, dt, offset=off))
                off += size(shape, dt)
            return made, off

        ident = keep("ident", [P, P])
        gates = keep("gates", [P, B * NT, TOPK])
        chosen = keep("chosen", [P, B * NT, TOPK], U32)
        first_free = cursor[0]
        ident16 = keep("ident16", [P, P], F16)
        mask16 = keep("mask16", [P, P], F16)
        Wqkv = keep("Wqkv", [P, 2, CC, 3 * C], F32R)
        Wout = keep("Wout", [P, 2, CC, C], F32R)
        Wgu = keep("Wgu", [P, CC, 2 * FF], F32R)
        Wd = keep("Wd", [P, NF, C], F32R)
        Wg1 = keep("Wg1", [P, 2, CC, P], F32R)
        Wg2 = keep("Wg2", [HG, NE])
        bg1c = keep("bg1c", [P, 1])
        bg2b = keep("bg2b", [P, NE])
        neghalf = keep("neghalf", [P, NT])
        zeros = keep("zeros", [P, T])
        xin = keep("xin", [P, NT, C])
        xres = keep("xres", [P, NT, C])
        xn = keep("xn", [P, NT, C])
        xnT = keep("xnT", [P, 2, CC, T], F32R)
        qs = keep("qs", [KS, NH, T], F32R)
        ks = keep("ks", [KS, NH, T], F32R)
        V = keep("V", [P, NT, NH, 2 * HD])
        G = keep("G", [P, NT, C])
        Mneg = keep("Mneg", [P, 2, NT, GH])
        Mhi = keep("Mhi", [P, NT, GH], F32R)
        Mparts = keep("Mparts", [P, NT, 2, GH])
        mrow = keep("mrow", [2 * GH, T])
        stats = keep("stats", [P, NT, 6])
        mv = keep("mv", [P, NT, 2])
        veps = keep("veps", [P, NT])
        rstd = keep("rstd", [P, NT])
        stats2 = keep("stats2", [P, NT, 6])
        mv2 = keep("mv2", [P, NT, 2])
        veps2 = keep("veps2", [P, NT])
        rstd2 = keep("rstd2", [P, NT])
        idle_p = keep("idle_p", [P, NH])
        idle_v = keep("idle_v", [P, 1])
        rinv = keep("rinv", [P, NT, NH])
        lg = keep("lg", [P, NT, NE])
        lge = keep("lge", [P, NT, NE])
        small = keep("small", [P, 4, NT])
        top8 = keep("top8", [P, NT, 8])
        idx8 = keep("idx8", [P, NT, 8], U32)
        (qhl, khl), e1 = share(("qhl", [P, 2, 2, T], F32R), ("khl", [P, 2, 2, T], F32R))
        (OT, On), e2 = share(("OT", [P, NG, T], F32), ("On", [P, NT, C], F32))
        cursor[0] = max(e1, e2)
        (xn2T,), _ = share(("xn2T", [P, 2, CC, T], F32R))
        (OnT,), e1 = share(("OnT", [P, 2, CC, T], F32R))
        cursor[0] = e1
        xn2 = xn
        hgT = keep("hgT", [P, T])
        (PT,), e1 = share(("PT", [P, 2, GH, 1280], F32))
        (sil, h32, h), e2 = share(("sil", [P, 2, T], F32), ("h32", [P, 2, T], F32), ("h", [P, NF, 2, T], F32R))
        assert 4 * T * (4 + 2 * FIRST_HALF) <= 4 * GH * 1280
        (st_qkv, st_out, st_gu, st_d, st_g1), e3 = share(
            ("st_qkv", [P, CC, 3 * C], F32), ("st_out", [P, CC, C], F32), ("st_gu", [P, CC, 2 * FF], I32),
            ("st_d", [P, NF, C], I32), ("st_g1", [P, CC, P], F32))
        cursor[0] = max(e1, e2, e3)
        PS = ctx.enter_context(nc.psum_tensor("PS", [P, 8, T], F32))

        def f(ap):
            return ap.bitcast(F32)

        w_in = sem("w_in"); w_ms = sem("w_ms"); w_zero = sem("w_zero"); w_hi = sem("w_hi"); w_done = sem("w_done")
        with nc.Block() as block:
            @block.sync
            def _(sp):
                sp.dma_start(st_qkv[:, :, :], wqkvT.rearrange("(c p) n -> p c n", p=P)).then_inc(w_in, 16)
                sp.dma_start(st_out[:, :, :], woutT.rearrange("(c p) n -> p c n", p=P)).then_inc(w_in, 16)
                sp.dma_start(st_g1[:, :, :], wg1.rearrange("(c p) n -> p c n", p=P)).then_inc(w_in, 16)
                sp.dma_start(ident[:, :], ident_c).then_inc(w_in, 16)
                sp.dma_start(st_gu[:, :, :], wguT.rearrange("(c p) n -> p c n", p=P)).then_inc(w_in, 16)
                sp.dma_start(st_d[:, :, :], wdT.rearrange("(c p) n -> p c n", p=P)).then_inc(w_in, 16)
                sp.dma_start(Wg2[:, :], wg2).then_inc(w_in, 16)
                sp.dma_start(bg1c[:, :], bg1).then_inc(w_in, 16)
                sp.dma_start(bg2b[:, :], bg2.partition_broadcast(P)).then_inc(w_in, 16)
                sp.wait_ge(w_in, 16 * 9)

            @block.gpsimd
            def _(pool):
                pool.memset(mask16[:, :], 0.0).then_inc(w_ms, 1)
                pool.memset(neghalf[:, :], -0.5)
                pool.memset(V[:, :, :, :], 1.0)
                pool.wait_ge(w_ms, 1)
                pool.affine_select(out=mask16[:, :], in_=mask16[:, :], compare_op=ALU.is_ge, fill=MASK, base=0,
                                   pattern=[[-1, P]], channel_multiplier=1).then_inc(w_ms, 1)
                pool.memset(f(ks[:, :, :]), 0.0).then_inc(w_zero, 1)
                pool.wait_ge(w_zero, 1)
                pool.memset(f(ks[M0:M0 + 2, :, :]), 1.0)

            @block.scalar
            def _(act):
                act.wait_ge(w_in, 16 * 9)
                for hi, src in ((Wqkv, st_qkv), (Wout, st_out), (Wg1, st_g1)):
                    act.activation(hi[:, HI, :, :], src[:, :, :], ACT.Copy).then_inc(w_hi, 1)
                act.activation(Wd[:, :, :], st_d[:, :, :], ACT.Copy)
                act.activation(ident16[:, :], ident[:, :], ACT.Copy).then_inc(w_done, 1)

            @block.vector
            def _(dve):
                dve.memset(zeros[:, :], 0.0)
                dve.memset(f(qs[:, :, :]), 0.0)
                dve.wait_ge(w_in, 16 * 9)
                for n, (w, src) in enumerate(((Wqkv, st_qkv), (Wout, st_out), (Wg1, st_g1))):
                    dve.wait_ge(w_hi, n + 1)
                    dve.tensor_tensor(w[:, LO, :, :], src[:, :, :], f(w[:, HI, :, :]), ALU.subtract)
                dve.tensor_copy(Wgu[:, :, :], st_gu[:, :, :]).then_inc(w_done, 1)

        names = """x_in ln_var ln_std ln_done tx xnT_hi xnT_lo qk_ps qk_hi qk_lo v_ps v_sb
            gu_ps silu_sb h32_sb h_hi h_lo h_lo_last down_ps g_sb ln2_var ln2_std ln2_done t2 xn2T_hi xn2T_lo hg_ps hg_sb
            lg_ps lg_in lge_sb x1_out xn2_out xn2T_out xres_in unit maxed m_parts mt mrow_sb m_in st_ps
            exped masked pv ot_sb otr rinv_sb on_sb ont ont_hi ont_lo op y_sb x1_sb step slots_clear"""
        S = {n: sem("s_" + n) for n in names.split()}
        UNITS = ((3, (0, 1), 512), (3, (2, 3), 512), (2, (0, 1), 384), (2, (2, 3), 384),
                 (1, (0, 1, 2, 3), 256), (0, (0, 1, 2, 3), 128))
        NU = len(UNITS)
        BANK = (0, 2, 4, 6, 4, 6)
        PIECES = (((0, 0, 0),), ((1, 0, 512), (3, 384, 896)), ((2, 0, 1024),))
        WIDTH = (512, 512, 256)
        COL = {0: 0, 1: 512, 2: 1024, 3: 896}

        def slot_of(g, u):
            if g == 0:
                return 2 if u % 2 == 0 else 4
            return 2 * (((NU + 1) * g + u + 1) % 2)

        def scores_of_unit(slot, u):
            qt, heads, keys = UNITS[u]
            if keys > 256:
                return [PS[:, slot + n, 0:keys] for n in range(2)], PS[:, slot:slot + 2, 0:keys]
            if keys == 256:
                both = PS[:, slot:slot + 2, :].rearrange("p a (b k) -> p (a b) k", b=2)
                return [PS[:, slot + n // 2, 256 * (n % 2):256 * (n % 2) + 256] for n in range(4)], both
            return ([PS[:, slot, 128 * n:128 * n + 128] for n in range(4)],
                    PS[:, slot, :].rearrange("p (a k) -> p a k", a=4))

        S["mhi"] = sem("s_mhi")
        S["stack_in"] = [sem(f"s_stack_in{g}") for g in range(NG)]
        S["spilt"] = [sem(f"s_spilt{m}") for m in range(2)]
        STACKED = 16 * 7

        def up_to(b):
            return min(b, B) if isinstance(b, int) else b

        with nc.Block() as block:
            @block.sync
            def _(sp):
                def load_x(b):
                    at_least(sp, S["ln_done"], b)
                    sp.dma_start(xin[:, :, :], x[b].rearrange("(t p) d -> p t d", p=P)).then_inc(S["x_in"], 16)

                def spill(b):
                    for g in range(NG):
                        at_least(sp, S["stack_in"][g], STACKED * b)
                    for m, (src, n) in enumerate(((qhl, 0), (khl, 1), (qhl, 0), (khl, 1))):
                        sp.wait_ge(S["qk_lo"], 4 * b + m + 1)
                        sp.dma_start(qk_parts[n, m // 2], f(src[:, m // 2, :, :])).then_inc(S["spilt"][m // 2], 16)

                def stack(b, g):
                    at_least(sp, S["st_ps"], 48 * (b - 1) + 12 * (g + 1))
                    if g % 2 == 0:
                        sp.wait_ge(S["spilt"][g // 2], 32 * (b + 1))
                    sp.dma_start(f(qs[M0:M0 + 2, GH * g:GH * g + GH, :]),
                                 zeros[0:2, :].unsqueeze(1).to_broadcast([2, GH, T])).then_inc(S["stack_in"][g], 16)
                    for n, (dst, parts) in enumerate(((qs, Q_PARTS), (ks, K_PARTS))):
                        for blk, part in enumerate(parts):
                            sp.dma_start(
                                f(dst[HD * blk:HD * blk + HD, GH * g:GH * g + GH, :]),
                                qk_parts[n, g // 2, 64 * (g % 2):64 * (g % 2) + 64, part, :].rearrange(
                                    "(h d) t -> d h t", d=HD)).then_inc(S["stack_in"][g], 16)

                def store(b):
                    sp.wait_ge(S["x1_sb"], b + 1)
                    sp.dma_start(x1_rows[b].rearrange("(t p) d -> p t d", p=P), xres[:, :, :]
                                 ).then_inc(S["x1_out"], 16)
                    sp.wait_ge(S["ln2_done"], NT * (b + 1))
                    sp.dma_start(xn2_rows[b].rearrange("(t p) d -> p t d", p=P), xn2[:, :, :]
                                 ).then_inc(S["xn2_out"], 16)
                    sp.wait_ge(S["x1_out"], 16 * (b + 1))

                def store_T(b):
                    sp.wait_ge(S["xn2T_lo"], b + 1)
                    sp.dma_start(xn2T_parts[b], f(xn2T[:, :, :, :])).then_inc(S["xn2T_out"], 16)

                def load_res(b):
                    sp.dma_start(xres[:, :, :], x[b].rearrange("(t p) d -> p t d", p=P)).then_inc(S["xres_in"], 16)

                def rows_of_maxima(b, g):
                    sp.wait_ge(S["mrow_sb"], NG * b + g + 1)
                    for r in range(2):
                        sp.dma_start(f(qs[M0 + r:M0 + r + 1, GH * g:GH * g + GH, :]),
                                     mrow[GH * r:GH * r + GH, :]).then_inc(S["m_in"], 16)

                def clear_slots(b):
                    sp.dma_start(slots_in.rearrange("s d -> (s d)").rearrange(
                        "(b p r e) -> b p r e", b=B, p=P, e=ZW)[b], 
                        zeros[:, 0:ZW].unsqueeze(1).to_broadcast([P, NBLK * C // (B * ZW), ZW])
                        ).then_inc(S["slots_clear"], 16)

                def sequence(b, first=False, last=False):
                    if not last:
                        load_x(b + 1)
                    if not first:
                        store(b - 1)
                    load_res(b)
                    if not first:
                        store_T(b - 1)
                    if not last:
                        spill(b + 1)
                    for g in range(NG + 1):
                        if g < NG:
                            rows_of_maxima(b, g)
                        if g > 0 and not last:
                            stack(b + 1, g - 1)
                    clear_slots(b)

                load_x(0)
                spill(0)
                for g in range(NG):
                    stack(0, g)
                sequence(0, first=True)
                with sp.Fori(1, B - 1) as b:
                    sequence(b)
                sequence(B - 1, last=True)
                store(B - 1)
                store_T(B - 1)
                for n in ("x1_out", "xn2_out", "xn2T_out", "slots_clear"):
                    sp.wait_ge(S[n], 16 * B)

            @block.tensor
            def _(pe):
                def split_products(out, lhs, rhs, chunks=CC, pairs=PAIRS):
                    n, last = len(pairs) * chunks, None
                    for c in range(chunks):
                        for i, j in pairs:
                            n -= 1
                            last = pe.matmul(out, lhs(i, c), rhs(j, c), start=last is None, stop=n == 0)
                    return last

                def transposed_x(b):
                    pe.wait_ge(S["ln_done"], NT * (b + 1))
                    at_least(pe, S["h32_sb"], NF * b)
                    for c in range(CC):
                        for t in range(NT):
                            last = pe.transpose(PS[:, 4 + c, P * t:P * t + P], xn[:, t, P * c:P * c + P], ident[:, :])
                    last.then_inc(S["tx"], 1)

                def project_qk(b, tiles):
                    for m in tiles:
                        if m == 0:
                            pe.wait_ge(S["xnT_hi"], b + 1)
                            pe.wait_ge(S["xnT_lo"], b + 1)
                            at_least(pe, S["g_sb"], 2 * b)
                        if m >= 2:
                            pe.wait_ge(S["qk_lo"], 4 * b + m - 1)
                        o = C * (m % 2) + P * (m // 2)
                        split_products(PS[:, m % 2, :],
                                       lambda i, c: Wqkv[:, i, c, o:o + P],
                                       lambda j, c: xnT[:, j, c, :]).then_inc(S["qk_ps"], 1)

                def project_v(b, tiles):
                    for t in tiles:
                        if t == 0:
                            at_least(pe, S["exped"], 48 * b)
                        if t == 2:
                            at_least(pe, S["ot_sb"], NG * b)
                        last = split_products(PS[:, 6 + t // 2, C * (t % 2):C * (t % 2) + C],
                                              lambda i, c: xnT[:, i, c, P * t:P * t + P],
                                              lambda j, c: Wqkv[:, j, c, 2 * C:3 * C])
                        if t % 2:
                            last.then_inc(S["v_ps"], 1)

                def gate_up(b, tiles, halves=range(2)):
                    for i in tiles:
                        bank = BANK[i]
                        gate_first = halves[0] == 0
                        if not gate_first:
                            assert i < 2
                        elif i == 0:
                            at_least(pe, S["mrow_sb"], NG * b)
                            if isinstance(b, int) and b == 0:
                                pe.wait_ge(S["qk_lo"], 4)
                            pe.wait_ge(S["xnT_hi"], b + 1)
                            pe.wait_ge(S["xnT_lo"], b + 1)
                        elif i == 2:
                            at_least(pe, S["exped"], 48 * b)
                        elif i == 3:
                            pe.wait_ge(S["v_sb"], 2 * (b + 1))
                        elif i >= 4:
                            pe.wait_ge(S["h32_sb"], NF * b + i - 1)
                        for half in halves:
                            o = FF * half + P * i
                            last = split_products(PS[:, bank + half, :],
                                                  lambda i_, c: Wgu[:, c, o:o + P],
                                                  lambda j, c: xnT[:, j, c, :], pairs=((HI, HI), (HI, LO)))
                            last.then_inc(S["gu_ps"], 1)

                def down(b, first):
                    for t in range(NT):
                        if t == 2 and not first:
                            route_transposes(b - 1)
                        if t == 0:
                            at_least(pe, S["ont_lo"], b)
                            if isinstance(b, int) and b == 0:
                                pe.wait_ge(S["qk_lo"], 4)
                        for i in range(NF):
                            if t == 0:
                                pe.wait_ge(S["h_hi"], NF * b + i + 1)
                                if i < NF - 1:
                                    pe.wait_ge(S["h_lo"], (NF - 1) * b + i + 1)
                                else:
                                    pe.wait_ge(S["h_lo_last"], b + 1)
                            for part in (HI, LO):
                                ins = pe.matmul(PS[:, t // 2, C * (t % 2):C * (t % 2) + C],
                                                 h[:, i, part, P * t:P * t + P], Wd[:, i, :],
                                                 start=(i == 0 and part == HI), stop=(i == NF - 1 and part == LO))
                        if t % 2:
                            ins.then_inc(S["down_ps"], 1)

                def route_transposes(b):
                    pe.wait_ge(S["ln2_done"], NT * (b + 1))
                    pe.wait_ge(S["y_sb"], 2 * (b + 1))
                    for c in range(CC):
                        for t in range(NT):
                            last = pe.transpose(PS[:, 2 + c, P * t:P * t + P], xn2[:, t, P * c:P * c + P],
                                                ident[:, :])
                    last.then_inc(S["t2"], 1)

                def route_hidden(b, mlps):
                    pe.wait_ge(S["xn2T_lo"], b + 1)
                    pe.wait_ge(S["h32_sb"], NF * mlps)
                    split_products(PS[:, 6, :], lambda i, c: Wg1[:, i, c, :],
                                   lambda j, c: xn2T[:, j, c, :]).then_inc(S["hg_ps"], 1)

                def route_logits(b):
                    pe.wait_ge(S["hg_sb"], b + 1)
                    for t in range(NT):
                        last = pe.matmul(PS[:, 7, 32 * t:32 * t + NE], hgT[0:HG, P * t:P * t + P], Wg2[:, :],
                                         start=True, stop=True)
                    last.then_inc(S["lg_ps"], 1)

                def unit(b, g, u):
                    slot = slot_of(g, u)
                    if u == 0:
                        pe.wait_ge(S["stack_in"][g], STACKED * (b + 1))
                    if g == 0 and u == 0:
                        at_least(pe, S["xn2T_lo"], b)
                    elif g == 0 and u == 1:
                        pe.wait_ge(S["xnT_lo"], up_to(b + 2))
                        pe.wait_ge(S["h32_sb"], NF * (b + 1))
                    elif g == 1 and u == 0:
                        pe.wait_ge(S["qk_lo"], 4 * up_to(b + 2))
                        pe.wait_ge(S["g_sb"], 2 * (b + 1))
                    elif u == 0:
                        pe.wait_ge(S["maxed"], NU * (NG * b + g))
                    elif u == 1:
                        pe.wait_ge(S["mrow_sb"], NG * b + g)
                    else:
                        pe.wait_ge(S["maxed"], NU * (NG * b + g) + u - 1)
                    qt, heads, keys = UNITS[u]
                    places, _ = scores_of_unit(slot, u)
                    for j, out in zip(heads, places):
                        hd = GH * g + j
                        pe.matmul(out, qs[:, hd, P * qt:P * qt + P], ks[:, hd, 0:keys], start=True, stop=False)
                        last = pe.matmul(out[:, keys - P:keys], ident16[:, :], mask16[:, :], start=False, stop=True)
                    last.then_inc(S["unit"], 1)

                def maxima_as_rows(b, g):
                    slot = slot_of(g, NU)
                    pe.wait_ge(S["m_parts"], NG * b + g + 1)
                    for qt in range(NT):
                        last = pe.matmul(PS[0:2 * GH, slot, P * qt:P * qt + P],
                                         Mparts[:, qt, :, :].rearrange("p r j -> p (r j)"), ident[:, :],
                                         start=True, stop=True)
                    last.then_inc(S["mt"], 1)

                def transposed_scores(b, g, j):
                    hd = GH * g + j
                    if hd == 0:
                        pe.wait_ge(S["xnT_lo"], up_to(b + 2))
                        pe.wait_ge(S["h32_sb"], NF * (b + 1))
                        at_least(pe, S["hg_sb"], b)
                    if j == 0:
                        pe.wait_ge(S["m_in"], 32 * (NG * b + g + 1))
                    for n, piece in enumerate(PIECES):
                        if hd > 0:
                            pe.wait_ge(S["exped"], 48 * b + 3 * (hd - 1) + n + 1)
                        for kt, col, _ in piece:
                            last = pe.matmul(PS[:, 4 + n, col:col + T - P * kt], ks[:, hd, P * kt:P * kt + P],
                                             qs[:, hd, P * kt:T], start=True, stop=True)
                        last.then_inc(S["st_ps"], 1)

                def values(b, g):
                    at_least(pe, S["ot_sb"], NG * b + g)
                    if g == 0:
                        at_least(pe, S["lg_in"], b)
                    pe.wait_ge(S["exped"], 48 * b + 12 * (g + 1))
                    pe.wait_ge(S["masked"], 16 * b + 4 * (g + 1))
                    for kt in range(NT):
                        for j in range(GH):
                            last = pe.matmul(PS[32 * j:32 * j + 32, 7, P * kt:T], V[:, kt, GH * g + j, :],
                                             PT[:, g % 2, j, COL[kt]:COL[kt] + T - P * kt],
                                             start=kt == 0, stop=kt == NT - 1)
                    last.then_inc(S["pv"], 1)

                def attention(b, last):
                    for s in range(1, NG + 2):
                        for u in range(NU + 1):
                            if s < NG and u < NU:
                                unit(b, s, u)
                            if u == 1 and 2 <= s:
                                values(b, s - 2)
                            if s == NG and u in (1, 2, 4, 6) and not last:
                                n = (1, 2, 4, 6).index(u)
                                gate_up(b + 1, (n // 2,), (n % 2,))
                            if s <= NG and u in (1, 2, 4, 5):
                                transposed_scores(b, s - 1, (1, 2, 4, 5).index(u))
                        if s < NG:
                            maxima_as_rows(b, s)

                def heads_as_rows(b, last):
                    for qt in range(NT):
                        if qt == 0:
                            pe.wait_ge(S["ot_sb"], NG * (b + 1))
                            pe.wait_ge(S["mrow_sb"], NG * (b + 1))
                            if not last:
                                pe.wait_ge(S["h32_sb"], NF * (b + 1) + 2)
                        for g in range(NG):
                            last = pe.transpose(PS[:, qt, P * g:P * g + P], OT[:, g, P * qt:P * qt + P], ident[:, :])
                        last.then_inc(S["otr"], 1)

                def output_transposes(b):
                    pe.wait_ge(S["on_sb"], NT * (b + 1))
                    for c in range(CC):
                        for t in range(NT):
                            last = pe.transpose(PS[:, c, P * t:P * t + P], On[:, t, P * c:P * c + P], ident[:, :])
                    last.then_inc(S["ont"], 1)

                def project_out(b):
                    pe.wait_ge(S["ont_hi"], b + 1)
                    pe.wait_ge(S["ont_lo"], b + 1)
                    for t in range(NT):
                        last = split_products(PS[:, 2 + t // 2, C * (t % 2):C * (t % 2) + C],
                                              lambda i, c: OnT[:, i, c, P * t:P * t + P],
                                              lambda j, c: Wout[:, j, c, :])
                        if t % 2:
                            last.then_inc(S["op"], 1)

                def sequence(b, first=False, last=False):
                    gate_up(b, range(EARLY, NF))
                    down(b, first)
                    if not last:
                        transposed_x(b + 1)
                    unit(b, 0, 0)
                    if not first:
                        route_hidden(b - 1, b + 1)
                    unit(b, 0, 1)
                    qk_tiles = iter(()) if last else iter(range(4))
                    for u in range(2, NU + 1):
                        if not last and u != 4:
                            project_qk(b + 1, (next(qk_tiles),))
                        if u < NU:
                            unit(b, 0, u)
                    maxima_as_rows(b, 0)
                    if not first:
                        route_logits(b - 1)
                    attention(b, last)
                    if not last:
                        project_v(b + 1, (0, 1))
                    heads_as_rows(b, last)
                    if not last:
                        project_v(b + 1, (2, 3))
                    output_transposes(b)
                    if not last:
                        gate_up(b + 1, (2,))
                    project_out(b)

                transposed_x(0)
                project_qk(0, range(4))
                gate_up(0, (0, 1))
                project_v(0, range(NT))
                gate_up(0, (2,))
                sequence(0, first=True)
                with pe.Fori(1, B - 1) as b:
                    sequence(b)
                sequence(B - 1, last=True)
                route_transposes(B - 1)
                route_hidden(B - 1, B)
                route_logits(B - 1)

            @block.scalar
            def _(act):
                def split_x(b):
                    act.wait_ge(S["tx"], b + 1)
                    at_least(act, S["gu_ps"], 2 * NF * b)
                    act.activation(xnT[:, HI, :, :], PS[:, 4:6, :], ACT.Copy).then_inc(S["xnT_hi"], 1)

                def split_qk(b):
                    for m in range(4):
                        if m == 0:
                            at_least(act, S["on_sb"], NT * (b - 1))
                            at_least(act, S["ont"], b - 1)
                        act.wait_ge(S["qk_ps"], 4 * b + m + 1)
                        dst = khl if m % 2 else qhl
                        act.activation(dst[:, m // 2, HI, :], PS[:, m % 2, :], ACT.Copy).then_inc(S["qk_hi"], 1)

                def keep_v(b):
                    for n in range(2):
                        act.wait_ge(S["v_ps"], 2 * b + n + 1)
                        if n == 0:
                            at_least(act, S["pv"], NG * b)
                        act.activation(V[:, 2 * n:2 * n + 2, :, 0:HD].rearrange("p t h d -> p (t h) d"),
                                       PS[:, 6 + n, :].rearrange("p (x d) -> p x d", d=HD), ACT.Copy
                                       ).then_inc(S["v_sb"], 1)

                def silu_of_gate(b, i):
                    act.wait_ge(S["gu_ps"], 2 * NF * b + 2 * i + 1)
                    if i == 0:
                        at_least(act, S["pv"], NG * b - 1)
                    if i == FIRST_HALF:
                        at_least(act, S["pv"], NG * b)
                    if i >= 2:
                        act.wait_ge(S["h32_sb"], NF * b + i - 1)
                    act.activation(sil[:, i % 2, :], PS[:, BANK[i], :], ACT.Silu, scale=QSCALE
                                   ).then_inc(S["silu_sb"], 1)

                def hidden(b, i):
                    act.wait_ge(S["h32_sb"], NF * b + i + 1)
                    if i == 0:
                        at_least(act, S["down_ps"], 2 * b)
                    act.activation(h[:, i, HI, :], h32[:, i % 2, :], ACT.Copy).then_inc(S["h_hi"], 1)

                def gate_of_output(b, first, last):
                    for n in range(2):
                        if n == 1 and not first:
                            split_x1(b - 1)
                        act.wait_ge(S["down_ps"], 2 * b + n + 1)
                        if n == 0:
                            at_least(act, S["y_sb"], 2 * b)
                        act.activation(G[:, 2 * n:2 * n + 2, :].rearrange("p t e -> p (t e)"), PS[:, n, :],
                                       ACT.Silu, scale=QSCALE).then_inc(S["g_sb"], 1)
                    if not last:
                        split_x(b + 1)

                def split_x1(b):
                    act.wait_ge(S["t2"], b + 1)
                    act.wait_ge(S["op"], 2 * (b + 1))
                    act.activation(xn2T[:, HI, :, :], PS[:, 2:4, :], ACT.Copy).then_inc(S["xn2T_hi"], 1)

                def route_hidden(b):
                    act.wait_ge(S["hg_ps"], b + 1)
                    act.activation(hgT[:, :], PS[:, 6, :], ACT.Gelu, bias=bg1c[:, 0:1]).then_inc(S["hg_sb"], 1)

                def route_exps(b):
                    act.wait_ge(S["lg_in"], b + 1)
                    act.activation(lge[:, :, :], lg[:, :, :], ACT.Exp).then_inc(S["lge_sb"], 1)

                def exps(b, g, j):
                    if j == 0 and g >= 2:
                        act.wait_ge(S["pv"], NG * b + g - 1)
                    if g == 0 and j == 0:
                        at_least(act, S["pv"], NG * b)
                        act.wait_ge(S["down_ps"], 2 * (b + 1))
                    hd = GH * g + j
                    for n, width in enumerate(WIDTH):
                        act.wait_ge(S["st_ps"], 48 * b + 3 * hd + n + 1)
                        act.activation(PT[:, g % 2, j, 512 * n:512 * n + width], PS[:, 4 + n, 0:width], ACT.Exp,
                                       scale=SCALE).then_inc(S["exped"], 1)

                def keep_heads(b, g):
                    act.wait_ge(S["pv"], NG * b + g + 1)
                    if g == 0:
                        for half in S["spilt"]:
                            act.wait_ge(half, 32 * up_to(b + 2))
                    act.activation(OT[:, g, :], PS[:, 7, :], ACT.Copy).then_inc(S["ot_sb"], 1)

                def attention(b, first, last):
                    if not first:
                        route_exps(b - 1)
                    for s in range(1, NG + 2):
                        if s == NG + 1 and not last:
                            silu_of_gate(b + 1, 0)
                            silu_of_gate(b + 1, 1)
                        for j in range(GH):
                            if s <= NG:
                                exps(b, s - 1, j)
                            if j == 1 and s >= 2:
                                keep_heads(b, s - 2)

                def split_output(b):
                    act.wait_ge(S["ont"], b + 1)
                    at_least(act, S["xn2T_out"], 16 * b)
                    at_least(act, S["hg_ps"], b)
                    act.activation(OnT[:, HI, :, :], PS[:, 0:2, :], ACT.Copy).then_inc(S["ont_hi"], 1)

                def sequence(b, first=False, last=False):
                    for i in range(EARLY, NF):
                        silu_of_gate(b, i)
                        hidden(b, i)
                    gate_of_output(b, first, last)
                    if not first:
                        route_hidden(b - 1)
                    if not last:
                        split_qk(b + 1)
                    attention(b, first, last)
                    if not last:
                        hidden(b + 1, 0)
                        hidden(b + 1, 1)
                        keep_v(b + 1)
                    split_output(b)
                    if not last:
                        silu_of_gate(b + 1, 2)
                        hidden(b + 1, 2)

                split_x(0)
                split_qk(0)
                for i in range(EARLY):
                    silu_of_gate(0, i)
                    hidden(0, i)
                keep_v(0)
                sequence(0, first=True)
                with act.Fori(1, B - 1) as b:
                    sequence(b)
                sequence(B - 1, last=True)
                split_x1(B - 1)
                route_hidden(B - 1)
                route_exps(B - 1)

            @block.vector
            def _(dve):
                NORM_X = (xin, stats, mv, veps, rstd, xn, "ln_var", "ln_std", "ln_done")
                NORM_X1 = (xres, stats2, mv2, veps2, rstd2, xn2, "ln2_var", "ln2_std", "ln2_done")

                def norm_stats(b, norm):
                    src, st, _, _, _, _, var_sem, _, _ = norm
                    if norm is NORM_X:
                        dve.wait_ge(S["x_in"], 16 * (b + 1))
                    else:
                        dve.wait_ge(S["x1_sb"], b + 1)
                    for t in range(NT):
                        last = dve.bn_stats(st[:, t, :], src[:, t, :])
                    last.then_inc(S[var_sem], 1)

                def norm_variance(b, norm):
                    _, st, m_, ve, _, _, var_sem, _, _ = norm
                    dve.wait_ge(S[var_sem], 3 * b + 1)
                    dve.memset(idle_v[:, :], 0.0)
                    for t in range(NT):
                        last = dve.bn_aggr(m_[:, t, :], st[:, t, :])
                    last.then_inc(S[var_sem], 1)
                    dve.wait_ge(S[var_sem], 3 * b + 2)
                    dve.tensor_scalar(ve[:, :], m_[:, :, 1], EPS, None, ALU.add).then_inc(S[var_sem], 1)

                def norm_rows(b, norm):
                    src, _, m_, _, rs, dst, _, std_sem, done_sem = norm
                    if norm is NORM_X:
                        at_least(dve, S["tx"], b)
                        at_least(dve, S["t2"], b - 1)
                        at_least(dve, S["xn2_out"], 16 * (b - 1))
                    else:
                        dve.wait_ge(S["tx"], b + 2 if not isinstance(b, int) else min(b + 2, B))
                    dve.wait_ge(S[std_sem], b + 1)
                    for t in range(NT):
                        dve.tensor_scalar(dst[:, t, :], src[:, t, :], m_[:, t, 0:1], rs[:, t:t + 1],
                                          ALU.subtract, ALU.mult).then_inc(S[done_sem], 1)

                def norm(b, which):
                    norm_stats(b, which)
                    norm_variance(b, which)
                    norm_rows(b, which)

                def split_x(b):
                    dve.wait_ge(S["xnT_hi"], b + 1)
                    dve.tensor_tensor(xnT[:, LO, :, :], PS[:, 4:6, :], f(xnT[:, HI, :, :]), ALU.subtract
                                      ).then_inc(S["xnT_lo"], 1)

                def split_qk(b, tiles):
                    for m in tiles:
                        dve.wait_ge(S["qk_hi"], 4 * b + m + 1)
                        dst = khl if m % 2 else qhl
                        dve.tensor_tensor(dst[:, m // 2, LO, :], PS[:, m % 2, :], f(dst[:, m // 2, HI, :]),
                                          ALU.subtract).then_inc(S["qk_lo"], 1)

                def gated(b, i):
                    dve.wait_ge(S["gu_ps"], 2 * NF * b + 2 * i + 2)
                    dve.wait_ge(S["silu_sb"], NF * b + i + 1)
                    if i >= 2:
                        dve.wait_ge(S["h_hi"], NF * b + i - 1)
                        dve.wait_ge(S["h_lo"], (NF - 1) * b + i - 1)
                    dve.scalar_tensor_tensor(out=h32[:, i % 2, :], in0=PS[:, BANK[i] + 1, :], scalar=QSCALE,
                                             in1=sil[:, i % 2, :], op0=ALU.mult, op1=ALU.mult
                                             ).then_inc(S["h32_sb"], 1)

                def last_hidden_low(b):
                    dve.wait_ge(S["h_hi"], NF * (b + 1))
                    dve.tensor_tensor(h[:, NF - 1, LO, :], h32[:, (NF - 1) % 2, :], f(h[:, NF - 1, HI, :]), ALU.subtract
                                      ).then_inc(S["h_lo_last"], 1)

                ROUTE_STEPS = 9

                def route_step(b, n, ins, wait=True):
                    ins.then_inc(S["step"], 1)
                    if wait:
                        dve.wait_ge(S["step"], ROUTE_STEPS * b + n)

                def route_logits(b):
                    dve.wait_ge(S["lg_ps"], b + 1)
                    logits = PS[:, 7, 0:P].rearrange("p (t e) -> p t e", t=NT)[:, :, 0:NE]
                    route_step(b, 1, dve.tensor_tensor(
                        lg[:, :, :], logits, bg2b[:, :].unsqueeze(1).to_broadcast([P, NT, NE]), ALU.add))
                    route_step(b, 2, dve.tensor_reduce(out=small[:, 0, :], in_=lg[:, :, :], op=ALU.max, axis=AX.X))
                    dve.tensor_tensor(lg[:, :, :], lg[:, :, :],
                                      small[:, 0, :].unsqueeze(2).to_broadcast([P, NT, NE]),
                                      ALU.subtract).then_inc(S["lg_in"], 1)

                def route_choice(b):
                    dve.wait_ge(S["lge_sb"], b + 1)
                    route_step(b, 3, dve.tensor_reduce(out=small[:, 1, :], in_=lge[:, :, :], op=ALU.add, axis=AX.X))
                    route_step(b, 4, dve.reciprocal(small[:, 2, :], small[:, 1, :]))
                    route_step(b, 5, dve.tensor_tensor(lg[:, :, :], lge[:, :, :],
                                                       small[:, 2, :].unsqueeze(2).to_broadcast([P, NT, NE]), ALU.mult))
                    dve.memset(idle_v[:, :], 0.0)
                    for t in range(NT):
                        last = dve.max(out=top8[:, t, :], in_=lg[:, t, :])
                    route_step(b, 6, last)
                    dve.memset(idle_v[:, :], 0.0)
                    for t in range(NT):
                        last = dve.max_index(out=idx8[:, t, :], in_max=top8[:, t, :], in_values=lg[:, t, :])
                    route_step(b, 7, last)
                    route_step(b, 8, dve.tensor_copy(gates[:, bass.ds(NT * b, NT), :], top8[:, :, 0:TOPK]), wait=False)
                    route_step(b, 9, dve.tensor_copy(chosen[:, bass.ds(NT * b, NT), :], idx8[:, :, 0:TOPK]))

                def maxima(b, g, u):
                    slot = slot_of(g, u)
                    qt, heads, keys = UNITS[u]
                    dve.wait_ge(S["unit"], NU * (NG * b + g) + u + 1)
                    if u == 0 and not (isinstance(b, int) and b == 0 and g == 0):
                        dve.wait_ge(S["m_parts"], NG * b + g)
                    _, all_of = scores_of_unit(slot, u)
                    dve.tensor_reduce(out=Mneg[:, 0, qt, heads[0]:heads[-1] + 1], in_=all_of, op=ALU.max, axis=AX.X,
                                      negate=True).then_inc(S["maxed"], 1)

                def parts_of_maxima(b, g):
                    dve.wait_ge(S["maxed"], NU * (NG * b + g + 1))
                    at_least(dve, S["mt"], NG * b + g)
                    dve.tensor_copy(Mhi[:, :, :], Mneg[:, 0, :, :]).then_inc(S["mhi"], 1)
                    dve.wait_ge(S["mhi"], NG * b + g + 1)
                    dve.tensor_copy(Mparts[:, :, HI, :], f(Mhi[:, :, :]))
                    dve.tensor_tensor(Mparts[:, :, LO, :], Mneg[:, 0, :, :], f(Mhi[:, :, :]), ALU.subtract
                                      ).then_inc(S["m_parts"], 1)

                def rows_of_maxima(b, g):
                    slot = slot_of(g, NU)
                    dve.wait_ge(S["mt"], NG * b + g + 1)
                    at_least(dve, S["m_in"], 32 * (NG * b + g))
                    dve.tensor_copy(mrow[:, :], PS[0:2 * GH, slot, :]).then_inc(S["mrow_sb"], 1)

                def first_group(b, first, last):
                    maxima(b, 0, 0)
                    maxima(b, 0, 1)
                    qk_tiles = iter(range(4))
                    for u in range(2, NU + 1):
                        if not last and u != 4:
                            split_qk(b + 1, (next(qk_tiles),))
                        if u < NU:
                            maxima(b, 0, u)
                        if u == NU - 1:
                            parts_of_maxima(b, 0)
                    rows_of_maxima(b, 0)
                    if not first:
                        route_logits(b - 1)

                def attention(b, first):
                    for g in range(1, NG):
                        for u in range(NU):
                            maxima(b, g, u)
                        parts_of_maxima(b, g)
                        rows_of_maxima(b, g)
                    if not first:
                        route_choice(b - 1)

                def normed_heads(b):
                    for qt in range(NT):
                        dve.wait_ge(S["otr"], NT * b + qt + 1)
                        if qt == 0:
                            for half in S["spilt"]:
                                dve.wait_ge(half, 32 * up_to(b + 2))
                        heads = PS[:, qt, :].rearrange("p (h x) -> p h x", x=2 * HD)
                        dve.reciprocal(rinv[:, qt, :], heads[:, :, HD]).then_inc(S["rinv_sb"], 1)
                        dve.wait_ge(S["rinv_sb"], NT * b + qt + 1)
                        dve.tensor_tensor(On[:, qt, :].rearrange("p (h d) -> p h d", d=HD), heads[:, :, 0:HD],
                                          rinv[:, qt, :].unsqueeze(2).to_broadcast([P, NH, HD]), ALU.mult
                                          ).then_inc(S["on_sb"], 1)

                def split_output(b):
                    dve.wait_ge(S["ont_hi"], b + 1)
                    dve.tensor_tensor(OnT[:, LO, :, :], PS[:, 0:2, :], f(OnT[:, HI, :, :]), ALU.subtract
                                      ).then_inc(S["ont_lo"], 1)

                def residual(b):
                    for n in range(2):
                        dve.wait_ge(S["op"], 2 * b + n + 1)
                        dve.wait_ge(S["g_sb"], 2 * b + n + 1)
                        part = G[:, 2 * n:2 * n + 2, :].rearrange("p t e -> p (t e)")
                        dve.tensor_tensor(part, PS[:, 2 + n, :], part, ALU.mult).then_inc(S["y_sb"], 1)
                    dve.wait_ge(S["y_sb"], 2 * (b + 1))
                    dve.wait_ge(S["xres_in"], 16 * (b + 1))
                    dve.tensor_tensor(xres[:, :, :], xres[:, :, :], G[:, :, :], ALU.add).then_inc(S["x1_sb"], 1)

                def sequence(b, first=False, last=False):
                    gated(b, 3)
                    if not first:
                        norm_stats(b - 1, NORM_X1)
                    gated(b, 4)
                    if not first:
                        norm_variance(b - 1, NORM_X1)
                    gated(b, 5)
                    last_hidden_low(b)
                    if not first:
                        norm_rows(b - 1, NORM_X1)
                    if not last:
                        norm_stats(b + 1, NORM_X)
                        norm_variance(b + 1, NORM_X)
                        norm_rows(b + 1, NORM_X)
                    if not first:
                        split_x1(b - 1)
                    if not last:
                        split_x(b + 1)
                    first_group(b, first, last)
                    attention(b, first)
                    if not last:
                        gated(b + 1, 0)
                        gated(b + 1, 1)
                    normed_heads(b)
                    split_output(b)
                    if not last:
                        gated(b + 1, 2)
                    residual(b)

                def split_x1(b):
                    dve.wait_ge(S["xn2T_hi"], b + 1)
                    dve.tensor_tensor(xn2T[:, LO, :, :], PS[:, 2:4, :], f(xn2T[:, HI, :, :]), ALU.subtract
                                      ).then_inc(S["xn2T_lo"], 1)

                norm(0, NORM_X)
                split_x(0)
                split_qk(0, range(4))
                for i in range(EARLY):
                    gated(0, i)
                sequence(0, first=True)
                with dve.Fori(1, B - 1) as b:
                    sequence(b)
                sequence(B - 1, last=True)
                norm(B - 1, NORM_X1)
                split_x1(B - 1)
                route_logits(B - 1)
                route_choice(B - 1)

            @block.gpsimd
            def _(pool):
                def power(b, ve, rs, var_sem, std_sem):
                    pool.wait_ge(S[var_sem], 3 * b + 3)
                    pool.tensor_tensor(rs[:, :], ve[:, :], neghalf[:, :], ALU.pow).then_inc(S[std_sem], 1)

                def hidden_low(b, i):
                    pool.wait_ge(S["h_hi"], NF * b + i + 1)
                    pool.tensor_tensor(h[:, i, LO, :], h32[:, i % 2, :], f(h[:, i, HI, :]), ALU.subtract
                                       ).then_inc(S["h_lo"], 1)

                def masks(b):
                    for g in range(NG):
                        for j in range(GH):
                            pool.wait_ge(S["exped"], 48 * b + 3 * (GH * g + j + 1))
                            pool.tensor_tensor(idle_p[:, GH * g + j:GH * g + j + 1], neghalf[:, 0:1],
                                               neghalf[:, 0:1], ALU.mult)
                            p = PT[:, g % 2, j, :]
                            first = p[:, 0:1024].rearrange("p (a k) -> p a k", a=2)[:, :, 0:P]
                            second = p[:, 896:896 + 2 * P].rearrange("p (a k) -> p a k", a=2)
                            for blocks in (first, second):
                                last = pool.affine_select(out=blocks, in_=blocks, compare_op=ALU.is_ge, fill=0.0,
                                                          base=0, pattern=[[0, 2], [1, P]], channel_multiplier=-1)
                            last.then_inc(S["masked"], 1)

                def sequence(b, first=False, last=False):
                    hidden_low(b, 3)
                    hidden_low(b, 4)
                    if not first:
                        power(b - 1, veps2, rstd2, "ln2_var", "ln2_std")
                    if not last:
                        power(b + 1, veps, rstd, "ln_var", "ln_std")
                    masks(b)
                    if not last:
                        for i in range(EARLY):
                            hidden_low(b + 1, i)

                power(0, veps, rstd, "ln_var", "ln_std")
                for i in range(EARLY):
                    hidden_low(0, i)
                sequence(0, first=True)
                with pool.Fori(1, B - 1) as b:
                    sequence(b)
                sequence(B - 1, last=True)
                power(B - 1, veps2, rstd2, "ln2_var", "ln2_std")

        cursor[0] = first_free
        pos = keep("pos", [P, B, NT, TOPK], U32)
        block_expert = keep("block_expert", [P, NBLK], I32)
        idle_q = keep("idle_q", [P, 4])
        ramp_col = ident[:, 0:1]
        s2_at = cursor[0]
        s2 = keep("s2", [P, B * NT, C])
        after_shared = cursor[0]
        slotcnt = keep("slotcnt", [P, NBLK])
        Fwd = keep("Fwd", [P, 2, 2, FQ], F32R)
        Inv = keep("Inv", [P, 2, NQ, FQ], F32R)
        HA = keep("HA", [P, 2, 2, C])
        HB = keep("HB", [P, 2, 2, C])
        HN = keep("HN", [P, 2, 2, C])
        Win = keep("Win", [P, 2, CC, 2 * C], F32R)
        Wo2 = keep("Wo2", [P, 2, CC, C], F32R)
        bo2b = keep("bo2b", [P, C])
        binc = keep("binc", [P, 4])
        shortc = keep("shortc", [P, CC, 4])
        xT = keep("xT", [P, 2, CC, T], F32R)
        vt = keep("vt", [P, CC, T + 2])
        cv = keep("cv", [P, 2, CC, T])
        v2 = keep("v2", [P, 2, NT, C], F32R)
        Vf = keep("Vf", [P, 2, NQ, C])
        tmp = keep("tmp", [P, 4, 2 * C])
        tmq = keep("tmq", [P, 4, 2 * C])
        Z = keep("Z", [P, 2, NQ, C])
        Zs = keep("Zs", [P, 2, 2, NQ, C], F32R)
        o32 = keep("o32", [P, CC, T])
        oTs = keep("oTs", [P, 2, CC, T], F32R)
        xrows = keep("xrows", [P, NT, C])
        posb = keep("posb", [P, NT, TOPK], U32)
        not_used_by_loop = cursor[0]
        (st_f, st_i, st_win, st_wo), _ = share(("st_f", [P, 2, FQ], F32), ("st_i", [P, NQ, FQ], F32),
                                               ("st_win", [P, CC, 2 * C], F32), ("st_wo", [P, CC, C], F32))
        cursor[0] += size([P, 2, FQ], F32) + size([P, NQ, FQ], F32) + size([P, CC, 2 * C], F32) + size([P, CC, C], F32)
        fw1s = keep("fw1s", [1, 64]); posr = keep("posr", [1, T]); fb1c = keep("fb1c", [64, 1])
        fw2s = keep("fw2s", [64, P]); fb2c = keep("fb2c", [P, 1]); fw3s = keep("fw3s", [P, C])
        fb3b = keep("fb3b", [P, C]); h1s = keep("h1s", [64, T]); h2s = keep("h2s", [P, T])
        cursor[0] = not_used_by_loop
        bes = keep("bes", [P, NE * C])
        WE_RING = 3
        NW = 10
        EW = NE // NW * C
        st_we = keep("st_we", [P, WE_RING, CC, EW])
        assert cursor[0] <= nc.sbuf_usable_end
        b_in = sem("b_in"); e_hi = sem("e_hi"); e_lo = sem("e_lo")
        e_in = [sem(f"e_in{n}") for n in range(WE_RING)]

        def load_experts(sp, n):
            for c in range(CC):
                sp.dma_start(st_we[:, n % WE_RING, c, :], We[NE // NW * n:NE // NW * (n + 1), P * c:P * c + P, :
                                                             ].rearrange("e p n -> p e n")
                             ).then_inc(e_in[n % WE_RING], 16)

        off = s2_at

        def over_s2(name, shape, dt=F32):
            nonlocal off
            t = nc.alloc_sbuf_tensor_at(name, shape, dt, offset=off)
            off += size(shape, dt)
            return t

        ramp = over_s2("ramp", [P, P])
        before = over_s2("before", [P, P])
        ones = over_s2("ones", [P, P])
        chf = over_s2("chf", [P, B * NT, TOPK])
        per = over_s2("per", [P, 12, NE])
        peri = over_s2("peri", [P, 2, NE], I32)
        NTT = B * NT
        onehot = [over_s2(f"onehot{k}", [P, NTT, NE]) for k in range(TOPK)]
        cnt = over_s2("cnt", [P, NTT, NE])
        tots = [over_s2(f"tots{k}", [P, NTT, NE]) for k in range(3)]
        slot = over_s2("slot", [P, NTT, NE])
        slotf = over_s2("slotf", [P, NTT, TOPK])
        be_cmp = over_s2("be_cmp", [P, NBLK, NE])
        assert off <= after_shared

        U = {n: sem("u_" + n) for n in """xT_in xr_in posb_sb sent vx_ps vx_sb conv0 conv tr v2_hi v2_lo vf_ps vf_sb
            dstep pstep z_hi z_lo y_ps o_sb o_hi o_lo s_ps s_sb""".split()}
        r_in = sem("r_in"); r_pool = sem("r_pool"); r_dve = sem("r_dve"); r_ps = sem("r_ps")
        t_hi = sem("t_hi"); t_in = sem("t_in"); f_ps = sem("f_ps"); f_sb = sem("f_sb")
        f_hi = sem("f_hi"); f_lo = sem("f_lo"); h_sb = sem("h_sb"); f_cf = sem("f_cf")

        def transform(pe, src, bank, done):
            for half in range(2):
                for q_ in range(NQ):
                    n = 0
                    for kc in range(2):
                        for i, j in PAIRS:
                            last = pe.matmul(PS[:, bank + 2 * half + q_ // 2, C * (q_ % 2):C * (q_ % 2) + C],
                                             Fwd[:, i, kc, P * q_:P * q_ + P], src[:, j, 2 * half + kc, :],
                                             start=n == 0, stop=n == 5)
                            n += 1
                    if q_ % 2:
                        last.then_inc(done, 1)

        with nc.Block() as block:
            @block.sync
            def _(sp):
                sp.dma_start(ramp[:, :], ramp_c.partition_broadcast(P)).then_inc(r_in, 16)
                for dst, src in ((st_f[:, :, :], dft_c.rearrange("(c p) n -> p c n", p=P)),
                                 (st_i[:, :, :], idft_c.rearrange("(c p) n -> p c n", p=P)),
                                 (st_win[:, :, :], winT.rearrange("(c p) n -> p c n", p=P)),
                                 (st_wo[:, :, :], wo2.rearrange("(c p) n -> p c n", p=P)),
                                 (bo2b[:, :], bo2.partition_broadcast(P)), (binc[:, :], bin_),
                                 (shortc[:, :, :], short), (fw1s[:, :], fw1), (posr[:, :], pos_c),
                                 (fb1c[:, :], fb1), (fw2s[:, :], fw2), (fb2c[:, :], fb2), (fw3s[:, :], fw3),
                                 (fb3b[:, :], fb3.partition_broadcast(P))):
                    sp.dma_start(dst, src).then_inc(t_in, 16)
                sp.dma_start(f(xT[:, :, :, :]), xn2T_parts[0]).then_inc(U["xT_in"], 16)
                sp.dma_start(xrows[:, :, :], xn2_rows[0].rearrange("(t p) d -> p t d", p=P)).then_inc(U["xr_in"], 16)

            @block.gpsimd
            def _(pool):
                pool.memset(ones[:, :], 1.0).then_inc(r_pool, 1)
                pool.wait_ge(r_pool, 1)
                pool.affine_select(out=before[:, :], in_=ones[:, :], compare_op=ALU.is_gt, fill=0.0, base=0,
                                   pattern=[[1, P]], channel_multiplier=-1).then_inc(r_pool, 1)
                pool.memset(vt[:, :, 0:1], 0.0)
                pool.memset(vt[:, :, T + 1:T + 2], 0.0)
                for n, (w, src) in enumerate(((Inv, st_i), (Win, st_win), (Wo2, st_wo))):
                    pool.wait_ge(t_hi, n + 2)
                    pool.tensor_tensor(w[:, LO, :, :], src[:, :, :], f(w[:, HI, :, :]), ALU.subtract)

            @block.scalar
            def _(act):
                act.wait_ge(t_in, 16 * 14)
                act.activation(Fwd[:, HI, :, :], st_f[:, :, :], ACT.Copy).then_inc(t_hi, 1)
                act.wait_ge(f_ps, 1)
                act.activation(h1s[:, :], PS[0:64, 4, :], ACT.Gelu, bias=fb1c[:, 0:1]).then_inc(f_sb, 1)
                act.wait_ge(f_ps, 2)
                act.activation(h2s[:, :], PS[:, 5, :], ACT.Gelu, bias=fb2c[:, 0:1]).then_inc(f_sb, 1)
                for hi, src in ((Inv, st_i), (Win, st_win), (Wo2, st_wo)):
                    act.activation(hi[:, HI, :, :], src[:, :, :], ACT.Copy).then_inc(t_hi, 1)
                act.wait_ge(f_cf, 1)
                act.activation(v2[:, HI, :, :], Z[:, 0, :, :], ACT.Copy).then_inc(f_hi, 1)
                for half in range(2):
                    act.wait_ge(f_ps, 4 + 2 * half)
                    act.activation(HA[:, half, :, :].rearrange("p a c -> p (a c)"), PS[:, 4 + 2 * half, :], ACT.Copy
                                   ).then_inc(h_sb, 1)
                    act.activation(HN[:, half, :, :].rearrange("p a c -> p (a c)"), PS[:, 4 + 2 * half, :], ACT.Copy
                                   ).then_inc(h_sb, 1)
                    act.wait_ge(f_ps, 5 + 2 * half)
                    act.activation(HB[:, half, :, :].rearrange("p a c -> p (a c)"), PS[:, 5 + 2 * half, :], ACT.Copy
                                   ).then_inc(h_sb, 1)

            @block.tensor
            def _(pe):
                pe.wait_ge(r_pool, 2)
                pe.wait_ge(r_dve, 4)
                for n, lhs in enumerate((before, ones)):
                    for half in range(2):
                        last = pe.matmul(PS[:, 2 * n + half, 0:16 * NE], lhs[:, :],
                                         cnt[:, 16 * half:16 * half + 16, :].rearrange("p t e -> p (t e)"),
                                         start=True, stop=True)
                last.then_inc(r_ps, 1)
                pe.wait_ge(t_in, 16 * 14)
                pe.matmul(PS[0:64, 4, :], fw1s[:, :], posr[:, :], start=True, stop=True).then_inc(f_ps, 1)
                pe.wait_ge(f_sb, 1)
                pe.matmul(PS[:, 5, :], fw2s[:, :], h1s[:, :], start=True, stop=True).then_inc(f_ps, 1)
                pe.wait_ge(f_sb, 2)
                for t in range(NT):
                    last = pe.matmul(PS[:, 6 + t // 2, C * (t % 2):C * (t % 2) + C], h2s[:, P * t:P * t + P], fw3s[:, :],
                                     start=True, stop=True)
                last.then_inc(f_ps, 1)
                pe.wait_ge(f_lo, 1)
                transform(pe, v2, 4, f_ps)

            @block.vector
            def _(dve):
                made = [0]

                def step(ins):
                    made[0] += 1
                    ins.then_inc(r_dve, 1)
                    dve.wait_ge(r_dve, made[0])

                def bc_e(ap, n):
                    return ap.unsqueeze(1).to_broadcast([P, n, NE])

                dve.wait_ge(r_in, 16)
                step(dve.tensor_copy(chf[:, :, :], chosen[:, :, :]))
                for k in range(TOPK):
                    step(dve.tensor_tensor(onehot[k][:, :, :], bc_e(ramp[:, 0:NE], NTT),
                                           chf[:, :, k].unsqueeze(2).to_broadcast([P, NTT, NE]), ALU.is_equal))
                step(dve.tensor_tensor(cnt[:, :, :], onehot[0][:, :, :], onehot[1][:, :, :], ALU.add))
                dve.wait_ge(r_ps, 1)
                tiles = lambda n: PS[:, n:n + 2, 0:16 * NE].rearrange("p a (t e) -> p a t e", e=NE)
                halves = lambda t: t[:, :, :].rearrange("p (a t) e -> p a t e", a=2)
                step(dve.tensor_copy(halves(tots[0]), tiles(2)))
                step(dve.tensor_copy(tots[1][:, :, :], tots[0][:, :, :]))
                src, dst = 1, 2
                for d in (1, 2, 4, 8, 16):
                    dve.tensor_copy(tots[dst][:, 0:d, :], tots[src][:, 0:d, :])
                    step(dve.tensor_tensor(tots[dst][:, d:, :], tots[src][:, d:, :], tots[src][:, 0:NTT - d, :], ALU.add))
                    src, dst = dst, src
                run = tots[src]
                step(dve.tensor_scalar(peri[:, 0, :], run[:, NTT - 1, :], float(P - 1), None, ALU.add))
                step(dve.tensor_scalar(peri[:, 1, :], peri[:, 0, :], 7, None, ALU.arith_shift_right))
                step(dve.tensor_copy(per[:, 0, :], peri[:, 1, :]))
                step(dve.tensor_copy(per[:, 1, :], per[:, 0, :]))
                a, z = 1, 2
                for d in (1, 2, 4, 8, 16):
                    dve.tensor_copy(per[:, z, 0:d], per[:, a, 0:d])
                    step(dve.tensor_tensor(per[:, z, d:NE], per[:, a, d:NE], per[:, a, 0:NE - d], ALU.add))
                    a, z = z, a
                end = per[:, a, :]
                step(dve.tensor_tensor(per[:, 4, :], end, per[:, 0, :], ALU.subtract))
                step(dve.tensor_scalar(per[:, 5, :], per[:, 4, :], float(P), None, ALU.mult))
                step(dve.tensor_tensor(slot[:, :, :], run[:, :, :], tots[0][:, :, :], ALU.subtract))
                step(dve.tensor_tensor(slot[:, :, :], slot[:, :, :], bc_e(per[:, 5, :], NTT), ALU.add))
                step(dve.tensor_tensor(halves(slot), halves(slot), tiles(0), ALU.add))
                for k in range(TOPK):
                    step(dve.tensor_tensor(onehot[k][:, :, :], onehot[k][:, :, :], slot[:, :, :], ALU.mult))
                    step(dve.tensor_reduce(out=slotf[:, :, k], in_=onehot[k][:, :, :], op=ALU.add, axis=AX.X))
                step(dve.tensor_copy(pos[:, :, :, :].rearrange("p b t k -> p (b t) k"), slotf[:, :, :]))
                step(dve.tensor_tensor(be_cmp[:, :, :], bc_e(end, NBLK),
                                       ramp[:, 0:NBLK].unsqueeze(2).to_broadcast([P, NBLK, NE]), ALU.is_le))
                step(dve.tensor_reduce(out=slotcnt[:, :],
                                       in_=be_cmp[:, :, :], op=ALU.add, axis=AX.X))
                step(dve.tensor_scalar(block_expert[:, :], slotcnt[:, :], float(NE - 1), None, ALU.min))
                dve.wait_ge(f_ps, 3)
                for n in range(2):
                    last = dve.tensor_tensor(Z[:, 0, 2 * n:2 * n + 2, :], PS[:, 6 + n, :].rearrange("p (t c) -> p t c", t=2),
                                             fb3b[:, :].unsqueeze(1).to_broadcast([P, 2, C]), ALU.add)
                last.then_inc(f_cf, 1)
                dve.wait_ge(t_hi, 1)
                dve.tensor_tensor(Fwd[:, LO, :, :], st_f[:, :, :], f(Fwd[:, HI, :, :]), ALU.subtract)
                dve.wait_ge(f_hi, 1)
                dve.tensor_tensor(v2[:, LO, :, :], Z[:, 0, :, :], f(v2[:, HI, :, :]), ALU.subtract).then_inc(f_lo, 1)
                dve.wait_ge(h_sb, 6)
                step(dve.tensor_copy(HN[0:1, :, 0, :], HB[0:1, :, 0, :]))
                dve.memset(HB[0:1, :, 0, :], 0.0)

        ND, NPQ = 13, 7

        def x2_of(b, m):
            return s2[:, bass.ds(NT * b + 2 * m, 2), :].rearrange("p t c -> p (t c)")

        def turns(eng, before, turn):
            before()
            turn(0)
            with eng.Fori(1, B - 1) as b:
                turn(b)
            turn(B - 1, last=True)

        with nc.Block() as block:
            @block.sync
            def _(sp):
                def load_T(b):
                    at_least(sp, U["vx_ps"], 4 * b)
                    sp.dma_start(f(xT[:, :, :, :]), xn2T_parts[b]).then_inc(U["xT_in"], 16)

                def turn(b, last=False):
                    if not (isinstance(b, int) and b == 0):
                        sp.wait_ge(U["sent"], 128 * b)
                        sp.dma_start(xrows[:, :, :], xn2_rows[b].rearrange("(t p) d -> p t d", p=P)
                                     ).then_inc(U["xr_in"], 16)
                    if not last:
                        load_T(b + 1)
                    if isinstance(b, int) and b == 0:
                        sp.dma_start(bes[:, :], be.partition_broadcast(P)).then_inc(b_in, 16)
                        for n in range(WE_RING):
                            load_experts(sp, n)

                turns(sp, lambda: None, turn)

            @block.tensor
            def _(pe):
                def products(out, lhs, rhs, chunks, stop=True):
                    n, last = len(PAIRS) * chunks, None
                    for c in range(chunks):
                        for i, j in PAIRS:
                            n -= 1
                            last = pe.matmul(out, lhs(i, c), rhs(j, c), start=last is None, stop=stop and n == 0,
                                             skip_group_check=not stop)
                    return last

                def project(b):
                    pe.wait_ge(U["xT_in"], 16 * (b + 1))
                    at_least(pe, U["vf_sb"], 4 * b)
                    for m in range(4):
                        products(PS[:, m, :], lambda i, c: Win[:, i, c, P * m:P * m + P],
                                 lambda j, c: xT[:, j, c, :], CC).then_inc(U["vx_ps"], 1)

                def transposes(b):
                    pe.wait_ge(U["conv"], 4 * (b + 1))
                    if not (isinstance(b, int) and b == 0):
                        at_least(pe, U["s_sb"], 2 * (b - 1))
                    for t in range(NT):
                        for m in range(CC):
                            o = C * (t % 2) + P * m
                            last = pe.transpose(PS[:, 4 + t // 2, o:o + P], cv[:, 0, m, P * t:P * t + P], ident[:, :])
                    last.then_inc(U["tr"], 1)

                def forward(b):
                    pe.wait_ge(U["v2_lo"], b + 1)
                    pe.wait_ge(U["vx_sb"], 4 * (b + 1))
                    transform(pe, v2, 0, U["vf_ps"])

                def back_whole(b):
                    pe.wait_ge(U["z_lo"], 2 * b + 1)
                    at_least(pe, U["o_sb"], 2 * b)
                    for m in range(CC):
                        products(PS[:, 6 + m, :], lambda i, c: Zs[:, i, 0, c, P * m:P * m + P],
                                 lambda j, c: Inv[:, j, c, :], NQ, stop=False)

                def back_mixed(b):
                    pe.wait_ge(U["z_lo"], 2 * (b + 1))
                    for m in range(CC):
                        n = 0
                        for c in range(NQ):
                            for i, j in PAIRS:
                                n += 1
                                last = pe.matmul(PS[:, 6 + m, T // 2:T], Zs[:, i, 1, c, P * m:P * m + P],
                                                 Inv[:, j, c, 0:T // 2], start=False, stop=n == 3 * NQ,
                                                 skip_group_check=True)
                        last.then_inc(U["y_ps"], 1)

                def project_out(b, last):
                    pe.wait_ge(U["o_lo"], b + 1)
                    pe.wait_ge(U["v2_lo"], B if last else b + 2)
                    if last:
                        pe.wait_ge(U["s_sb"], 2 * b)
                    for t in range(NT):
                        ins = products(PS[:, 4 + t // 2, C * (t % 2):C * (t % 2) + C],
                                       lambda i, c: oTs[:, i, c, P * t:P * t + P], lambda j, c: Wo2[:, j, c, :], CC)
                        if t % 2:
                            ins.then_inc(U["s_ps"], 1)

                def before():
                    project(0)
                    transposes(0)
                    forward(0)

                def turn(b, last=False):
                    if not last:
                        project(b + 1)
                    back_whole(b)
                    if not last:
                        transposes(b + 1)
                    back_mixed(b)
                    if not last:
                        forward(b + 1)
                    project_out(b, last)

                turns(pe, before, turn)

            @block.scalar
            def _(act):
                def projected(b, tiles):
                    for m in tiles:
                        act.wait_ge(U["vx_ps"], 4 * b + m + 1)
                        if m < 2:
                            at_least(act, U["conv"], 4 * b)
                        dst = vt[:, m, 1:T + 1] if m < 2 else x2_of(b, m - 2)
                        act.activation(dst, PS[:, m, :], ACT.Identity, bias=binc[:, m:m + 1]).then_inc(U["vx_sb"], 1)

                def first_tap(b):
                    for m in range(CC):
                        act.wait_ge(U["vx_sb"], 4 * b + m + 1)
                        if m == 0:
                            at_least(act, U["tr"], b)
                        act.activation(cv[:, 0, m, :], vt[:, m, 0:T], ACT.Identity, scale=shortc[:, m, 0:1],
                                       bias=shortc[:, m, 3:4]).then_inc(U["conv0"], 1)

                def split_v(b):
                    act.wait_ge(U["tr"], b + 1)
                    at_least(act, U["vf_ps"], 4 * b)
                    act.activation(v2[:, HI, :, :].rearrange("p (a t) c -> p a (t c)", a=2), PS[:, 4:6, :], ACT.Copy
                                   ).then_inc(U["v2_hi"], 1)

                def transformed(b):
                    for n in range(4):
                        act.wait_ge(U["vf_ps"], 4 * b + n + 1)
                        if n == 0:
                            at_least(act, U["dstep"], ND * b)
                            at_least(act, U["pstep"], NPQ * b)
                        act.activation(Vf[:, n // 2, 2 * (n % 2):2 * (n % 2) + 2, :].rearrange("p q c -> p (q c)"),
                                       PS[:, n, :], ACT.Copy).then_inc(U["vf_sb"], 1)

                def split_z(b, z):
                    if z == 0:
                        act.wait_ge(U["dstep"], ND * b + 6)
                        at_least(act, U["y_ps"], 2 * b)
                    else:
                        act.wait_ge(U["dstep"], ND * b + ND)
                        act.wait_ge(U["pstep"], NPQ * (b + 1))
                    act.activation(Zs[:, HI, z, :, :], Z[:, z, :, :], ACT.Copy).then_inc(U["z_hi"], 1)

                def split_o(b):
                    act.wait_ge(U["o_sb"], 2 * (b + 1))
                    at_least(act, U["s_ps"], 2 * b)
                    act.activation(oTs[:, HI, :, :], o32[:, :, :], ACT.Copy).then_inc(U["o_hi"], 1)

                def before():
                    projected(0, (0, 1))
                    first_tap(0)
                    projected(0, (2, 3))
                    split_v(0)
                    transformed(0)

                def turn(b, last=False):
                    split_z(b, 0)
                    if not last:
                        projected(b + 1, (0, 1))
                        first_tap(b + 1)
                        projected(b + 1, (2,))
                    split_z(b, 1)
                    if not last:
                        projected(b + 1, (3,))
                        split_v(b + 1)
                    split_o(b)
                    if not last:
                        transformed(b + 1)

                turns(act, before, turn)

            @block.vector
            def _(dve):
                def short_filter(b):
                    for k in (1, 2):
                        for m in range(CC):
                            if k == 1:
                                dve.wait_ge(U["conv0"], 2 * b + m + 1)
                                at_least(dve, U["tr"], b)
                            else:
                                dve.wait_ge(U["conv"], 4 * b + m + 1)
                            if k == 2:
                                dve.wait_ge(U["vx_sb"], 4 * b + 2)
                            dve.scalar_tensor_tensor(out=cv[:, 2 - k, m, :], in0=vt[:, m, k:k + T],
                                                     scalar=shortc[:, m, k:k + 1],
                                                     in1=cv[:, k - 1, m, :], op0=ALU.mult, op1=ALU.add
                                                     ).then_inc(U["conv"], 1)

                def split_v(b):
                    dve.wait_ge(U["v2_hi"], b + 1)
                    dve.tensor_tensor(v2[:, LO, :, :].rearrange("p (a t) c -> p a (t c)", a=2), PS[:, 4:6, :],
                                      f(v2[:, HI, :, :]).rearrange("p (a t) c -> p a (t c)", a=2), ALU.subtract
                                      ).then_inc(U["v2_lo"], 1)

                def split_z(b, z):
                    dve.wait_ge(U["z_hi"], 2 * b + z + 1)
                    dve.tensor_tensor(Zs[:, LO, z, :, :], Z[:, z, :, :], f(Zs[:, HI, z, :, :]), ALU.subtract
                                      ).then_inc(U["z_lo"], 1)

                def with_filter(b):
                    made = 0

                    def step(ins):
                        nonlocal made
                        made += 1
                        ins.then_inc(U["dstep"], 1)

                    def done(n):
                        dve.wait_ge(U["dstep"], ND * b + n)

                    flat = lambda ap: ap.rearrange("p q c -> p (q c)")
                    re = lambda h_: flat(Vf[:, h_, 0:2, :])
                    im = lambda h_: flat(Vf[:, h_, 2:4, :])
                    tb = lambda t_, h_: flat(t_[:, h_, :, :])
                    mul = lambda n, a_, b_: step(dve.tensor_tensor(tmp[:, n, :], a_, b_, ALU.mult))
                    dve.wait_ge(U["vf_sb"], 4 * b + 2)
                    at_least(dve, U["z_lo"], 2 * b)
                    mul(0, re(0), tb(HA, 0))
                    mul(1, im(0), tb(HB, 0))
                    mul(2, re(0), tb(HB, 0))
                    mul(3, im(0), tb(HN, 0))
                    done(2)
                    step(dve.tensor_tensor(flat(Z[:, 0, 0:2, :]), tmp[:, 0, :], tmp[:, 1, :], ALU.subtract))
                    done(4)
                    step(dve.tensor_tensor(flat(Z[:, 0, 2:4, :]), tmp[:, 2, :], tmp[:, 3, :], ALU.add))
                    done(5)
                    mul(0, re(0), tb(HA, 1))
                    mul(1, im(0), tb(HB, 1))
                    dve.wait_ge(U["vf_sb"], 4 * b + 4)
                    done(6)
                    mul(2, re(1), tb(HA, 0))
                    mul(3, im(1), tb(HB, 0))
                    split_z(b, 0)
                    done(8)
                    step(dve.tensor_tensor(tmp[:, 0, :], tmp[:, 0, :], tmp[:, 1, :], ALU.subtract))
                    done(10)
                    step(dve.tensor_tensor(tmp[:, 2, :], tmp[:, 2, :], tmp[:, 3, :], ALU.subtract))
                    done(12)
                    step(dve.tensor_tensor(flat(Z[:, 1, 0:2, :]), tmp[:, 0, :], tmp[:, 2, :], ALU.add))
                    assert made == ND

                def slots_of(b):
                    at_least(dve, U["sent"], 128 * b)
                    dve.tensor_copy(posb[:, :, :], pos[:, bass.ds(b, 1), :, :].rearrange("p o t k -> p (o t) k")
                                    ).then_inc(U["posb_sb"], 1)

                def gated(b):
                    for m in range(CC):
                        dve.wait_ge(U["y_ps"], 2 * b + m + 1)
                        if m == 0:
                            at_least(dve, U["o_lo"], b)
                            dve.wait_ge(U["vx_sb"], 4 * (b + 1))
                        dve.tensor_tensor(o32[:, m, :], PS[:, 6 + m, :], x2_of(b, m), ALU.mult).then_inc(U["o_sb"], 1)

                def split_o(b):
                    dve.wait_ge(U["o_hi"], b + 1)
                    dve.tensor_tensor(oTs[:, LO, :, :], o32[:, :, :], f(oTs[:, HI, :, :]), ALU.subtract
                                      ).then_inc(U["o_lo"], 1)

                def branch_out(b):
                    for n in range(2):
                        dve.wait_ge(U["s_ps"], 2 * b + n + 1)
                        if n == 0:
                            dve.wait_ge(U["o_sb"], 2 * (b + 1))
                        dve.tensor_tensor(s2[:, bass.ds(NT * b + 2 * n, 2), :],
                                          PS[:, 4 + n, :].rearrange("p (t c) -> p t c", t=2),
                                          bo2b[:, :].unsqueeze(1).to_broadcast([P, 2, C]), ALU.add
                                          ).then_inc(U["s_sb"], 1)

                def before():
                    short_filter(0)
                    split_v(0)

                def turn(b, last=False):
                    with_filter(b)
                    slots_of(b)
                    if not (isinstance(b, int) and b == 0):
                        branch_out(b - 1)
                    if not last:
                        short_filter(b + 1)
                    split_z(b, 1)
                    if not last:
                        split_v(b + 1)
                    gated(b)
                    split_o(b)

                turns(dve, before, turn)
                branch_out(B - 1)

            @block.gpsimd
            def _(pool):
                flat = lambda ap: ap.rearrange("p q c -> p (q c)")

                def with_filter(b):
                    made = 0

                    def step(ins):
                        nonlocal made
                        made += 1
                        ins.then_inc(U["pstep"], 1)

                    pool.wait_ge(U["vf_sb"], 4 * b + 2)
                    at_least(pool, U["z_lo"], 2 * b)
                    mul = lambda n, a_, b_: step(pool.tensor_tensor(tmq[:, n, :], flat(a_), flat(b_), ALU.mult))
                    mul(0, Vf[:, 0, 0:2, :], HB[:, 1, :, :])
                    mul(1, Vf[:, 0, 2:4, :], HN[:, 1, :, :])
                    pool.wait_ge(U["vf_sb"], 4 * b + 4)
                    mul(2, Vf[:, 1, 0:2, :], HB[:, 0, :, :])
                    mul(3, Vf[:, 1, 2:4, :], HN[:, 0, :, :])
                    pool.wait_ge(U["pstep"], NPQ * b + 2)
                    step(pool.tensor_tensor(tmq[:, 0, :], tmq[:, 0, :], tmq[:, 1, :], ALU.add))
                    pool.wait_ge(U["pstep"], NPQ * b + 4)
                    step(pool.tensor_tensor(tmq[:, 2, :], tmq[:, 2, :], tmq[:, 3, :], ALU.add))
                    pool.wait_ge(U["pstep"], NPQ * b + 6)
                    step(pool.tensor_tensor(flat(Z[:, 1, 2:4, :]), tmq[:, 0, :], tmq[:, 2, :], ALU.add))

                def send(b):
                    pool.wait_ge(U["xr_in"], 16 * (b + 1))
                    pool.wait_ge(U["posb_sb"], b + 1)
                    pool.wait_ge(U["pstep"], NPQ * (b + 1))
                    pool.tensor_tensor(idle_q[:, 2:3], ramp_col[:, :], ramp_col[:, :], ALU.mult)
                    for t in range(NT):
                        for k in range(TOPK):
                            pool.indirect_dma_start(slots_in, bass.IndirectOffsetOnAxis(posb[:, t, k:k + 1], axis=0),
                                                    xrows[:, t, :], None).then_inc(U["sent"], 16)

                def turn(b, last=False):
                    with_filter(b)
                    send(b)

                turns(pool, lambda: None, turn)
                pool.wait_ge(U["sent"], 128 * B)

        cursor[0] = after_shared
        Wes = keep("Wes", [P, 2, CC, NE * C], F32R)
        RING, HALF = 6, 3
        xb = keep("xb", [P, RING, C])
        xbT = keep("xbT", [P, RING, 2, CC, P], F32R)
        yb = keep("yb", [P, RING, C])
        assert cursor[0] <= not_used_by_loop
        xb_in = [sem(f"xb_in{h_}") for h_ in range(2)]
        yb_out = [sem(f"yb_out{h_}") for h_ in range(2)]
        NI = NBLK // RING

        def half_rows(ap, n):
            return ap.rearrange("(j k p) d -> j p k d", p=P, k=HALF)[n]

        with nc.Block() as block:
            @block.sync
            def _(sp):
                for n in range(WE_RING, NW):
                    sp.wait_ge(e_lo, n - WE_RING + 1)
                    load_experts(sp, n)
                for h_ in range(2):
                    sp.dma_start(xb[:, HALF * h_:HALF * h_ + HALF, :], half_rows(slots_in, h_)).then_inc(xb_in[h_], 16)
                sp.wait_ge(b_in, 16)

            @block.scalar
            def _(act):
                for n in range(NW):
                    act.wait_ge(e_in[n % WE_RING], 16 * CC * (n // WE_RING + 1))
                    act.activation(Wes[:, HI, :, EW * n:EW * n + EW], st_we[:, n % WE_RING, :, :], ACT.Copy
                                   ).then_inc(e_hi, 1)

            @block.vector
            def _(dve):
                for n in range(NW):
                    dve.wait_ge(e_hi, n + 1)
                    o = slice(EW * n, EW * n + EW)
                    dve.tensor_tensor(Wes[:, LO, :, o], st_we[:, n % WE_RING, :, :], f(Wes[:, HI, :, o]), ALU.subtract
                                      ).then_inc(e_lo, 1)

        W = {n: sem("e_" + n + "_of") for n in "tr hi lo out kept".split()}

        def in_turns(eng, before, turn):
            before()
            turn(0)
            with eng.Fori(1, NI - 1) as i:
                turn(i)
            turn(NI - 1, last=True)

        with nc.Block() as block:
            @block.sync
            def _(sp):
                def turn(i, last=False):
                    for h_ in range(2):
                        its = slice(HALF * h_, HALF * h_ + HALF)
                        if not last:
                            sp.wait_ge(W["tr"], RING * i + HALF * (h_ + 1))
                            sp.dma_start(xb[:, its, :], half_rows(slots_in, 2 * (i + 1) + h_)).then_inc(xb_in[h_], 16)
                        sp.wait_ge(W["kept"], RING * i + HALF * (h_ + 1))
                        sp.dma_start(half_rows(slots_out, 2 * i + h_), yb[:, its, :]).then_inc(yb_out[h_], 16)

                in_turns(sp, lambda: None, turn)
                for h_ in range(2):
                    sp.wait_ge(yb_out[h_], 16 * NI)

            @block.tensor
            def _(pe):
                def transposes(i, u):
                    if u % HALF == 0:
                        pe.wait_ge(xb_in[u // HALF % 2], 16 * (i + u // RING + 1))
                    at_least(pe, W["lo"], RING * i + u - HALF + 1)
                    for c in range(CC):
                        last = pe.transpose(PS[:, u % HALF, P * c:P * c + P], xb[:, u % RING, P * c:P * c + P],
                                            ident[:, :])
                    last.then_inc(W["tr"], 1)

                def turn(i, last=False):
                    for u in range(RING):
                        expert = pe.value_load(block_expert[0:1, bass.ds(RING * i + u, 1)], min_val=0, max_val=NE - 1)
                        if not last or u + 2 < RING:
                            transposes(i, u + 2)
                        pe.wait_ge(W["lo"], RING * i + u + 1)
                        at_least(pe, W["kept"], RING * i + u - HALF + 1)
                        n = 0
                        for c in range(CC):
                            for a, z in PAIRS:
                                ins = pe.matmul(PS[:, HALF + u % HALF, 0:C], xbT[:, u, a, c, :],
                                                Wes[:, z, c, bass.ds(expert * C, C)], start=n == 0, stop=n == 5)
                                n += 1
                        ins.then_inc(W["out"], 1)

                def before():
                    transposes(0, 0)
                    transposes(0, 1)

                in_turns(pe, before, turn)

            @block.scalar
            def _(act):
                def turn(i, last=False):
                    for u in range(RING):
                        act.wait_ge(W["tr"], RING * i + u + 1)
                        at_least(act, W["out"], RING * (i - 1) + u + 1)
                        act.activation(xbT[:, u, HI, :, :].rearrange("p c k -> p (c k)"), PS[:, u % HALF, 0:C],
                                       ACT.Copy).then_inc(W["hi"], 1)

                in_turns(act, lambda: None, turn)

            @block.vector
            def _(dve):
                def split(i, u):
                    dve.wait_ge(W["hi"], RING * i + u + 1)
                    r = u % RING
                    dve.tensor_tensor(xbT[:, r, LO, :, :].rearrange("p c k -> p (c k)"), PS[:, u % HALF, 0:C],
                                      f(xbT[:, r, HI, :, :]).rearrange("p c k -> p (c k)"), ALU.subtract
                                      ).then_inc(W["lo"], 1)

                def turn(i, last=False):
                    for u in range(RING):
                        expert = dve.value_load(block_expert[0:1, bass.ds(RING * i + u, 1)], min_val=0, max_val=NE - 1)
                        if not last or u + 2 < RING:
                            split(i, u + 2)
                        dve.wait_ge(W["out"], RING * i + u + 1)
                        if u % HALF == 0:
                            at_least(dve, yb_out[u // HALF], 16 * i)
                        dve.tensor_tensor(yb[:, u, :], PS[:, HALF + u % HALF, 0:C], bes[:, bass.ds(expert * C, C)],
                                          ALU.add).then_inc(W["kept"], 1)

                def before():
                    split(0, 0)
                    split(0, 1)

                in_turns(dve, before, turn)

        cursor[0] = after_shared
        yg = keep("yg", [P, 2, TOPK, NT, C])
        acc = keep("acc", [P, 2, NT, C])
        acc2 = keep("acc2", [P, 2, NT, C])
        sg = keep("sg", [P, 2, NT, C])
        x1b = keep("x1b", [P, 2, NT, C])
        posc = keep("posc", [P, 2, NT, TOPK], U32)
        X = {n: sem("x_" + n) for n in "idle posc_sb acc_sb acc2_sb sg_sb prod out_sb".split()}
        for n in ("x1_in", "got", "stored"):
            X[n] = [sem(f"x_{n}{e}") for e in range(2)]

        def pairs(eng, pair):
            pair(0)
            with eng.Fori(1, B // 2) as i:
                pair(i)

        with nc.Block() as block:
            @block.sync
            def _(sp):
                def pair(i):
                    for e in range(2):
                        b = 2 * i + e
                        at_least(sp, X["out_sb"], b - 1)
                        sp.dma_start(x1b[:, e, :, :], x1_rows[b].rearrange("(t p) d -> p t d", p=P)
                                     ).then_inc(X["x1_in"][e], 16)

                pairs(sp, pair)

            @block.gpsimd
            def _(pool):
                def pair(i):
                    for e in range(2):
                        b = 2 * i + e
                        pool.wait_ge(X["posc_sb"], b + 1)
                        at_least(pool, X["acc2_sb"], b - 1)
                        at_least(pool, X["idle"], b)
                        pool.tensor_tensor(idle_q[:, 3:4], ramp_col[:, :], ramp_col[:, :], ALU.mult
                                           ).then_inc(X["idle"], 1)
                        for k in range(TOPK):
                            for t in range(NT):
                                pool.indirect_dma_start(yg[:, e, k, t, :], None, slots_out,
                                                        bass.IndirectOffsetOnAxis(posc[:, e, t, k:k + 1], axis=0)
                                                        ).then_inc(X["got"][e], 16)

                pairs(pool, pair)

            @block.vector
            def _(dve):
                def slots_of(b, e, gathered):
                    at_least(dve, X["got"][e], 128 * gathered)
                    dve.tensor_copy(posc[:, e, :, :], pos[:, bass.ds(b, 1), :, :].rearrange("p o t k -> p (o t) k")
                                    ).then_inc(X["posc_sb"], 1)

                def pair(i, last_pair=False):
                    for e in range(2):
                        b = 2 * i + e
                        dve.wait_ge(X["got"][e], 128 * (i + 1))
                        gate = lambda t, k: gates[:, bass.ds(NT * b + t, 1), k]
                        for t in range(NT):
                            last = dve.tensor_scalar(acc[:, e, t, :], yg[:, e, 0, t, :], gate(t, 0), None, ALU.mult)
                        last.then_inc(X["acc_sb"], 1)
                        dve.wait_ge(X["acc_sb"], b + 1)
                        at_least(dve, X["sg_sb"], b - 1)
                        for t in range(NT):
                            last = dve.scalar_tensor_tensor(out=acc2[:, e, t, :], in0=yg[:, e, 1, t, :],
                                                            scalar=gate(t, 1), in1=acc[:, e, t, :],
                                                            op0=ALU.mult, op1=ALU.add)
                        last.then_inc(X["acc2_sb"], 1)
                        if not last_pair:
                            slots_of(b + 2, e, i + 1)
                        dve.wait_ge(X["sg_sb"], b + 1)
                        dve.tensor_tensor(acc[:, e, :, :], sg[:, e, :, :], s2[:, bass.ds(NT * b, NT), :], ALU.mult
                                          ).then_inc(X["prod"], 1)
                        dve.wait_ge(X["prod"], b + 1)
                        dve.wait_ge(X["x1_in"][e], 16 * (i + 1))
                        dve.tensor_tensor(sg[:, e, :, :], acc[:, e, :, :], x1b[:, e, :, :], ALU.add
                                          ).then_inc(X["out_sb"], 1)

                slots_of(0, 0, 0)
                slots_of(1, 1, 0)
                pair(0)
                with dve.Fori(1, B // 2 - 1) as i:
                    pair(i)
                pair(B // 2 - 1, last_pair=True)

            @block.scalar
            def _(act):
                def pair(i):
                    for e in range(2):
                        b = 2 * i + e
                        act.wait_ge(X["acc2_sb"], b + 1)
                        at_least(act, X["stored"][e], 16 * i)
                        act.activation(sg[:, e, :, :], acc2[:, e, :, :], ACT.Silu).then_inc(X["sg_sb"], 1)
                        act.wait_ge(X["out_sb"], b + 1)
                        act.dma_start(out[b].rearrange("(t p) d -> p t d", p=P), sg[:, e, :, :]
                                      ).then_inc(X["stored"][e], 16)

                pairs(act, pair)
                for e in range(2):
                    act.wait_ge(X["stored"][e], 16 * B // 2)


def constants():
    half = T // 2
    t = np.arange(FQ, dtype=np.float64)
    k = np.arange(half, dtype=np.float64)
    angle = 2 * np.pi * np.outer(t, k) / FQ
    top = np.where(t % 2 == 0, 1.0, -1.0)
    fwd = np.concatenate([np.cos(angle), -np.sin(angle)], axis=1)
    fwd[:, half] = top
    weight = np.full(half, 2.0 / FQ)
    weight[0] = 1.0 / FQ
    inv = np.concatenate([(np.cos(angle) * weight).T, (-np.sin(angle) * weight).T], axis=0)
    inv[half] = top / FQ
    return {"ident_c": np.eye(P, dtype=np.float32), "ramp_c": np.arange(P, dtype=np.float32)[None],
            "pos_c": np.linspace(0.0, 1.0, T, dtype=np.float32)[None],
            "dft_c": np.ascontiguousarray(fwd[:half], dtype=np.float32), "idft_c": inv.astype(np.float32)}


def kernel(**inputs):
    import concourse.bacc as bacc
    from concourse.bass_utils import run_bass_kernel_spmd

    a = {name: np.asarray(v) for name, v in inputs.items()}

    def padded(w, shape):
        out = np.zeros(shape, w.dtype)
        out[tuple(slice(0, n) for n in w.shape)] = w
        return out

    columns = lambda v: v.reshape(-1, P).T
    w_in, b_in = a["L1_attn_in_proj_w"], a["L1_attn_in_proj_b"]
    short = np.concatenate([a["L1_attn_short_w"][:, 0, :], a["L1_attn_short_b"][:, None]], axis=1)
    arrays = {
        "x": a["L0_attn_x"], "wqkvT": a["L0_attn_w_qkv"].T, "woutT": a["L0_attn_w_out"].T,
        "wguT": np.concatenate([a["L0_ffn_w_gate"], a["L0_ffn_w_up"]]).T, "wdT": a["L0_ffn_w_down"].T,
        "wg1": padded(a["L1_ffn_wg1"], (C, P)), "bg1": padded(a["L1_ffn_bg1"][:, None], (P, 1)),
        "wg2": a["L1_ffn_wg2"][:, :NE], "bg2": a["L1_ffn_bg2"][None, :NE],
        "winT": np.concatenate([w_in[:, 0::3], w_in[:, 2::3]], axis=1),
        "bin_": columns(np.concatenate([b_in[0::3], b_in[2::3]])),
        "short": short.reshape(CC, P, 4).transpose(1, 0, 2),
        "wo2": a["L1_attn_out_w"], "bo2": a["L1_attn_out_b"][None],
        "fw1": a["L1_attn_fw1"], "fb1": a["L1_attn_fb1"][:, None], "fw2": a["L1_attn_fw2"],
        "fb2": a["L1_attn_fb2"][:, None], "fw3": a["L1_attn_fw3"][:, 1::2], "fb3": a["L1_attn_fb3"][None, 1::2],
        "We": a["L1_ffn_We"], "be": a["L1_ffn_be"].reshape(1, -1),
    }
    arrays.update(constants())
    arrays = {name: np.ascontiguousarray(v) for name, v in arrays.items()}
    nc = bacc.Bacc("TRN2", target_bir_lowering=False, num_devices=1)
    args = {name: nc.dram_tensor(name, v.shape, mybir.dt.from_np(v.dtype), kind="ExternalInput").ap()
            for name, v in arrays.items()}
    args["out"] = nc.dram_tensor("out", (B, T, C), F32, kind="ExternalOutput").ap()
    program(nc, **args)
    return run_bass_kernel_spmd(nc, [arrays], core_ids=[0]).results[0]["out"]
```
